# Optimizing a Trainium2 kernel written in Bass

```python
import numpy as np
import jax
import jax.numpy as jnp

def _softmax(x, axis=-1):
    return jax.nn.softmax(x, axis=axis)

def _gelu(x):
    return jax.nn.gelu(x, approximate=True)

def _silu(x):
    return jax.nn.silu(x)

def _sigmoid(x):
    return jax.nn.sigmoid(x)

def _layernorm(x, axis=-1, eps=1e-05):
    m = jnp.mean(x, axis=axis, keepdims=True)
    v = jnp.var(x, axis=axis, keepdims=True)
    return (x - m) / jnp.sqrt(v + eps)

def _scatter_add(tgt, idx, src, axis=0):
    return tgt.at[idx].add(src)

def _segment_sum(src, seg, n):
    return jax.ops.segment_sum(src, seg, n)
kernel_name = 'mk_gnn_resnorm_d4_gnn_r32_6bf23d'

def setup_inputs(seed: int=0):
    np.random.seed(seed)
    _w = jnp.asarray

    def _rec_inputs():
        import jax
        import jax.numpy as jnp
        _gk = jax.random.key(seed)
        x = -0.000202 + 1 * jax.random.normal(jax.random.fold_in(_gk, 1), (50000, 128), jnp.float32)
        src = jax.random.randint(jax.random.fold_in(_gk, 2), (50000,), 0, 50000, jnp.int32)
        dst = jax.random.randint(jax.random.fold_in(_gk, 3), (50000,), 0, 50000, jnp.int32)
        _o = jnp.argsort(dst, stable=True)
        src = src[_o]
        dst = dst[_o]
        edge_weight = jax.random.uniform(jax.random.fold_in(_gk, 13), (50000,), jnp.float32, 0.0, 0.999999)
        return (x, src, dst, edge_weight)
    x, src, dst, edge_weight = _rec_inputs()

    def _L0_gnn_setup():
        import jax, jax.numpy as jnp
        import numpy as np
        N, E, D = (50000, 25000, 128)
        H = 2 * D
        L = 3
        key = jax.random.key(seed)
        ks = jax.random.split(key, 12)
        g = lambda k, shape: jax.random.normal(k, shape, jnp.float32) * 0.05
        return {'x': jax.random.normal(ks[0], (N, D), jnp.float32), 'edge_index': jax.random.randint(ks[1], (2, E), 0, N), 'phi_w1': g(ks[2], (L, 2 * D, H)), 'phi_b1': g(ks[3], (L, H)), 'phi_w2': g(ks[4], (L, H, D)), 'phi_b2': g(ks[5], (L, D)), 'psi_w1': g(ks[6], (L, D, H)), 'psi_b1': g(ks[7], (L, H)), 'psi_w2': g(ks[8], (L, H, D)), 'psi_b2': g(ks[9], (L, D)), 'proj_w': g(ks[10], (D, D)), 'proj_b': g(ks[11], (D,))}
    _L0_gnn_all = _L0_gnn_setup()
    _L0_gnn_in = {k: v for k, v in _L0_gnn_all.items() if k in ('phi_w1', 'phi_b1', 'phi_w2', 'phi_b2', 'psi_w1', 'psi_b1', 'psi_w2', 'psi_b2', 'proj_w', 'proj_b')}
    del _L0_gnn_all

    def _L1_gnn_setup():
        import jax, jax.numpy as jnp
        import numpy as np
        N = 3125
        E = 50000
        IN = 128
        H = 4
        D = 32
        HD = H * D
        LN_EPS = 1e-05
        key = jax.random.key(seed)
        ks = jax.random.split(key, 16)
        w = lambda k, shp: jax.random.normal(k, shp, dtype=jnp.float32) * 0.05
        feat = jax.random.normal(ks[0], (N, IN), dtype=jnp.float32)
        src = jax.random.randint(ks[1], (E,), 0, N, dtype=jnp.int32)
        dst = jnp.concatenate([jnp.arange(N, dtype=jnp.int32), jax.random.randint(ks[2], (E - N,), 0, N, dtype=jnp.int32)])
        return {'feat': feat, 'src': src, 'dst': dst, 'Wq': w(ks[3], (IN, HD)), 'bq': jnp.zeros((HD,), jnp.float32), 'Wk': w(ks[4], (IN, HD)), 'bk': jnp.zeros((HD,), jnp.float32), 'Wv': w(ks[5], (IN, HD)), 'bv': jnp.zeros((HD,), jnp.float32), 'Wskip': w(ks[6], (IN, HD)), 'bskip': jnp.zeros((HD,), jnp.float32), 'Wgate': w(ks[7], (3 * HD, 1)), 'bgate': jnp.zeros((1,), jnp.float32), 'gamma': jnp.ones((HD,), jnp.float32), 'beta': jnp.zeros((HD,), jnp.float32), 'prelu_a': jnp.asarray(0.25, jnp.float32)}
    _L1_gnn_all = _L1_gnn_setup()
    _L1_gnn_in = {k: v for k, v in _L1_gnn_all.items() if k in ('Wq', 'bq', 'Wk', 'bk', 'Wv', 'bv', 'Wskip', 'bskip', 'Wgate', 'bgate', 'gamma', 'beta', 'prelu_a')}
    del _L1_gnn_all

    def _L2_gnn_setup():
        import jax, jax.numpy as jnp
        import numpy as np
        N_NODES = 3125
        N_EDGES = 50000
        EMB = 128
        HID = 64

        def _gcn_norm(edge_index, edge_weight, n_nodes):
            loop = jnp.arange(n_nodes, dtype=edge_index.dtype)
            src = jnp.concatenate([edge_index[0], loop])
            dst = jnp.concatenate([edge_index[1], loop])
            w = jnp.concatenate([edge_weight, jnp.ones((n_nodes,), dtype=edge_weight.dtype)])
            deg = jax.ops.segment_sum(w, dst, num_segments=n_nodes)
            dinv = jnp.where(deg > 0, jax.lax.rsqrt(deg), 0.0)
            norm = dinv[src] * w * dinv[dst]
            return (src, dst, norm)

        def _gcn_conv(h, W, b, src, dst, norm, n_nodes):
            h = h @ W
            msg = h[src] * norm[:, None]
            out = jax.ops.segment_sum(msg, dst, num_segments=n_nodes)
            return out + b
        key = jax.random.key(seed)
        ks = jax.random.split(key, 6)
        x = jax.random.normal(ks[0], (N_NODES, EMB), dtype=jnp.float32)
        edge_index = jax.random.randint(ks[1], (2, N_EDGES), 0, N_NODES, dtype=jnp.int64)
        edge_weight = jax.random.uniform(ks[2], (N_EDGES,), dtype=jnp.float32)
        W1 = jax.random.normal(ks[3], (EMB, HID), dtype=jnp.float32) / np.sqrt(EMB)
        b1 = jnp.zeros((HID,), dtype=jnp.float32)
        W2 = jax.random.normal(ks[4], (HID, HID), dtype=jnp.float32) / np.sqrt(HID)
        b2 = jnp.zeros((HID,), dtype=jnp.float32)
        return {'x': x, 'edge_index': edge_index, 'edge_weight': edge_weight, 'W1': W1, 'b1': b1, 'W2': W2, 'b2': b2}
    _L2_gnn_all = _L2_gnn_setup()
    _L2_gnn_in = {k: v for k, v in _L2_gnn_all.items() if k in ('W1', 'b1', 'W2', 'b2')}
    del _L2_gnn_all

    def _L3_gnn_setup():
        import jax, jax.numpy as jnp
        import numpy as np
        N_NODES = 3125
        N_EDGES = 50000
        N_FEAT = 128
        HIDDEN = 128

        def _gcn_layer(h, W, b, src, dst, dinv_src_dst, n_nodes):
            hw = h @ W
            msg = hw[src] * dinv_src_dst[:, None]
            agg = jax.ops.segment_sum(msg, dst, num_segments=n_nodes)
            return agg + b

        def _gcn_norm(edge_index, n_nodes):
            src, dst = (edge_index[0], edge_index[1])
            loop = jnp.arange(n_nodes, dtype=src.dtype)
            src = jnp.concatenate([src, loop])
            dst = jnp.concatenate([dst, loop])
            deg = jax.ops.segment_sum(jnp.ones_like(dst, dtype=jnp.float32), dst, num_segments=n_nodes)
            dinv = jnp.where(deg > 0, jax.lax.rsqrt(deg), 0.0)
            norm = dinv[src] * dinv[dst]
            return (src, dst, norm)
        key = jax.random.key(seed)
        k_x, k_e, k_w1, k_w2 = jax.random.split(key, 4)
        x = jax.random.normal(k_x, (N_NODES, N_FEAT), dtype=jnp.float32)
        edge_index = jax.random.randint(k_e, (2, N_EDGES), 0, N_NODES, dtype=jnp.int32)
        s1 = float(np.sqrt(6.0 / (N_FEAT + HIDDEN)))
        s2 = float(np.sqrt(6.0 / (HIDDEN + HIDDEN)))
        W1 = jax.random.uniform(k_w1, (N_FEAT, HIDDEN), jnp.float32, -s1, s1)
        W2 = jax.random.uniform(k_w2, (HIDDEN, HIDDEN), jnp.float32, -s2, s2)
        b1 = jnp.zeros((HIDDEN,), jnp.float32)
        b2 = jnp.zeros((HIDDEN,), jnp.float32)
        return {'x': x, 'edge_index': edge_index, 'W1': W1, 'b1': b1, 'W2': W2, 'b2': b2}
    _L3_gnn_all = _L3_gnn_setup()
    _L3_gnn_in = {k: v for k, v in _L3_gnn_all.items() if k in ('W1', 'b1', 'W2', 'b2')}
    del _L3_gnn_all
    return {'x': x, 'src': src, 'dst': dst, 'edge_weight': edge_weight, 'L0_gnn_phi_w1': _L0_gnn_in['phi_w1'], 'L0_gnn_phi_b1': _L0_gnn_in['phi_b1'], 'L0_gnn_phi_w2': _L0_gnn_in['phi_w2'], 'L0_gnn_phi_b2': _L0_gnn_in['phi_b2'], 'L0_gnn_psi_w1': _L0_gnn_in['psi_w1'], 'L0_gnn_psi_b1': _L0_gnn_in['psi_b1'], 'L0_gnn_psi_w2': _L0_gnn_in['psi_w2'], 'L0_gnn_psi_b2': _L0_gnn_in['psi_b2'], 'L0_gnn_proj_w': _L0_gnn_in['proj_w'], 'L0_gnn_proj_b': _L0_gnn_in['proj_b'], 'L1_gnn_Wq': _L1_gnn_in['Wq'], 'L1_gnn_bq': _L1_gnn_in['bq'], 'L1_gnn_Wk': _L1_gnn_in['Wk'], 'L1_gnn_bk': _L1_gnn_in['bk'], 'L1_gnn_Wv': _L1_gnn_in['Wv'], 'L1_gnn_bv': _L1_gnn_in['bv'], 'L1_gnn_Wskip': _L1_gnn_in['Wskip'], 'L1_gnn_bskip': _L1_gnn_in['bskip'], 'L1_gnn_Wgate': _L1_gnn_in['Wgate'], 'L1_gnn_bgate': _L1_gnn_in['bgate'], 'L1_gnn_gamma': _L1_gnn_in['gamma'], 'L1_gnn_beta': _L1_gnn_in['beta'], 'L1_gnn_prelu_a': _L1_gnn_in['prelu_a'], 'L2_gnn_W1': _L2_gnn_in['W1'], 'L2_gnn_b1': _L2_gnn_in['b1'], 'L2_gnn_W2': _L2_gnn_in['W2'], 'L2_gnn_b2': _L2_gnn_in['b2'], 'L3_gnn_W1': _L3_gnn_in['W1'], 'L3_gnn_b1': _L3_gnn_in['b1'], 'L3_gnn_W2': _L3_gnn_in['W2'], 'L3_gnn_b2': _L3_gnn_in['b2']}

def reference(x, src, dst, edge_weight, L0_gnn_phi_w1, L0_gnn_phi_b1, L0_gnn_phi_w2, L0_gnn_phi_b2, L0_gnn_psi_w1, L0_gnn_psi_b1, L0_gnn_psi_w2, L0_gnn_psi_b2, L0_gnn_proj_w, L0_gnn_proj_b, L1_gnn_Wq, L1_gnn_bq, L1_gnn_Wk, L1_gnn_bk, L1_gnn_Wv, L1_gnn_bv, L1_gnn_Wskip, L1_gnn_bskip, L1_gnn_Wgate, L1_gnn_bgate, L1_gnn_gamma, L1_gnn_beta, L1_gnn_prelu_a, L2_gnn_W1, L2_gnn_b1, L2_gnn_W2, L2_gnn_b2, L3_gnn_W1, L3_gnn_b1, L3_gnn_W2, L3_gnn_b2):
    import jax
    import jax.numpy as jnp

    def _L0_gnn_ref(x, edge_index, phi_w1, phi_b1, phi_w2, phi_b2, psi_w1, psi_b1, psi_w2, psi_b2, proj_w, proj_b):
        import jax, jax.numpy as jnp
        import numpy as np
        N, E, D = (50000, 25000, 128)
        H = 2 * D
        L = 3
        relu = jax.nn.relu

        def mlp(h, w1, b1, w2, b2):
            return relu(h @ w1 + b1) @ w2 + b2
        src, dst = (edge_index[0], edge_index[1])
        n = x.shape[0]
        deg = jax.ops.segment_sum(jnp.ones((edge_index.shape[1],), x.dtype), dst, num_segments=n)
        deg = jnp.maximum(deg, 1.0)[:, None]

        def conv(h, l):
            x_i = h[dst]
            x_j = h[src]
            m = mlp(jnp.concatenate([x_i, x_j - x_i], axis=1), phi_w1[l], phi_b1[l], phi_w2[l], phi_b2[l])
            agg = jax.ops.segment_sum(m, dst, num_segments=n) / deg
            return mlp(agg, psi_w1[l], psi_b1[l], psi_w2[l], psi_b2[l])
        pr = x @ proj_w + proj_b
        h = relu(conv(x, 0)) + pr
        h = relu(conv(h, 1)) + h
        return conv(h, 2)

    def _L1_gnn_ref(feat, src, dst, Wq, bq, Wk, bk, Wv, bv, Wskip, bskip, Wgate, bgate, gamma, beta, prelu_a):
        import jax, jax.numpy as jnp
        import numpy as np
        N = 3125
        E = 50000
        IN = 128
        H = 4
        D = 32
        HD = H * D
        LN_EPS = 1e-05
        n = feat.shape[0]
        q = (feat @ Wq + bq).reshape(n, H, D)
        k = (feat @ Wk + bk).reshape(n, H, D)
        v = (feat @ Wv + bv).reshape(n, H, D)
        a = jnp.einsum('ehd,ehd->eh', q[src], k[dst]) / jnp.sqrt(jnp.float32(D))
        m = jax.ops.segment_max(a, dst, num_segments=n)
        ex = jnp.exp(a - m[dst])
        den = jax.ops.segment_sum(ex, dst, num_segments=n)
        sa = ex / den[dst]
        agg = jax.ops.segment_sum(sa[:, :, None] * v[src], dst, num_segments=n)
        rst = agg.reshape(n, HD)
        skip = feat @ Wskip + bskip
        g = jax.nn.sigmoid(jnp.concatenate([skip, rst, skip - rst], axis=-1) @ Wgate + bgate)
        rst = g * skip + (1.0 - g) * rst
        mu = jnp.mean(rst, axis=-1, keepdims=True)
        var = jnp.mean(jnp.square(rst - mu), axis=-1, keepdims=True)
        rst = (rst - mu) * jax.lax.rsqrt(var + LN_EPS) * gamma + beta
        return jnp.where(rst > 0, rst, prelu_a * rst)

    def _L2_gnn_ref(x, edge_index, edge_weight, W1, b1, W2, b2):
        import jax, jax.numpy as jnp
        import numpy as np
        N_NODES = 3125
        N_EDGES = 50000
        EMB = 128
        HID = 64

        def _gcn_norm(edge_index, edge_weight, n_nodes):
            loop = jnp.arange(n_nodes, dtype=edge_index.dtype)
            src = jnp.concatenate([edge_index[0], loop])
            dst = jnp.concatenate([edge_index[1], loop])
            w = jnp.concatenate([edge_weight, jnp.ones((n_nodes,), dtype=edge_weight.dtype)])
            deg = jax.ops.segment_sum(w, dst, num_segments=n_nodes)
            dinv = jnp.where(deg > 0, jax.lax.rsqrt(deg), 0.0)
            norm = dinv[src] * w * dinv[dst]
            return (src, dst, norm)

        def _gcn_conv(h, W, b, src, dst, norm, n_nodes):
            h = h @ W
            msg = h[src] * norm[:, None]
            out = jax.ops.segment_sum(msg, dst, num_segments=n_nodes)
            return out + b
        n = x.shape[0]
        src, dst, norm = _gcn_norm(edge_index, edge_weight, n)
        x1 = jax.nn.relu(_gcn_conv(x, W1, b1, src, dst, norm, n))
        x2 = jax.nn.relu(_gcn_conv(x1, W2, b2, src, dst, norm, n))
        return jnp.concatenate([x1, x2], axis=1)

    def _L3_gnn_ref(x, edge_index, W1, b1, W2, b2):
        import jax, jax.numpy as jnp
        import numpy as np
        N_NODES = 3125
        N_EDGES = 50000
        N_FEAT = 128
        HIDDEN = 128

        def _gcn_layer(h, W, b, src, dst, dinv_src_dst, n_nodes):
            hw = h @ W
            msg = hw[src] * dinv_src_dst[:, None]
            agg = jax.ops.segment_sum(msg, dst, num_segments=n_nodes)
            return agg + b

        def _gcn_norm(edge_index, n_nodes):
            src, dst = (edge_index[0], edge_index[1])
            loop = jnp.arange(n_nodes, dtype=src.dtype)
            src = jnp.concatenate([src, loop])
            dst = jnp.concatenate([dst, loop])
            deg = jax.ops.segment_sum(jnp.ones_like(dst, dtype=jnp.float32), dst, num_segments=n_nodes)
            dinv = jnp.where(deg > 0, jax.lax.rsqrt(deg), 0.0)
            norm = dinv[src] * dinv[dst]
            return (src, dst, norm)
        n_nodes = x.shape[0]
        src, dst, norm = _gcn_norm(edge_index, n_nodes)
        h = jax.nn.relu(_gcn_layer(x, W1, b1, src, dst, norm, n_nodes))
        h = jax.nn.relu(_gcn_layer(h, W2, b2, src, dst, norm, n_nodes))
        return h
    edge_index = jnp.stack([src, dst])
    x = _layernorm(x + _L0_gnn_ref(x, edge_index, L0_gnn_phi_w1, L0_gnn_phi_b1, L0_gnn_phi_w2, L0_gnn_phi_b2, L0_gnn_psi_w1, L0_gnn_psi_b1, L0_gnn_psi_w2, L0_gnn_psi_b2, L0_gnn_proj_w, L0_gnn_proj_b), axis=-1)
    x = _layernorm(x + _L1_gnn_ref(x, src, dst, L1_gnn_Wq, L1_gnn_bq, L1_gnn_Wk, L1_gnn_bk, L1_gnn_Wv, L1_gnn_bv, L1_gnn_Wskip, L1_gnn_bskip, L1_gnn_Wgate, L1_gnn_bgate, L1_gnn_gamma, L1_gnn_beta, L1_gnn_prelu_a), axis=-1)
    x = _layernorm(x + _L2_gnn_ref(x, edge_index, edge_weight, L2_gnn_W1, L2_gnn_b1, L2_gnn_W2, L2_gnn_b2), axis=-1)
    x = _layernorm(x + _L3_gnn_ref(x, edge_index, L3_gnn_W1, L3_gnn_b1, L3_gnn_W2, L3_gnn_b2), axis=-1)
    return x

_drawn_inputs = setup_inputs


def setup_inputs(seed=0):
    import zlib

    import numpy as np

    out = dict(_drawn_inputs(seed))
    spreads = {'L1_gnn_bq': (0.0, 0.8),
     'L1_gnn_bk': (0.0, 0.8),
     'L1_gnn_bv': (0.0, 0.1),
     'L1_gnn_bskip': (0.0, 0.1),
     'L1_gnn_gamma': (1.0, 0.2),
     'L1_gnn_beta': (0.0, 0.1),
     'L2_gnn_b1': (0.0, 0.1),
     'L2_gnn_b2': (0.0, 0.1),
     'L3_gnn_b1': (0.0, 0.1),
     'L3_gnn_b2': (0.0, 0.1)}
    factors = {'L0_gnn_phi_b1': 8.0, 'L0_gnn_phi_b2': 4.769, 'L0_gnn_proj_b': 8.0}
    for name, (base, spread) in spreads.items():
        noise = np.random.default_rng([zlib.crc32(name.encode()), seed]).standard_normal(out[name].shape)
        drawn = base * np.exp(spread * noise) if base else spread * noise
        out[name] = jnp.asarray(drawn.astype(out[name].dtype))
    for name, factor in factors.items():
        out[name] = (out[name] * factor).astype(out[name].dtype)
    return out
```

```python
from contextlib import ExitStack

import concourse.bass as bass
from concourse import mybir

F32 = mybir.dt.float32
I32 = mybir.dt.int32
BF16 = mybir.dt.bfloat16
ALU = mybir.AluOpType
ACT = mybir.ActivationFunctionType
AX = mybir.AxisListType

N = 50000
P = 128
D = 128
GROUP = 512
TILES = GROUP // P
GROUPS = 98
ROWS = GROUPS * GROUP
COLS = ROWS // P
H0 = 256
HALVES = H0 // P
LAYERS = 3
HEADS, HEAD = 4, 32
HID2 = 64
NODE0 = ROWS
NOWHERE = 4 * ROWS
FAR = -1.0e30
EPS = 1e-5


class Named:
    pass


def wait_from(eng, sem, count):
    if not isinstance(count, int) or count > 0:
        eng.wait_ge(sem, count)


def wait_alone(eng, passed, sem, count):
    wait_from(eng, sem, count)
    if not isinstance(count, int):
        eng.sem_inc(passed, 1)


def landed(g, s, slots, each):
    return (g - s) * (each // slots) + each


def groups_of_slot(s, slots=4):
    return (GROUPS - s + slots - 1) // slots


def run_steps(eng, step, slots, peeled, tail):
    for i in range(peeled):
        step(i, i % slots)
    with eng.Fori(peeled // slots, GROUPS // slots) as k:
        for s in range(slots):
            step(slots * k + s, s)
    for i in range(GROUPS - GROUPS % slots, GROUPS + tail):
        step(i, i % slots)


def live(i, lag):
    if isinstance(i, int) and not 0 <= i - lag < GROUPS:
        return None
    return i - lag


def group_rows(table, first_row, g):
    return table[bass.ds(first_row + g * GROUP, GROUP), :].rearrange("(j p) f -> p j f", p=P)


def tiles(ap):
    return ap.rearrange("p (j f) -> p j f", j=TILES)


def over_features(ap, width):
    return ap.unsqueeze(2).to_broadcast([P, TILES, width])


def build(nc, a, out):
    with ExitStack() as ctx:
        def sb(name, shape, dt=F32):
            return ctx.enter_context(nc.sbuf_tensor(name, shape, dt))

        def dram(name, shape, dt=F32):
            return nc.dram_tensor(name, shape, dt, kind="Internal").ap()

        c = Named()
        c.ident = sb("ident", [P, P])
        c.eps = sb("eps", [P, 1])
        c.w_own = [sb(f"w_own{l}", [P, H0]) for l in range(LAYERS)]
        c.w_src = [sb(f"w_src{l}", [P, H0]) for l in range(LAYERS)]
        c.phi_w2 = [sb(f"phi_w2_{l}", [P, HALVES, D]) for l in range(LAYERS)]
        c.psi_w1 = [sb(f"psi_w1_{l}", [P, H0]) for l in range(LAYERS)]
        c.psi_w2 = [sb(f"psi_w2_{l}", [P, HALVES, D]) for l in range(LAYERS)]
        c.phi_b1 = sb("phi_b1", [P, LAYERS, HALVES])
        c.phi_b2 = sb("phi_b2", [P, LAYERS])
        c.psi_b1 = sb("psi_b1", [P, LAYERS, HALVES])
        c.psi_b1_mean = sb("psi_b1_mean", [P, LAYERS, HALVES])
        c.psi_b2 = sb("psi_b2", [P, LAYERS])
        c.hid_empty = sb("hid_empty", [P, LAYERS, HALVES])
        c.empty = sb("empty", [P, LAYERS])
        c.empty_relu = sb("empty_relu", [P, LAYERS])
        c.empty_row = sb("empty_row", [P, D])
        c.proj_w = sb("proj_w", [P, D])
        c.proj_b = sb("proj_b", [P, 1])
        c.h1_bias = sb("h1_bias", [P, 1])
        c.h2_bias = sb("h2_bias", [P, 1])
        c.wq, c.wk, c.wv, c.wskip = (sb(n, [P, D]) for n in ("wq", "wk", "wv", "wskip"))
        c.bq, c.bk, c.bv, c.bskip = (sb(n, [P, 1]) for n in ("bq", "bk", "bv", "bskip"))
        c.bskip_row = sb("bskip_row", [P, D])
        c.gate3 = sb("gate3", [P, 3])
        c.gate_skip = sb("gate_skip", [P, 1])
        c.gate_rst = sb("gate_rst", [P, 1])
        c.head_sum = sb("head_sum", [P, D])
        c.head_pick = sb("head_pick", [P, HEADS])
        c.gate_heads = sb("gate_heads", [P, HEADS])
        c.wskip_t = sb("wskip_t", [P, D])
        c.gate_own = sb("gate_own", [P, 1])
        c.gate_bias = sb("gate_bias", [P, 1])
        c.bgate = sb("bgate", [P, 1])
        c.gamma_row, c.beta_row = sb("gamma_row", [P, D]), sb("beta_row", [P, D])
        c.prelu = sb("prelu", [P, 1])
        c.minus_half = sb("minus_half", [P, TILES])
        c.ones = sb("ones", [P, P])
        c.gcn_w = [sb(f"gcn_w{n}", s) for n, s in enumerate(([P, HID2], [HID2, HID2], [P, D], [P, D]))]
        c.gcn_b = [sb(f"gcn_b{n}", [P, 1]) for n in range(4)]

        e = Named()
        e.place = sb("e_place", [P, COLS, 4])
        e.place_row = sb("e_place_row", [P, COLS], I32)
        e.fetched = sb("e_fetched", [P, COLS, 4])
        e.src, e.dst, e.src_at_end, e.src_at_start, e.out_row = (
            sb(f"e_{n}", [P, COLS], I32) for n in ("src", "dst", "src_at_end", "src_at_start", "out_row"))
        e.norm2, e.norm3, e.self2, e.self3, e.is_end, e.is_start = (
            sb(f"e_{n}", [P, COLS]) for n in ("norm2", "norm3", "self2", "self3", "is_end", "is_start"))

        r = Named()
        r.same_prev, r.same_next, r.cut_next = (dram(n, [ROWS], BF16) for n in ("same_prev", "same_next", "cut_next"))
        r.inv_count, r.dinv2, r.dinv3 = (dram(n, [ROWS]) for n in ("inv_count", "dinv2", "dinv3"))
        t = Named()
        t.h1, t.h2, t.x1, t.x2, t.x3, t.z1 = (dram(f"t_{n}", [2 * ROWS, D]) for n in ("h1", "h2", "x1", "x2", "x3", "z1"))
        t.y1 = dram("t_y1", [2 * ROWS, HID2])
        t.place = dram("t_place", [ROWS, 4])
        bank = [ctx.enter_context(nc.psum_tensor(f"bank{n}", [P, GROUP], F32)) for n in range(8)]

        constants(nc, a, c, bank)
        segments(nc, a, c, e, r, t, bank)
        node_space(nc, a, c, e, t, bank)
        edge_scalars(nc, a, c, e, r, bank)
        conv_pass(nc, a, c, e, r, bank, 0, a["x"], a["x"], e.src, False, t.h1, e.is_end)
        conv_pass(nc, a, c, e, r, bank, 1, t.h1, t.h1, e.src_at_end, True, t.h2, e.is_start)
        conv_pass(nc, a, c, e, r, bank, 2, t.h2, t.h2, e.src_at_start, False, t.x1, e.is_end)
        attention_pass(nc, a, c, e, r, bank, t.x1, t.x2)
        gcn_pass(nc, c, e, r, bank, 0, t.x2, e.src_at_start, False, t.y1, None, t.x3)
        gcn_pass(nc, c, e, r, bank, 1, t.y1, e.src_at_end, True, t.x3, t.x2, None)
        gcn_pass(nc, c, e, r, bank, 2, t.x3, e.src_at_start, False, t.z1, None, out)
        gcn_pass(nc, c, e, r, bank, 3, t.z1, e.src_at_end, True, out, t.x3, None)


def named_semaphores(nc, ctx, stage, names, slots="", four_slots=""):
    taken = []

    def take(name):
        taken.append(nc.alloc_semaphore(f"{stage}_{name}"))
        return taken[-1]

    def give_back():
        nc.clear_and_free_semaphores(taken)
        nc.all_engine_barrier()

    found = {n: take(n) for n in ["passed", *names.split()]}
    for count, some in ((2, slots), (4, four_slots)):
        for n in some.split():
            found[n] = [take(f"{n}{s}") for s in range(count)]
    ctx.callback(give_back)
    return found


def constants(nc, a, c, bank):
    with ExitStack() as ctx:
        S = named_semaphores(nc, ctx, "const", "loaded filled picked on_dve on_pe on_act")
        w_far = [ctx.enter_context(nc.sbuf_tensor(f"w_far{l}", [P, H0], F32)) for l in range(LAYERS)]
        hid_wide = ctx.enter_context(nc.sbuf_tensor("hid_wide", [P, HALVES, P], F32))
        psi_b2_row = ctx.enter_context(nc.sbuf_tensor("psi_b2_row", [P, D], F32))
        loads = []

        def column(ap, dst):
            loads.append((dst, ap.rearrange("(p o) -> p o", o=1)))

        def on_all(ap, dst, width):
            loads.append((dst, ap.rearrange("(o n) -> o n", o=1).to_broadcast([P, width])))

        for l in range(LAYERS):
            loads.append((w_far[l][:, :], a["L0_gnn_phi_w1"][l, 0:D, :]))
            loads.append((c.w_src[l][:, :], a["L0_gnn_phi_w1"][l, D:2 * D, :]))
            loads.append((c.phi_w2[l][:, :, :], a["L0_gnn_phi_w2"][l].rearrange("(k p) n -> p k n", p=P)))
            loads.append((c.psi_w1[l][:, :], a["L0_gnn_psi_w1"][l]))
            loads.append((c.psi_w2[l][:, :, :], a["L0_gnn_psi_w2"][l].rearrange("(k p) n -> p k n", p=P)))
            for h in range(HALVES):
                column(a["L0_gnn_phi_b1"][l, h * P:(h + 1) * P], c.phi_b1[:, l, h:h + 1])
                column(a["L0_gnn_psi_b1"][l, h * P:(h + 1) * P], c.psi_b1[:, l, h:h + 1])
            column(a["L0_gnn_phi_b2"][l], c.phi_b2[:, l:l + 1])
            column(a["L0_gnn_psi_b2"][l], c.psi_b2[:, l:l + 1])
        on_all(a["L0_gnn_psi_b2"][LAYERS - 1], psi_b2_row[:, :], D)
        loads.append((c.proj_w[:, :], a["L0_gnn_proj_w"]))
        column(a["L0_gnn_proj_b"], c.proj_b[:, :])
        for n, w, b in (("q", c.wq, c.bq), ("k", c.wk, c.bk), ("v", c.wv, c.bv), ("skip", c.wskip, c.bskip)):
            loads.append((w[:, :], a[f"L1_gnn_W{n}"]))
            column(a[f"L1_gnn_b{n}"], b[:, :])
        on_all(a["L1_gnn_bskip"], c.bskip_row[:, :], D)
        for n in range(3):
            loads.append((c.gate3[:, n:n + 1], a["L1_gnn_Wgate"][n * D:(n + 1) * D, :]))
        on_all(a["L1_gnn_bgate"], c.bgate[:, :], 1)
        on_all(a["L1_gnn_gamma"], c.gamma_row[:, :], D)
        on_all(a["L1_gnn_beta"], c.beta_row[:, :], D)
        on_all(a["L1_gnn_prelu_a"], c.prelu[:, :], 1)
        for n, (w, b) in enumerate((("L2_gnn_W1", "L2_gnn_b1"), ("L2_gnn_W2", "L2_gnn_b2"),
                                    ("L3_gnn_W1", "L3_gnn_b1"), ("L3_gnn_W2", "L3_gnn_b2"))):
            loads.append((c.gcn_w[n][:, :], a[w]))
            at = HID2 if n == 1 else 0
            width = HID2 if n < 2 else D
            column(a[b], c.gcn_b[n][at:at + width, :])

        with nc.Block() as block:
            @block.sync
            def _(sp):
                for dst, src in loads[::2]:
                    sp.dma_start(dst, src).then_inc(S["loaded"], 16)
                sp.wait_ge(S["loaded"], 16 * len(loads))

            @block.scalar
            def _(act):
                for dst, src in loads[1::2]:
                    act.dma_start(dst, src).then_inc(S["loaded"], 16)
                act.wait_ge(S["loaded"], 16 * len(loads))
                act.activation(c.hid_empty[:, :, :], c.psi_b1[:, :, :], ACT.Relu).then_inc(S["on_act"], 1)

            @block.gpsimd
            def _(pool):
                pool.memset(c.ident[:, :], 0.0)
                pool.memset(c.ones[:, :], 1.0)
                pool.memset(c.eps[:, :], EPS)
                pool.memset(c.minus_half[:, :], -0.5)
                pool.memset(c.head_sum[:, :], 0.0)
                pool.memset(c.head_pick[:, :], 0.0)
                pool.memset(c.gate_heads[:, :], 0.0).then_inc(S["filled"], 1)
                pool.wait_ge(S["filled"], 1)
                pool.affine_select(out=c.ident[:, :], in_=c.ident[:, :], compare_op=ALU.not_equal, fill=1.0,
                                   base=0, pattern=[[-1, P]], channel_multiplier=1)
                pool.memset(c.gate_bias[:, :], 0.0).then_inc(S["picked"], 1)

            @block.vector
            def _(dve):
                dve.wait_ge(S["loaded"], 16 * len(loads))
                dve.wait_ge(S["picked"], 1)
                for h in range(HEADS):
                    at = slice(h * HEAD, (h + 1) * HEAD)
                    dve.memset(c.head_sum[at, at], float(HEAD) ** -0.5)
                    dve.memset(c.head_pick[h * HEAD:h * HEAD + 1, h:h + 1], 1.0)
                for l in range(LAYERS):
                    dve.tensor_tensor(c.w_own[l][:, :], w_far[l][:, :], c.w_src[l][:, :], ALU.subtract)
                dve.tensor_tensor(c.gate_skip[:, :], c.gate3[:, 0:1], c.gate3[:, 2:3], ALU.add)
                dve.tensor_tensor(c.gate_rst[:, :], c.gate3[:, 1:2], c.gate3[:, 2:3], ALU.subtract).then_inc(S["on_dve"], 1)
                dve.wait_ge(S["on_dve"], 1)
                for h in range(HEADS):
                    at = slice(h * HEAD, (h + 1) * HEAD)
                    dve.tensor_copy(c.gate_heads[at, h:h + 1], c.gate_rst[at, :])
                dve.wait_ge(S["on_pe"], 1)
                dve.tensor_copy(c.wskip_t[:, :], bank[0][:, 0:D]).then_inc(S["on_dve"], 1)
                dve.wait_ge(S["on_act"], 1)
                for h in range(HALVES):
                    last = dve.tensor_scalar(hid_wide[:, h, :], c.ones[:, :], c.hid_empty[:, LAYERS - 1, h:h + 1],
                                             None, ALU.mult)
                last.then_inc(S["on_dve"], 1)
                dve.wait_ge(S["on_pe"], 2)
                for l in range(LAYERS):
                    dve.tensor_tensor(c.psi_b1_mean[:, l, :], bank[1][:, 2 * l:2 * l + 2], c.psi_b1[:, l, :], ALU.add)
                dve.tensor_tensor(c.empty[:, :], bank[2][:, 0:LAYERS], c.psi_b2[:, :], ALU.add).then_inc(S["on_dve"], 1)
                dve.tensor_tensor(c.empty_row[:, :], bank[4][:, 0:D], psi_b2_row[:, :], ALU.add)
                dve.tensor_copy(c.gate_own[:, :], bank[3][:, 0:1])
                dve.tensor_tensor(c.bgate[:, :], c.bgate[:, :], bank[5][:, 0:1], ALU.add).then_inc(S["on_dve"], 1)
                dve.wait_ge(S["on_dve"], 5)
                dve.tensor_scalar(c.gate_bias[:, :], c.bgate[:, :], 0.5, None, ALU.mult)
                dve.tensor_scalar(c.empty_relu[:, :], c.empty[:, :], 0.0, None, ALU.max).then_inc(S["on_dve"], 1)
                dve.wait_ge(S["on_dve"], 6)
                dve.tensor_tensor(c.h1_bias[:, :], c.proj_b[:, :], c.empty_relu[:, 0:1], ALU.add).then_inc(S["on_dve"], 1)
                dve.wait_ge(S["on_dve"], 7)
                dve.tensor_tensor(c.h2_bias[:, :], c.h1_bias[:, :], c.empty_relu[:, 1:2], ALU.add)

            @block.tensor
            def _(pe):
                pe.wait_ge(S["loaded"], 16 * len(loads))
                pe.wait_ge(S["picked"], 1)
                pe.transpose(bank[0][:, 0:D], c.wskip[:, :], c.ident[:, :]).then_inc(S["on_pe"], 1)
                pe.wait_ge(S["on_act"], 1)
                pe.wait_ge(S["on_dve"], 3)
                for l in range(LAYERS):
                    for h in range(HALVES):
                        pe.matmul(bank[1][:, 2 * l + h:2 * l + h + 1], c.psi_w1[l][:, h * P:(h + 1) * P],
                                  c.phi_b2[:, l:l + 1], start=True, stop=True)
                    for h in range(HALVES):
                        pe.matmul(bank[2][:, l:l + 1], c.psi_w2[l][:, h, :], c.hid_empty[:, l, h:h + 1],
                                  start=(h == 0), stop=(h == HALVES - 1))
                for h in range(HALVES):
                    pe.matmul(bank[4][:, 0:D], hid_wide[:, h, :], c.psi_w2[LAYERS - 1][:, h, :],
                              start=(h == 0), stop=(h == HALVES - 1))
                pe.matmul(bank[3][:, 0:1], c.wskip_t[:, :], c.gate_skip[:, :], start=True, stop=True)
                pe.matmul(bank[5][:, 0:1], c.bskip[:, :].to_broadcast([P, P]), c.gate_skip[:, :],
                          start=True, stop=True).then_inc(S["on_pe"], 1)


def segments(nc, a, c, e, r, t, bank):
    with ExitStack() as ctx:
        S = named_semaphores(nc, ctx, "seg", "loaded filled chain columns lines carried carry_columns safe root "
                             "computed stored")

        def sb(name, shape, dt=F32):
            return ctx.enter_context(nc.sbuf_tensor(f"seg_{name}", shape, dt))

        raw = [sb(f"raw{n}", [P, COLS], I32) for n in range(3)]
        dst = [sb(f"dst{n}", [P, COLS]) for n in range(3)]
        weight, pos, one = sb("weight", [P, COLS]), sb("pos", [P, COLS]), sb("one", [P, COLS])
        pos_int = sb("pos_int", [P, COLS], I32)
        same = [sb("same_prev", [P, COLS]), sb("same_next", [P, COLS])]
        first, last = sb("first", [P, COLS]), sb("last", [P, COLS])
        row16 = [sb(f"row16_{n}", [P, COLS], BF16) for n in range(3)]
        data = [[sb(f"data{d}{q}", [P, COLS]) for q in range(3)] for d in range(2)]
        part = [[sb(f"part{d}{q}", [P, COLS]) for q in range(3)] for d in range(2)]
        whole = [[sb(f"whole{d}{q}", [P, COLS]) for q in range(3)] for d in range(2)]
        through = [sb(f"through{d}", [P, COLS]) for d in range(2)]
        columns = [sb(f"columns{d}", [P, 2, 3]) for d in range(2)]
        lines = [sb(f"lines{d}", [3, 2, P]) for d in range(2)]
        carry = [sb(f"carry{d}", [3, P + 1]) for d in range(2)]
        carry_in = [sb(f"carry_in{d}", [P, 3]) for d in range(2)]
        deg, above, inv = sb("deg", [P, 2, COLS]), sb("above", [P, 2, COLS]), sb("inv", [P, 2, COLS])
        safe, root, raw_inv = sb("safe", [P, 2, COLS]), sb("root", [P, 2, COLS]), sb("raw_inv", [P, 2, COLS])
        inv_count, elsewhere = sb("inv_count", [P, COLS]), sb("elsewhere", [P, COLS])
        node = sb("node", [P, COLS, 4])

        def linear(row):
            return row.rearrange("(p c) -> p c", p=P)

        with nc.Block() as block:
            @block.sync
            def _(sp):
                for n in range(3):
                    sp.dma_start(raw[n][:, :], linear(a["dst_line"][n:n + ROWS])).then_inc(S["loaded"], 16)
                sp.dma_start(weight[:, :], linear(a["weight_line"])).then_inc(S["loaded"], 16)
                sp.dma_start(e.src[:, :], a["src_tiles"]).then_inc(S["loaded"], 16)
                sp.dma_start(e.dst[:, :], a["dst_tiles"]).then_inc(S["loaded"], 16)
                sp.wait_ge(S["computed"], 1)
                sp.dma_start(t.place.rearrange("(p c) k -> p c k", p=P), node[:, :, :]).then_inc(S["stored"], 16)
                for row, tile in ((r.same_prev, row16[0]), (r.same_next, row16[1]), (r.cut_next, row16[2]),
                                  (r.inv_count, inv_count)):
                    sp.dma_start(linear(row), tile[:, :]).then_inc(S["stored"], 16)
                for n, row in enumerate((r.dinv2, r.dinv3)):
                    sp.dma_start(linear(row), inv[:, n, :]).then_inc(S["stored"], 16)
                sp.wait_ge(S["stored"], 16 * 7)
                sp.wait_ge(S["loaded"], 16 * 6)

            @block.gpsimd
            def _(pool):
                pool.iota(pos_int[:, :], pattern=[[1, COLS]], base=0, channel_multiplier=COLS)
                pool.memset(one[:, :], 1.0)
                for d in range(2):
                    pool.memset(carry[d][:, :], 0.0)
                pool.memset(node[:, :, 2:4], 1.0).then_inc(S["filled"], 1)

            @block.tensor
            def _(pe):
                for d in range(2):
                    pe.wait_ge(S["columns"], d + 1)
                    for n in range(2):
                        last_ = pe.transpose(bank[d][0:3, n * P:(n + 1) * P], columns[d][:, n, :], c.ident[:, :])
                    last_.then_inc(S["lines"], 1)
                    pe.wait_ge(S["carried"], d + 1)
                    pe.transpose(bank[2 + d][:, 0:3], carry[d][:, d:d + P], c.ident[0:3, 0:3])\
                      .then_inc(S["carry_columns"], 1)

            @block.scalar
            def _(act):
                act.wait_ge(S["safe"], 1)
                act.activation(root[:, :, :], safe[:, :, :], ACT.Sqrt).then_inc(S["root"], 1)

            @block.vector
            def _(dve):
                links = [0]

                def link(ins):
                    links[0] += 1
                    ins.then_inc(S["chain"], 1)
                    dve.wait_ge(S["chain"], links[0])

                dve.wait_ge(S["loaded"], 16 * 6)
                dve.wait_ge(S["filled"], 1)
                for n in range(3):
                    dve.tensor_copy(dst[n][:, :], raw[n][:, :])
                link(dve.tensor_copy(pos[:, :], pos_int[:, :]))
                dve.tensor_tensor(same[0][:, :], dst[1][:, :], dst[0][:, :], ALU.is_equal)
                dve.tensor_tensor(same[1][:, :], dst[1][:, :], dst[2][:, :], ALU.is_equal)
                dve.tensor_tensor(first[:, :], dst[1][:, :], dst[0][:, :], ALU.not_equal)
                link(dve.tensor_tensor(last[:, :], dst[1][:, :], dst[2][:, :], ALU.not_equal))
                dve.tensor_copy(row16[0][:, :], same[0][:, :])
                dve.tensor_copy(row16[1][:, :], same[1][:, :])
                dve.tensor_scalar(row16[2][:, :], last[:, :], FAR, None, ALU.mult)
                dve.tensor_scalar(elsewhere[:, :], last[:, :], -float(NOWHERE), float(NOWHERE), ALU.mult, ALU.add)
                link(dve.tensor_tensor(data[0][2][:, :], first[:, :], pos[:, :], ALU.mult))
                dve.tensor_tensor(e.place_row[:, :], elsewhere[:, :], dst[1][:, :], ALU.add)
                for d in range(2):
                    flow = slice(None, None, 1 - 2 * d)
                    edge = (COLS - 1) * (1 - d)
                    add = data[1] if d else [weight, one, data[0][2]]
                    if d:
                        for q, x in enumerate((whole[0][0], whole[0][1], pos)):
                            last_ = dve.tensor_tensor(data[1][q][:, :], last[:, :], x[:, :], ALU.mult)
                        link(last_)
                    for q in range(3):
                        dve.tensor_tensor_scan(part[d][q][:, flow], same[d][:, flow], add[q][:, flow], 0.0,
                                               ALU.mult, ALU.add)
                    link(dve.tensor_tensor_scan(through[d][:, flow], same[d][:, flow], one[:, flow], 1.0,
                                                ALU.mult, ALU.min))
                    for q in range(3):
                        dve.tensor_copy(columns[d][:, 0, q:q + 1], part[d][q][:, edge:edge + 1])
                        last_ = dve.tensor_copy(columns[d][:, 1, q:q + 1], through[d][:, edge:edge + 1])
                    last_.then_inc(S["columns"], 1)
                    dve.wait_ge(S["lines"], d + 1)
                    link(dve.tensor_copy(lines[d][:, :, :], bank[d][0:3, 0:2 * P].rearrange("q (n p) -> q n p", n=2)))
                    into = carry[d][:, 1 - d:1 - d + P][:, flow]
                    dve.tensor_tensor_scan(into, lines[d][:, 1, flow], lines[d][:, 0, flow], 0.0,
                                           ALU.mult, ALU.add).then_inc(S["carried"], 1)
                    dve.wait_ge(S["carry_columns"], d + 1)
                    link(dve.tensor_copy(carry_in[d][:, :], bank[2 + d][:, 0:3]))
                    for q in range(3):
                        last_ = dve.scalar_tensor_tensor(whole[d][q][:, :], through[d][:, :], carry_in[d][:, q:q + 1],
                                                         part[d][q][:, :], ALU.mult, ALU.add)
                    link(last_)
                total_weight, count, end = whole[1]
                start = whole[0][2]
                dve.tensor_scalar(deg[:, 0, :], total_weight[:, :], 1.0, None, ALU.add)
                link(dve.tensor_scalar(deg[:, 1, :], count[:, :], 1.0, None, ALU.add))
                dve.tensor_scalar(safe[:, :, :], deg[:, :, :], 1e-30, None, ALU.max).then_inc(S["safe"], 1)
                dve.tensor_scalar(above[:, :, :], deg[:, :, :], 0.0, None, ALU.is_gt)
                dve.wait_ge(S["root"], 1)
                link(dve.reciprocal(raw_inv[:, :, :], root[:, :, :]))
                link(dve.tensor_tensor(inv[:, :, :], raw_inv[:, :, :], above[:, :, :], ALU.mult))
                dve.reciprocal(inv_count[:, :], count[:, :])
                dve.tensor_copy(e.place[:, :, 0], end[:, :])
                dve.tensor_copy(e.place[:, :, 1], start[:, :])
                for n in range(2):
                    dve.tensor_copy(e.place[:, :, 2 + n], inv[:, n, :])
                for n in range(2):
                    last_ = dve.tensor_scalar(node[:, :, n], pos[:, :], float(NODE0), None, ALU.add)
                last_.then_inc(S["computed"], 1)


class LayerNorm:

    def __init__(self, sb, name):
        self.stats, self.moments = sb(f"{name}_stats", [P, TILES, 6]), sb(f"{name}_moments", [P, TILES, 2])
        self.scale, self.shift = sb(f"{name}_scale", [P, TILES]), sb(f"{name}_shift", [P, TILES])


def layernorm_buffers(sb, name):
    return [LayerNorm(sb, f"{name}{s}") for s in range(2)]


def layernorm_stats(dve, S, stats_done, moments_done, g, rows, ln, spread):
    for j in range(TILES):
        last = dve.bn_stats(ln.stats[:, j, :], rows[:, j * D:(j + 1) * D])
    last.then_inc(stats_done, 1)
    wait_alone(dve, S["passed"], stats_done, g + 1)
    for j in range(TILES):
        last = dve.bn_aggr(ln.moments[:, j, :], ln.stats[:, j, :])
    last.then_inc(moments_done, 1)
    dve.wait_ge(moments_done, g + 1)
    return dve.tensor_scalar(spread, ln.moments[:, :, 1], EPS, None, ALU.add)


def layernorm_factors(dve, scale_done, shift_done, g, root, mask, ln):
    if mask is None:
        dve.tensor_copy(ln.scale[:, :], root).then_inc(scale_done, 1)
    else:
        dve.tensor_tensor(ln.scale[:, :], root, mask, ALU.mult).then_inc(scale_done, 1)
    dve.wait_ge(scale_done, g + 1)
    dve.scalar_tensor_tensor(ln.shift[:, :], ln.moments[:, :, 0], -1.0, ln.scale[:, :], ALU.mult, ALU.mult)\
       .then_inc(shift_done, 1)


def layernorm_apply(act, out, rows, ln):
    for j in range(TILES):
        at = slice(j * D, (j + 1) * D)
        last = act.activation(out[:, at], rows[:, at], ACT.Identity, bias=ln.shift[:, j:j + 1], scale=ln.scale[:, j:j + 1])
    return last


def transpose_tiles(pe, out, rows, c):
    for j in range(TILES):
        at = slice(j * P, (j + 1) * P)
        last = pe.transpose(out[:, at], rows[:, at], c.ident[:, :])
    return last


def node_space(nc, a, c, e, t, bank):
    BATCH = 2 * TILES
    HALF = GROUPS // 2
    with ExitStack() as ctx:
        S = named_semaphores(nc, ctx, "node", "x_turned xT projected hT h_turned h_rows x1_turned x1T skipped tanh "
                             "centred stats0 moments0 scale0 shift0 x1_rows stats1 moments1 scale1 shift1 normed "
                             "skip_bias gate mixed scaled_gamma affine negative prelu_done residual "
                             "stats2 moments2 scale2 shift2 x2_rows spread root filled staged unstaged",
                             "h1_out h2_out x1_out x2_out scattered gathered", "x_in")

        def sb(name, shape, dt=F32):
            return ctx.enter_context(nc.sbuf_tensor(f"node_{name}", shape, dt))

        x_rows = [sb(f"x_rows{s}", [P, GROUP]) for s in range(4)]
        x1_rows = [sb(f"x1_rows{s}", [P, GROUP]) for s in range(4)]
        (xT, h1T, h2T, h1_rows, h2_rows, xc, x1T, skip, mixed, normed, gam, aff, neg, pre, res, x2_rows) = (
            [sb(f"{n}{s}", [P, GROUP]) for s in range(2)] for n in
            "xT h1T h2T h1_rows h2_rows xc x1T skip mixed normed gam aff neg pre res x2_rows".split())
        th, gate = ([sb(f"{n}{s}", [P, TILES]) for s in range(2)] for n in ("th", "gate"))
        ln = [layernorm_buffers(sb, f"ln{n}") for n in range(3)]
        spread, root = ([sb(f"{n}{s}", [P, 3, TILES]) for s in range(2)] for n in ("spread", "root"))
        power = sb("power", [P, 3, TILES])
        stage_row = [sb(f"stage_row{s}", [P, BATCH], I32) for s in range(2)]
        stage = [sb(f"stage{s}", [P, BATCH, 4]) for s in range(2)]
        fetch_row = [sb(f"fetch_row{s}", [P, BATCH], I32) for s in range(2)]
        fetch = [sb(f"fetch{s}", [P, BATCH, 4]) for s in range(2)]

        with nc.Block() as block:
            @block.sync
            def _(sp):
                def step(i, u):
                    g = live(i, 0)
                    if g is not None:
                        s = u
                        wait_alone(sp, S["passed"], S["x_turned"], g - 3)
                        wait_alone(sp, S["passed"], S["centred"], g - 3)
                        sp.dma_start(tiles(x_rows[s][:, :]), group_rows(a["x"], 0, g)).then_inc(S["x_in"][s], 16)
                    g = live(i, 1)
                    if g is not None:
                        s = (u - 1) % 2
                        wait_alone(sp, S["passed"], S["h_rows"], g + 1)
                        sp.dma_start(group_rows(t.h1, NODE0, g), tiles(h1_rows[s][:, :])).then_inc(S["h1_out"][s], 16)
                        sp.dma_start(group_rows(t.h2, NODE0, g), tiles(h2_rows[s][:, :])).then_inc(S["h2_out"][s], 16)
                        wait_alone(sp, S["passed"], S["x1_rows"], g + 1)
                        sp.dma_start(group_rows(t.x1, NODE0, g), tiles(x1_rows[(u - 1) % 4][:, :]))\
                          .then_inc(S["x1_out"][s], 16)
                    g = live(i, 5)
                    if g is not None:
                        s = (u - 5) % 2
                        wait_alone(sp, S["passed"], S["x2_rows"], g + 1)
                        sp.dma_start(group_rows(t.x2, NODE0, g), tiles(x2_rows[s][:, :])).then_inc(S["x2_out"][s], 16)

                run_steps(sp, step, 4, 8, 5)
                for s in range(2):
                    for out_ in (S["h1_out"], S["h2_out"], S["x1_out"], S["x2_out"]):
                        sp.wait_ge(out_[s], 16 * HALF)

            @block.gpsimd
            def _(pool):
                for s in range(2):
                    pool.memset(spread[s][:, :, :], 1.0)
                pool.memset(power[:, :, :], -0.5).then_inc(S["filled"], 1)
                pool.wait_ge(S["filled"], 1)

                def norms(i, s):
                    wait_alone(pool, S["passed"], S["spread"], i + 1)
                    pool.tensor_tensor(root[s][:, :, :], spread[s][:, :, :], power[:, :, :], ALU.pow).then_inc(S["root"], 1)

                def scatter(i, s):
                    at = bass.ds(i * BATCH, BATCH)
                    if not isinstance(i, int) or i >= 2:
                        wait_alone(pool, S["passed"], S["scattered"][s], (i - s) * (8 * BATCH))
                    pool.tensor_copy(stage_row[s][:, :], e.place_row[:, at])
                    pool.tensor_copy(stage[s][:, :, :], e.place[:, at, :]).then_inc(S["staged"], 1)
                    wait_alone(pool, S["passed"], S["staged"], i + 1)
                    for j in range(BATCH):
                        pool.indirect_dma_start(t.place[:, :], bass.IndirectOffsetOnAxis(ap=stage_row[s][:, j:j + 1], axis=0),
                                                stage[s][:, j, :], None, bounds_check=ROWS - 1, oob_is_err=False)\
                            .then_inc(S["scattered"][s], 16)
                    norms(i, s)

                def fetched(m, s):
                    wait_alone(pool, S["passed"], S["gathered"][s], (m - s) * (8 * BATCH) + 16 * BATCH)
                    pool.tensor_copy(e.fetched[:, bass.ds(m * BATCH, BATCH), :], fetch[s][:, :, :]).then_inc(S["unstaged"], 1)
                    wait_alone(pool, S["passed"], S["unstaged"], m + 1)

                def gather(m, s, norm_slot):
                    if not isinstance(m, int) or m >= 2:
                        fetched(m - 2, s)
                    pool.tensor_copy(fetch_row[s][:, :], e.src[:, bass.ds(m * BATCH, BATCH)]).then_inc(S["staged"], 1)
                    wait_alone(pool, S["passed"], S["staged"], HALF + m + 1)
                    for j in range(BATCH):
                        pool.indirect_dma_start(fetch[s][:, j, :], None, t.place[:, :],
                                                bass.IndirectOffsetOnAxis(ap=fetch_row[s][:, j:j + 1], axis=0))\
                            .then_inc(S["gathered"][s], 16)
                    norms(HALF + m, norm_slot)

                for i in range(2):
                    scatter(i, i)
                with pool.Fori(1, HALF // 2) as k:
                    for s in range(2):
                        scatter(2 * k + s, s)
                scatter(HALF - 1, (HALF - 1) % 2)
                for s in range(2):
                    pool.wait_ge(S["scattered"][s], 16 * BATCH * ((HALF + 1 - s) // 2))
                for m in range(2):
                    gather(m, m, (HALF + m) % 2)
                with pool.Fori(1, HALF // 2) as k:
                    for s in range(2):
                        gather(2 * k + s, s, (HALF + s) % 2)
                gather(HALF - 1, (HALF - 1) % 2, (2 * HALF - 1) % 2)
                for i in range(GROUPS, GROUPS + 5):
                    norms(i, i % 2)
                for m in (HALF - 2, HALF - 1):
                    fetched(m, m % 2)

            @block.tensor
            def _(pe):
                def step(i, u):
                    g = live(i, 0)
                    if g is not None:
                        pe.wait_ge(S["x_in"][u], landed(g, u, 4, 16))
                        wait_from(pe, S["xT"], g)
                        transpose_tiles(pe, bank[0], x_rows[u], c).then_inc(S["x_turned"], 1)
                    g = live(i, 2)
                    if g is not None:
                        s = (u - 2) % 2
                        pe.wait_ge(S["x1_rows"], g + 1)
                        wait_from(pe, S["x1T"], g)
                        transpose_tiles(pe, bank[4], x1_rows[(u - 2) % 4], c).then_inc(S["x1_turned"], 1)
                    g = live(i, 1)
                    if g is not None:
                        s = (u - 1) % 2
                        pe.wait_ge(S["hT"], g + 1)
                        wait_from(pe, S["h_rows"], g)
                        transpose_tiles(pe, bank[2], h1T[s], c)
                        transpose_tiles(pe, bank[3], h2T[s], c).then_inc(S["h_turned"], 1)
                    g = live(i, 0)
                    if g is not None:
                        pe.wait_ge(S["xT"], g + 1)
                        wait_from(pe, S["hT"], g)
                        pe.matmul(bank[1][:, :], c.proj_w[:, :], xT[u % 2][:, :], start=True, stop=True)\
                          .then_inc(S["projected"], 1)
                    g = live(i, 2)
                    if g is not None:
                        s = (u - 2) % 2
                        pe.wait_ge(S["x1T"], g + 1)
                        wait_from(pe, S["skip_bias"], g)
                        wait_from(pe, S["tanh"], g)
                        for j in range(TILES):
                            at = slice(j * P, (j + 1) * P)
                            pe.matmul(bank[5][:, at], x1T[s][:, at], c.wskip[:, :], start=True, stop=True)
                            last = pe.matmul(bank[6][:, j:j + 1], x1T[s][:, at], c.gate_own[:, :], start=True, stop=True)
                        last.then_inc(S["skipped"], 1)

                run_steps(pe, step, 4, 8, 5)

            @block.scalar
            def _(act):
                def step(i, u):
                    g = live(i, 5)
                    if g is not None:
                        s = (u - 5) % 2
                        act.wait_ge(S["shift2"], g + 1)
                        if not isinstance(g, int) or g >= 2:
                            act.wait_ge(S["x2_out"][s], landed(g - 2, s, 2, 16))
                        layernorm_apply(act, x2_rows[s], res[s], ln[2][s]).then_inc(S["x2_rows"], 1)
                    g = live(i, 1)
                    if g is not None:
                        s, s4 = (u - 1) % 2, (u - 1) % 4
                        act.wait_ge(S["shift0"], g + 1)
                        wait_from(act, S["x1_turned"], g - 3)
                        wait_from(act, S["residual"], g - 3)
                        if not isinstance(g, int) or g >= 4:
                            act.wait_ge(S["x1_out"][s], landed(g - 4, s, 2, 16))
                        layernorm_apply(act, x1_rows[s4], xc[s], ln[0][s]).then_inc(S["x1_rows"], 1)
                    g = live(i, 3)
                    if g is not None:
                        s = (u - 3) % 2
                        act.wait_ge(S["shift1"], g + 1)
                        wait_from(act, S["scaled_gamma"], g - 1)
                        layernorm_apply(act, normed[s], mixed[s], ln[1][s]).then_inc(S["normed"], 1)
                    g = live(i, 0)
                    if g is not None:
                        s = u % 2
                        act.wait_ge(S["x_turned"], g + 1)
                        wait_from(act, S["projected"], g - 1)
                        act.copy(xT[s][:, :], bank[0][:, :]).then_inc(S["xT"], 1)
                    g = live(i, 1)
                    if g is not None:
                        s = (u - 1) % 2
                        act.wait_ge(S["h_turned"], g + 1)
                        if not isinstance(g, int) or g >= 2:
                            act.wait_ge(S["h1_out"][s], landed(g - 2, s, 2, 16))
                            act.wait_ge(S["h2_out"][s], landed(g - 2, s, 2, 16))
                        act.copy(h1_rows[s][:, :], bank[2][:, :])
                        act.copy(h2_rows[s][:, :], bank[3][:, :]).then_inc(S["h_rows"], 1)
                    g = live(i, 2)
                    if g is not None:
                        s = (u - 2) % 2
                        act.wait_ge(S["x1_turned"], g + 1)
                        wait_from(act, S["skipped"], g - 1)
                        act.copy(x1T[s][:, :], bank[4][:, :]).then_inc(S["x1T"], 1)
                    g = live(i, 0)
                    if g is not None:
                        s = u % 2
                        act.wait_ge(S["projected"], g + 1)
                        wait_from(act, S["h_turned"], g - 1)
                        act.activation(h1T[s][:, :], bank[1][:, :], ACT.Identity, bias=c.h1_bias[:, :])
                        act.activation(h2T[s][:, :], bank[1][:, :], ACT.Identity, bias=c.h2_bias[:, :]).then_inc(S["hT"], 1)
                    g = live(i, 2)
                    if g is not None:
                        s = (u - 2) % 2
                        act.wait_ge(S["skipped"], g + 1)
                        wait_from(act, S["gate"], g - 1)
                        act.activation(th[s][:, :], bank[6][:, 0:TILES], ACT.Tanh, bias=c.gate_bias[:, :], scale=0.5)\
                           .then_inc(S["tanh"], 1)

                run_steps(act, step, 4, 8, 5)

            @block.vector
            def _(dve):
                def step(i, u):
                    for lag, mark_scale, mark_shift, n in ((5, S["scale2"], S["shift2"], 2), (1, S["scale0"], S["shift0"], 0),
                                                           (3, S["scale1"], S["shift1"], 1)):
                        g = live(i, lag)
                        if g is not None:
                            s = (u - lag) % 2
                            dve.wait_ge(S["root"], i)
                            done = {0: S["x1_rows"], 1: S["normed"], 2: S["x2_rows"]}[n]
                            wait_from(dve, done, g - 1)
                            layernorm_factors(dve, mark_scale, mark_shift, g, root[(u - 1) % 2][:, n, :], None, ln[n][s])
                    here = spread[u % 2]
                    if not (isinstance(i, int) and i == 0):
                        dve.wait_ge(S["root"], i)
                    last = None
                    g = live(i, 0)
                    if g is not None:
                        s = u % 2
                        dve.wait_ge(S["x_in"][u], landed(g, u, 4, 16))
                        wait_from(dve, S["x1_rows"], g - 1)
                        dve.wait_ge(S["filled"], 1)
                        dve.tensor_tensor(tiles(xc[s][:, :]), tiles(x_rows[u][:, :]),
                                          c.empty_row[:, :].unsqueeze(1).to_broadcast([P, TILES, D]), ALU.add)\
                           .then_inc(S["centred"], 1)
                        dve.wait_ge(S["centred"], g + 1)
                        last = layernorm_stats(dve, S, S["stats0"], S["moments0"], g, xc[s], ln[0][s], here[:, 0, :])
                    g = live(i, 4)
                    if g is not None:
                        s = (u - 4) % 2
                        last = prelu_residual(dve, S, c, g, aff[s], neg[s], pre[s], x1_rows[(u - 4) % 4][:, :], res[s],
                                              S["x2_rows"], ln[2][s], here[:, 2, :])
                    g = live(i, 2)
                    if g is not None:
                        s = (u - 2) % 2
                        dve.wait_ge(S["skipped"], g + 1)
                        dve.tensor_tensor(tiles(skip[s][:, :]), tiles(bank[5][:, :]),
                                          c.bskip_row[:, :].unsqueeze(1).to_broadcast([P, TILES, D]), ALU.add)\
                           .then_inc(S["skip_bias"], 1)
                        dve.wait_ge(S["tanh"], g + 1)
                        dve.tensor_scalar(gate[s][:, :], th[s][:, :], 0.5, 0.5, ALU.mult, ALU.add).then_inc(S["gate"], 1)
                        dve.wait_ge(S["gate"], g + 1)
                        wait_from(dve, S["normed"], g - 1)
                        dve.tensor_tensor(tiles(mixed[s][:, :]), tiles(skip[s][:, :]), over_features(gate[s][:, :], D),
                                          ALU.mult).then_inc(S["mixed"], 1)
                        dve.wait_ge(S["mixed"], g + 1)
                        last = layernorm_stats(dve, S, S["stats1"], S["moments1"], g, mixed[s], ln[1][s], here[:, 1, :])
                    if last is None:
                        last = dve.memset(here[:, 0, :], 1.0)
                    last.then_inc(S["spread"], 1)
                    g = live(i, 3)
                    if g is not None:
                        affine(dve, S, c, g, normed[(u - 3) % 2], gam[(u - 3) % 2], aff[(u - 3) % 2])

                run_steps(dve, step, 4, 8, 5)


def affine(eng, S, c, g, normed, gam, aff):
    eng.wait_ge(S["normed"], g + 1)
    eng.tensor_tensor(tiles(gam[:, :]), tiles(normed[:, :]), c.gamma_row[:, :].unsqueeze(1).to_broadcast([P, TILES, D]),
                      ALU.mult).then_inc(S["scaled_gamma"], 1)
    eng.wait_ge(S["scaled_gamma"], g + 1)
    wait_from(eng, S["prelu_done"], g - 1)
    eng.tensor_tensor(tiles(aff[:, :]), tiles(gam[:, :]), c.beta_row[:, :].unsqueeze(1).to_broadcast([P, TILES, D]),
                      ALU.add).then_inc(S["affine"], 1)


def prelu_residual(dve, S, c, g, aff, neg, pre, x1_rows, res, res_read, ln, spread):
    dve.wait_ge(S["affine"], g + 1)
    dve.tensor_scalar(neg[:, :], aff[:, :], 0.0, c.prelu[:, :], ALU.min, ALU.mult).then_inc(S["negative"], 1)
    dve.wait_ge(S["negative"], g + 1)
    dve.scalar_tensor_tensor(pre[:, :], aff[:, :], 0.0, neg[:, :], ALU.max, ALU.add).then_inc(S["prelu_done"], 1)
    dve.wait_ge(S["prelu_done"], g + 1)
    wait_from(dve, res_read, g - 1)
    dve.tensor_tensor(res[:, :], pre[:, :], x1_rows, ALU.add).then_inc(S["residual"], 1)
    dve.wait_ge(S["residual"], g + 1)
    return layernorm_stats(dve, S, S["stats2"], S["moments2"], g, res, ln, spread)


def edge_scalars(nc, a, c, e, r, bank):
    QUARTER = COLS // 4
    with ExitStack() as ctx:
        S = named_semaphores(nc, ctx, "scal", "loaded turned chain")

        def sb(name, shape, dt=F32):
            return ctx.enter_context(nc.sbuf_tensor(f"scal_{name}", shape, dt))

        line = [sb(f"line{n}", [QUARTER, 4, P]) for n in range(2)]
        own = [sb(f"own{n}", [P, COLS]) for n in range(2)]
        near = [sb(f"near{n}", [P, COLS], I32) for n in range(2)]
        weight, dst = sb("weight", [P, COLS]), sb("dst", [P, COLS])
        nearf = [sb(f"nearf{n}", [P, COLS]) for n in range(2)]
        both, elsewhere = sb("both", [P, COLS]), sb("elsewhere", [P, COLS])

        with nc.Block() as block:
            @block.sync
            def _(sp):
                for n, row in enumerate((r.dinv2, r.dinv3)):
                    sp.dma_start(line[n][:, :, :], row.rearrange("(b t p) -> t b p", b=4, p=P)).then_inc(S["loaded"], 16)
                sp.dma_start(near[0][:, :], a["prev_tiles"]).then_inc(S["loaded"], 16)
                sp.dma_start(near[1][:, :], a["next_tiles"]).then_inc(S["loaded"], 16)
                sp.dma_start(weight[:, :], a["weight_tiles"]).then_inc(S["loaded"], 16)
                sp.wait_ge(S["loaded"], 16 * 5)

            @block.tensor
            def _(pe):
                pe.wait_ge(S["loaded"], 16 * 5)
                for n in range(2):
                    for b in range(4):
                        last = pe.transpose(bank[n][:, b * QUARTER:(b + 1) * QUARTER], line[n][:, b, :],
                                            c.ident[0:QUARTER, 0:QUARTER])
                last.then_inc(S["turned"], 1)

            @block.vector
            def _(dve):
                links = [0]

                def link(ins):
                    links[0] += 1
                    ins.then_inc(S["chain"], 1)
                    dve.wait_ge(S["chain"], links[0])

                dve.wait_ge(S["loaded"], 16 * 5)
                dve.tensor_copy(dst[:, :], e.dst[:, :])
                for n in range(2):
                    dve.tensor_copy(nearf[n][:, :], near[n][:, :])
                dve.tensor_copy(e.src_at_end[:, :], e.fetched[:, :, 0])
                dve.tensor_copy(e.src_at_start[:, :], e.fetched[:, :, 1])
                dve.wait_ge(S["turned"], 1)
                for n in range(2):
                    last = dve.tensor_copy(own[n][:, :], bank[n][:, 0:COLS])
                link(last)
                dve.tensor_tensor(e.is_start[:, :], dst[:, :], nearf[0][:, :], ALU.not_equal)
                dve.tensor_tensor(e.is_end[:, :], dst[:, :], nearf[1][:, :], ALU.not_equal)
                dve.tensor_tensor(both[:, :], weight[:, :], e.fetched[:, :, 2], ALU.mult)
                dve.tensor_tensor(e.self2[:, :], own[0][:, :], own[0][:, :], ALU.mult)
                dve.tensor_tensor(e.self3[:, :], own[1][:, :], own[1][:, :], ALU.mult)
                link(dve.tensor_tensor(e.norm3[:, :], own[1][:, :], e.fetched[:, :, 3], ALU.mult))
                dve.tensor_tensor(e.norm2[:, :], own[0][:, :], both[:, :], ALU.mult)
                link(dve.tensor_scalar(elsewhere[:, :], e.is_start[:, :], -float(NOWHERE), float(NOWHERE),
                                       ALU.mult, ALU.add))
                dve.tensor_tensor(e.out_row[:, :], elsewhere[:, :], dst[:, :], ALU.add)


def conv_pass(nc, a, c, e, r, bank, l, src_table, own_table, src_rows_at, backward, out_table, place_mask):
    first_layer, last_layer = l == 0, l == LAYERS - 1
    flow = slice(None, None, -1) if backward else slice(None)
    entry = slice(GROUP - 1, GROUP) if not backward else slice(0, 1)
    same = r.same_next if backward else r.same_prev

    def at(g):
        return GROUPS - 1 - g if backward else g

    with ExitStack() as ctx:
        S = named_semaphores(nc, ctx, f"conv{l}", "staged own_staged turned src_done own_done phi_hid phi_act msg summed mean psi_hid "
                             "psi_act conv conv_act h h_turned rows residual stats moments spread root plain scale shift",
                             "gathered own_in mask_in inv_in x_in stored")

        def sb(name, shape, dt=F32):
            return [ctx.enter_context(nc.sbuf_tensor(f"conv{l}_{name}{s}", shape, dt)) for s in range(2)]

        src_rows, own_rows, x_rows = (sb(n, [P, GROUP]) for n in ("src_rows", "own_rows", "x_rows"))
        srcT, ownT, phi0, phi1, psi0, psi1, total, mean, convT, hT, res, rows = (
            sb(n, [P, GROUP]) for n in "srcT ownT phi0 phi1 psi0 psi1 total mean convT hT res rows".split())
        phi, psi = list(zip(phi0, phi1)), list(zip(psi0, psi1))
        mask, inv = sb("mask", [P, GROUP], BF16), sb("inv", [P, GROUP])
        at_src, at_own = sb("at_src", [P, TILES], I32), sb("at_own", [P, TILES], I32)
        spread, root, plain = (sb(n, [P, TILES]) for n in ("spread", "root", "plain"))
        ln = layernorm_buffers(lambda n, s: ctx.enter_context(nc.sbuf_tensor(f"conv{l}_{n}", s, F32)), "ln")
        b_own, b_src, b_phi, b_msg, b_psi, b_rows = bank[0], bank[1], bank[2:4], bank[4], bank[5:7], bank[7]
        b_conv, b_proj = b_src, b_own
        out_done = S["rows"]

        with nc.Block() as block:
            @block.sync
            def _(sp):
                def step(i, u):
                    g = live(i, 0)
                    if g is not None:
                        s = u
                        if not first_layer:
                            wait_alone(sp, S["passed"], S["turned"], g - 1)
                            sp.dma_start(tiles(own_rows[s][:, :]), group_rows(own_table, 0, at(g))).then_inc(S["own_in"][s], 16)
                        wait_alone(sp, S["passed"], S["summed"], g - 1)
                        sp.dma_start(mask[s][:, :], same[bass.ds(at(g) * GROUP, GROUP)].rearrange("(o n) -> o n", o=1)
                                     .to_broadcast([P, GROUP])).then_inc(S["mask_in"][s], 16)
                        wait_alone(sp, S["passed"], S["mean"], g - 1)
                        sp.dma_start(inv[s][:, :], r.inv_count[bass.ds(at(g) * GROUP, GROUP)].rearrange("(o n) -> o n", o=1)
                                     .to_broadcast([P, GROUP])).then_inc(S["inv_in"][s], 16)
                    g = live(i, 2)
                    if g is not None:
                        s = u
                        wait_alone(sp, S["passed"], out_done, g + 1)
                        sp.dma_start(group_rows(out_table, 0, at(g)), tiles(rows[s][:, :])).then_inc(S["stored"][s], 16)

                run_steps(sp, step, 2, 4, 2)
                for s in range(2):
                    sp.wait_ge(S["stored"][s], 16 * (GROUPS // 2))

            @block.gpsimd
            def _(pool):
                def gather(rows_, index, table, arrived, s):
                    for j in range(TILES):
                        pool.indirect_dma_start(rows_[:, j * D:(j + 1) * D], None, table[:, :],
                                                bass.IndirectOffsetOnAxis(ap=index[:, j:j + 1], axis=0))\
                            .then_inc(arrived[s], 16)

                def step(i, u):
                    g = live(i, 0)
                    if g is not None:
                        s = u
                        wait_alone(pool, S["passed"], S["turned"], g - 1)
                        if first_layer:
                            pool.tensor_copy(at_own[s][:, :], e.dst[:, bass.ds(at(g) * TILES, TILES)])
                        pool.tensor_copy(at_src[s][:, :], src_rows_at[:, bass.ds(at(g) * TILES, TILES)]).then_inc(S["staged"], 1)
                        wait_alone(pool, S["passed"], S["staged"], g + 1)
                        gather(src_rows[s], at_src[s], src_table, S["gathered"], s)
                        if first_layer:
                            gather(own_rows[s], at_own[s], own_table, S["own_in"], s)
                    g = live(i, 1)
                    if g is not None and last_layer:
                        s = (u - 1) % 2
                        wait_alone(pool, S["passed"], S["residual"], g - 1)
                        pool.tensor_copy(at_own[s][:, :], e.dst[:, bass.ds(at(g) * TILES, TILES)]).then_inc(S["own_staged"], 1)
                        wait_alone(pool, S["passed"], S["own_staged"], g + 1)
                        gather(x_rows[s], at_own[s], a["x"], S["x_in"], s)

                run_steps(pool, step, 2, 4, 1)

            @block.tensor
            def _(pe):
                def step(i, u):
                    g = live(i, 0)
                    if g is not None:
                        s = u
                        pe.wait_ge(S["gathered"][s], landed(g, s, 2, 16 * TILES))
                        pe.wait_ge(S["own_in"][s], landed(g, s, 2, 16 * TILES if first_layer else 16))
                        wait_from(pe, S["own_done"], g)
                        wait_from(pe, S["conv_act"], g - 1)
                        if first_layer:
                            wait_from(pe, S["h"], g - 1)
                        transpose_tiles(pe, b_src, src_rows[s], c)
                        transpose_tiles(pe, b_own, own_rows[s], c).then_inc(S["turned"], 1)
                    g = live(i, 1)
                    if g is not None:
                        s = (u - 1) % 2
                        pe.wait_ge(S["mean"], g + 1)
                        for h in range(HALVES):
                            wait_from(pe, S["psi_act"], HALVES * g)
                            pe.matmul(b_psi[h][:, :], c.psi_w1[l][:, h * P:(h + 1) * P], mean[s][:, :],
                                      start=True, stop=True).then_inc(S["psi_hid"], 1)
                    g = live(i, 0)
                    if g is not None:
                        s = u
                        pe.wait_ge(S["src_done"], g + 1)
                        pe.wait_ge(S["own_done"], g + 1)
                        for h in range(HALVES):
                            wait_from(pe, S["phi_act"], HALVES * g)
                            pe.matmul(b_phi[h][:, :], c.w_src[l][:, h * P:(h + 1) * P], srcT[s][:, :], start=True, stop=False)
                            pe.matmul(b_phi[h][:, :], c.w_own[l][:, h * P:(h + 1) * P], ownT[s][:, :],
                                      start=False, stop=True).then_inc(S["phi_hid"], 1)
                    g = live(i, 1)
                    if g is not None:
                        s = (u - 1) % 2
                        pe.wait_ge(S["psi_act"], HALVES * g + HALVES)
                        for h in range(HALVES):
                            last = pe.matmul(b_conv[:, :], c.psi_w2[l][:, h, :], psi[s][h][:, :],
                                             start=(h == 0), stop=(h == HALVES - 1))
                        if first_layer:
                            last = pe.matmul(b_proj[:, :], c.proj_w[:, :], ownT[s][:, :], start=True, stop=True)
                        last.then_inc(S["conv"], 1)
                    g = live(i, 0)
                    if g is not None:
                        s = u
                        pe.wait_ge(S["phi_act"], HALVES * g + HALVES)
                        wait_from(pe, S["summed"], g)
                        for h in range(HALVES):
                            last = pe.matmul(b_msg[:, :], c.phi_w2[l][:, h, :], phi[s][h][:, :],
                                             start=(h == 0), stop=(h == HALVES - 1))
                        last.then_inc(S["msg"], 1)
                    g = live(i, 1)
                    if g is not None:
                        s = (u - 1) % 2
                        pe.wait_ge(S["conv_act"] if last_layer else S["h"], g + 1)
                        wait_from(pe, S["residual"] if last_layer else S["rows"], g)
                        transpose_tiles(pe, b_rows, convT[s] if last_layer else hT[s], c).then_inc(S["h_turned"], 1)

                run_steps(pe, step, 2, 4, 1)

            @block.scalar
            def _(act):
                def step(i, u):
                    g = live(i, 0)
                    if g is not None:
                        s = u
                        act.wait_ge(S["turned"], g + 1)
                        wait_from(act, S["phi_hid"], HALVES * (g - 1))
                        act.copy(srcT[s][:, :], b_src[:, :]).then_inc(S["src_done"], 1)
                        if first_layer:
                            wait_from(act, S["conv"], g - 1)
                            act.copy(ownT[s][:, :], b_own[:, :]).then_inc(S["own_done"], 1)
                    g = live(i, 1)
                    if g is not None:
                        s = (u - 1) % 2
                        wait_from(act, S["conv"], g - 1)
                        for h in range(HALVES):
                            act.wait_ge(S["psi_hid"], HALVES * g + h + 1)
                            act.activation(psi[s][h][:, :], b_psi[h][:, :], ACT.Relu,
                                           bias=c.psi_b1_mean[:, l, h:h + 1]).then_inc(S["psi_act"], 1)
                    g = live(i, 2)
                    if g is not None and last_layer:
                        s = u
                        act.wait_ge(S["spread"], g + 1)
                        act.activation(root[s][:, :], spread[s][:, :], ACT.Sqrt).then_inc(S["root"], 1)
                    g = live(i, 0)
                    if g is not None:
                        s = u
                        wait_from(act, S["msg"], g - 1)
                        for h in range(HALVES):
                            act.wait_ge(S["phi_hid"], HALVES * g + h + 1)
                            act.activation(phi[s][h][:, :], b_phi[h][:, :], ACT.Relu,
                                           bias=c.phi_b1[:, l, h:h + 1]).then_inc(S["phi_act"], 1)
                    g = live(i, 2)
                    if g is not None and last_layer:
                        s = u
                        act.wait_ge(S["shift"], g + 1)
                        if not isinstance(g, int) or g >= 2:
                            act.wait_ge(S["stored"][s], landed(g - 2, s, 2, 16))
                        layernorm_apply(act, rows[s], res[s], ln[s]).then_inc(S["rows"], 1)
                    g = live(i, 1)
                    if g is not None:
                        s = (u - 1) % 2
                        act.wait_ge(S["conv"], g + 1)
                        wait_from(act, S["h_turned"], g - 1)
                        act.activation(convT[s][:, :], b_conv[:, :], ACT.Identity if last_layer else ACT.Relu,
                                       bias=c.psi_b2[:, l:l + 1]).then_inc(S["conv_act"], 1)

                run_steps(act, step, 2, 4, 2)

            @block.vector
            def _(dve):
                def step(i, u):
                    g = live(i, 0)
                    if g is not None and not first_layer:
                        s = u
                        dve.wait_ge(S["mask_in"][s], landed(g, s, 2, 16))
                        dve.wait_ge(S["turned"], g + 1)
                        wait_from(dve, S["phi_hid"], HALVES * (g - 1))
                        wait_from(dve, S["own_done"], g)
                        carried = 0.0 if isinstance(g, int) and g == 0 else ownT[1 - s][:, entry]
                        dve.tensor_tensor_scan(ownT[s][:, flow], mask[s][:, flow], b_own[:, flow], carried,
                                               ALU.mult, ALU.add).then_inc(S["own_done"], 1)
                    g = live(i, 2)
                    if g is not None and last_layer:
                        s = u
                        dve.wait_ge(S["x_in"][s], landed(g, s, 2, 16 * TILES))
                        dve.wait_ge(S["h_turned"], g + 1)
                        wait_from(dve, S["rows"], g - 1)
                        dve.tensor_tensor(res[s][:, :], b_rows[:, :], x_rows[s][:, :], ALU.add).then_inc(S["residual"], 1)
                        dve.wait_ge(S["residual"], g + 1)
                        layernorm_stats(dve, S, S["stats"], S["moments"], g, res[s], ln[s], spread[s][:, :]).then_inc(S["spread"], 1)
                    g = live(i, 1)
                    if g is not None and not last_layer:
                        s = (u - 1) % 2
                        dve.wait_ge(S["conv_act"], g + 1)
                        wait_from(dve, S["h_turned"], g - 1)
                        if first_layer:
                            dve.scalar_tensor_tensor(hT[s][:, :], b_proj[:, :], c.proj_b[:, :], convT[s][:, :],
                                                     ALU.add, ALU.add).then_inc(S["h"], 1)
                        else:
                            dve.tensor_tensor(hT[s][:, :], convT[s][:, :], ownT[s][:, :], ALU.add).then_inc(S["h"], 1)
                    g = live(i, 2)
                    if g is not None and last_layer:
                        s = u
                        dve.wait_ge(S["root"], g + 1)
                        wait_from(dve, S["rows"], g - 1)
                        dve.reciprocal(plain[s][:, :], root[s][:, :]).then_inc(S["plain"], 1)
                        dve.wait_ge(S["plain"], g + 1)
                        layernorm_factors(dve, S["scale"], S["shift"], g, plain[s][:, :],
                                          place_mask[:, bass.ds(at(g) * TILES, TILES)], ln[s])
                    g = live(i, 0)
                    if g is not None:
                        s = u
                        dve.wait_ge(S["mask_in"][s], landed(g, s, 2, 16))
                        dve.wait_ge(S["msg"], g + 1)
                        wait_from(dve, S["summed"], g)
                        carried = 0.0 if isinstance(g, int) and g == 0 else total[1 - s][:, entry]
                        dve.tensor_tensor_scan(total[s][:, flow], mask[s][:, flow], b_msg[:, flow], carried,
                                               ALU.mult, ALU.add).then_inc(S["summed"], 1)
                        dve.wait_ge(S["inv_in"][s], landed(g, s, 2, 16))
                        dve.wait_ge(S["summed"], g + 1)
                        wait_from(dve, S["psi_hid"], HALVES * (g - 1))
                        dve.tensor_tensor(mean[s][:, :], total[s][:, :], inv[s][:, :], ALU.mult).then_inc(S["mean"], 1)
                    g = live(i, 1)
                    if g is not None and not last_layer:
                        s = (u - 1) % 2
                        dve.wait_ge(S["h_turned"], g + 1)
                        if not isinstance(g, int) or g >= 2:
                            wait_alone(dve, S["passed"], S["stored"][s], landed(g - 2, s, 2, 16))
                        dve.tensor_tensor(tiles(rows[s][:, :]), tiles(b_rows[:, :]),
                                          over_features(place_mask[:, bass.ds(at(g) * TILES, TILES)], D),
                                          ALU.mult).then_inc(S["rows"], 1)

                run_steps(dve, step, 2, 4, 2)


def gcn_pass(nc, c, e, r, bank, n, table, src_rows_at, backward, out_table, residual_table, node_table):
    final = residual_table is not None
    lane = not final
    weighted = n < 2
    wide = HID2 if n == 1 else D
    out_wide = HID2 if weighted else D
    norm, self_norm = (e.norm2, e.self2) if weighted else (e.norm3, e.self3)
    out_at = out_wide if n == 1 else 0
    to_output = n == 3
    flow = slice(None, None, -1) if backward else slice(None)
    entry = slice(GROUP - 1, GROUP) if not backward else slice(0, 1)
    same = r.same_next if backward else r.same_prev
    place_mask = e.is_start if backward else e.is_end
    row_wide = D if final else out_wide

    def at(g):
        return GROUPS - 1 - g if backward else g

    with ExitStack() as ctx:
        S = named_semaphores(nc, ctx, f"gcn{n}", "staged own_scaled src_scaled summed turned own_turned agg product y "
                             "own_done y_turned rows residual stats moments spread root plain scale shift normed out_staged "
                             "n_turned n_xT n_hid n_y1 n_hid2 n_y2 n_y1_turned n_y1_rows n_sum n_sum_turned n_sum_rows",
                             four_slots="gathered own_in mask_in res_in stored n_in n_y1_out n_out scattered")

        def sb(name, shape, dt=F32, slots=2):
            return [ctx.enter_context(nc.sbuf_tensor(f"gcn{n}_{name}{s}", shape, dt)) for s in range(slots)]

        src_rows, own_rows = (sb(m, [P, TILES * wide], slots=4) for m in ("src_rows", "own_rows"))
        src_scaled, own_scaled, summed = (sb(m, [P, TILES * wide]) for m in ("src_scaled", "own_scaled", "summed"))
        mask = sb("mask", [P, GROUP], BF16, 4)
        at_src = sb("at_src", [P, TILES], I32, 4)
        agg = sb("agg", [P, GROUP])
        y, rows = (sb(m, [P, GROUP], slots=4) for m in ("y", "rows"))
        if final:
            res_rows, res = (sb(m, [P, GROUP], slots=4) for m in ("res_rows", "res"))
            at_out = sb("at_out", [P, TILES], I32, 4)
        else:
            n_rows, n_xT, n_y, n_y2, n_y1_rows, n_sum_rows, n_new = (
                sb(m, [P, GROUP], slots=4) for m in "n_rows n_xT n_y n_y2 n_y1_rows n_sum_rows n_new".split())
            n_sum = sb("n_sum", [P, GROUP])
        spread, root, plain = (sb(m, [P, TILES]) for m in ("spread", "root", "plain"))
        ln = layernorm_buffers(lambda name, shape: ctx.enter_context(nc.sbuf_tensor(f"gcn{n}_{name}", shape, F32)), "ln")
        norm_lag = 3 if final else 5
        b_agg, b_product, b_rows, b_own = bank[0:4]
        nb_x, nb_hid, nb_hid2, nb_y1, nb_sum = bank[3:8]

        def by_tile(ap, width):
            return ap[:, 0:TILES * width].rearrange("p (j f) -> p j f", j=TILES)

        with nc.Block() as block:
            @block.sync
            def _(sp):
                def step(i, u):
                    g = live(i, 0)
                    if g is not None:
                        s = u
                        wait_alone(sp, S["passed"], S["own_scaled"], g - 3)
                        if n == 1:
                            wait_alone(sp, S["passed"], S["own_turned"], g - 3)
                        sp.dma_start(by_tile(own_rows[s], wide), group_rows(table, 0, at(g))).then_inc(S["own_in"][s], 16)
                        wait_alone(sp, S["passed"], S["own_done"] if n == 1 else S["agg"], g - 3)
                        sp.dma_start(mask[s][:, :], same[bass.ds(at(g) * GROUP, GROUP)].rearrange("(o n) -> o n", o=1)
                                     .to_broadcast([P, GROUP])).then_inc(S["mask_in"][s], 16)
                        if lane:
                            wait_alone(sp, S["passed"], S["n_turned"], g - 3)
                            sp.dma_start(tiles(n_rows[s][:, :]), group_rows(table, NODE0, g)).then_inc(S["n_in"][s], 16)
                    g = live(i, 1)
                    if g is not None and final:
                        s = (u - 1) % 4
                        wait_alone(sp, S["passed"], S["residual"], g - 3)
                        sp.dma_start(tiles(res_rows[s][:, :]), group_rows(residual_table, 0, at(g))).then_inc(S["res_in"][s], 16)
                    g = live(i, 6)
                    if g is not None:
                        s = (u - 6) % 4
                        if lane:
                            wait_alone(sp, S["passed"], S["rows"], g + 1)
                            sp.dma_start(group_rows(out_table, 0, at(g)), by_tile(rows[s], row_wide))\
                              .then_inc(S["stored"][s], 16)
                            wait_alone(sp, S["passed"], S["n_y1_rows"], g + 1)
                            sp.dma_start(group_rows(out_table, NODE0, g), by_tile(n_y1_rows[s], out_wide))\
                              .then_inc(S["n_y1_out"][s], 16)
                        elif not to_output:
                            wait_alone(sp, S["passed"], S["normed"], g + 1)
                            sp.dma_start(group_rows(out_table, 0, at(g)), tiles(rows[s][:, :])).then_inc(S["stored"][s], 16)
                    g = live(i, 9)
                    if g is not None and lane:
                        s = (u - 9) % 4
                        wait_alone(sp, S["passed"], S["normed"], g + 1)
                        base = 0 if node_table.shape[0] == ROWS else NODE0
                        sp.dma_start(group_rows(node_table, base, g), tiles(n_new[s][:, :])).then_inc(S["n_out"][s], 16)

                run_steps(sp, step, 4, 12, 9 if lane else 6)
                for s in range(4):
                    for out_ in ((S["stored"], S["n_y1_out"], S["n_out"]) if lane else () if to_output else (S["stored"],)):
                        sp.wait_ge(out_[s], 16 * groups_of_slot(s))

            @block.gpsimd
            def _(pool):
                def step(i, u):
                    g = live(i, 0)
                    if g is not None:
                        s = u
                        wait_alone(pool, S["passed"], S["src_scaled"], g - 3)
                        pool.tensor_copy(at_src[s][:, :], src_rows_at[:, bass.ds(at(g) * TILES, TILES)]).then_inc(S["staged"], 1)
                        wait_alone(pool, S["passed"], S["staged"], g + 1)
                        for j in range(TILES):
                            pool.indirect_dma_start(src_rows[s][:, j * wide:(j + 1) * wide], None, table[:, :],
                                                    bass.IndirectOffsetOnAxis(ap=at_src[s][:, j:j + 1], axis=0))\
                                .then_inc(S["gathered"][s], 16)
                    g = live(i, 7)
                    if g is not None and to_output:
                        s = (u - 7) % 4
                        wait_alone(pool, S["passed"], S["normed"], g + 1)
                        if not isinstance(g, int) or g >= 4:
                            wait_alone(pool, S["passed"], S["scattered"][s], landed(g - 4, s, 4, 16 * TILES))
                        pool.tensor_copy(at_out[s][:, :], e.out_row[:, bass.ds(at(g) * TILES, TILES)]).then_inc(S["out_staged"], 1)
                        wait_alone(pool, S["passed"], S["out_staged"], g + 1)
                        for j in range(TILES):
                            pool.indirect_dma_start(out_table[:, :], bass.IndirectOffsetOnAxis(ap=at_out[s][:, j:j + 1], axis=0),
                                                    rows[s][:, j * D:(j + 1) * D], None, bounds_check=ROWS - 1,
                                                    oob_is_err=False).then_inc(S["scattered"][s], 16)

                run_steps(pool, step, 4, 8, 7 if to_output else 0)
                if to_output:
                    for s in range(4):
                        pool.wait_ge(S["scattered"][s], 16 * TILES * groups_of_slot(s))

            @block.tensor
            def _(pe):
                def step(i, u):
                    g = live(i, 0)
                    if g is not None:
                        s = u % 2
                        wait_alone(pe, S["passed"], S["summed"], g + 1)
                        wait_alone(pe, S["passed"], S["agg"], g)
                        for j in range(TILES):
                            last = pe.transpose(b_agg[0:wide, j * P:(j + 1) * P],
                                                summed[s][:, j * wide:(j + 1) * wide], c.ident[:, :])
                        last.then_inc(S["turned"], 1)
                        if n == 1:
                            wait_alone(pe, S["passed"], S["own_done"], g)
                            for j in range(TILES):
                                last = pe.transpose(b_own[0:wide, j * P:(j + 1) * P],
                                                    own_rows[u][:, j * wide:(j + 1) * wide], c.ident[:, :])
                            last.then_inc(S["own_turned"], 1)
                        if lane:
                            wait_alone(pe, S["passed"], S["n_in"][u], landed(g, u, 4, 16))
                            wait_alone(pe, S["passed"], S["n_xT"], g)
                            transpose_tiles(pe, nb_x, n_rows[u], c).then_inc(S["n_turned"], 1)
                    g = live(i, 2)
                    if g is not None:
                        s = (u - 2) % 4
                        wait_alone(pe, S["passed"], S["y"], g + 1)
                        wait_alone(pe, S["passed"], S["residual"] if final else S["rows"], g)
                        for j in range(TILES):
                            last = pe.transpose(b_rows[:, j * row_wide:(j + 1) * row_wide],
                                                y[s][0:row_wide, j * P:(j + 1) * P], c.ident[0:row_wide, 0:row_wide])
                        last.then_inc(S["y_turned"], 1)
                        if lane:
                            wait_alone(pe, S["passed"], S["n_y1"], g + 1)
                            wait_alone(pe, S["passed"], S["n_y1_rows"], g)
                            for j in range(TILES):
                                last = pe.transpose(nb_y1[:, j * out_wide:(j + 1) * out_wide],
                                                    n_y[s][0:out_wide, j * P:(j + 1) * P], c.ident[0:out_wide, 0:out_wide])
                            last.then_inc(S["n_y1_turned"], 1)
                            wait_alone(pe, S["passed"], S["n_y2"], g)
                            at2 = out_wide if weighted else 0
                            pe.matmul(nb_hid2[at2:at2 + out_wide, :], c.gcn_w[n + 1][:, :], n_y[s][0:out_wide, :],
                                      start=True, stop=True).then_inc(S["n_hid2"], 1)
                    g = live(i, 1)
                    if g is not None:
                        s = (u - 1) % 2
                        wait_alone(pe, S["passed"], S["agg"], g + 1)
                        wait_alone(pe, S["passed"], S["y"], g)
                        pe.matmul(b_product[out_at:out_at + out_wide, :], c.gcn_w[n][:, :], agg[s][0:wide, :],
                                  start=True, stop=True).then_inc(S["product"], 1)
                        if lane:
                            wait_alone(pe, S["passed"], S["n_xT"], g + 1)
                            wait_alone(pe, S["passed"], S["n_y1"], g)
                            pe.matmul(nb_hid[0:out_wide, :], c.gcn_w[n][:, :], n_xT[(u - 1) % 4][:, :],
                                      start=True, stop=True).then_inc(S["n_hid"], 1)
                    g = live(i, 4)
                    if g is not None and lane:
                        s = u % 2
                        wait_alone(pe, S["passed"], S["n_sum"], g + 1)
                        wait_alone(pe, S["passed"], S["n_sum_rows"], g)
                        transpose_tiles(pe, nb_sum, n_sum[s], c).then_inc(S["n_sum_turned"], 1)

                run_steps(pe, step, 4, 8, 4)

            @block.scalar
            def _(act):
                def step(i, u):
                    g = live(i, norm_lag + 1)
                    if g is not None:
                        s = (u - norm_lag - 1) % 2
                        act.wait_ge(S["spread"], g + 1)
                        act.activation(root[s][:, :], spread[s][:, :], ACT.Sqrt).then_inc(S["root"], 1)
                    g = live(i, 0)
                    if g is not None and lane:
                        s = u
                        act.wait_ge(S["n_turned"], g + 1)
                        wait_from(act, S["n_hid"], g - 3)
                        wait_from(act, S["n_sum"], g - 3)
                        act.copy(n_xT[s][:, :], nb_x[:, :]).then_inc(S["n_xT"], 1)
                    g = live(i, 3)
                    if g is not None and lane:
                        s = (u - 3) % 4
                        act.wait_ge(S["n_y1_turned"], g + 1)
                        if not isinstance(g, int) or g >= 4:
                            act.wait_ge(S["n_y1_out"][s], landed(g - 4, s, 4, 16))
                        act.copy(n_y1_rows[s][:, 0:TILES * out_wide], nb_y1[:, 0:TILES * out_wide]).then_inc(S["n_y1_rows"], 1)
                    g = live(i, norm_lag + 2)
                    if g is not None:
                        s = (u - norm_lag - 2) % 4
                        act.wait_ge(S["shift"], g + 1)
                        into, from_ = (rows[s], res[s]) if final else (n_new[s], n_sum_rows[s])
                        sent, each = ((S["scattered"], 16 * TILES) if to_output else
                                      (S["stored"] if final else S["n_out"], 16))
                        if not isinstance(g, int) or g >= 4:
                            act.wait_ge(sent[s], landed(g - 4, s, 4, each))
                        layernorm_apply(act, into, from_, ln[s % 2]).then_inc(S["normed"], 1)
                    g = live(i, 2)
                    if g is not None and lane:
                        s = (u - 2) % 4
                        act.wait_ge(S["n_hid2"], g + 1)
                        wait_from(act, S["n_sum"], g - 3)
                        at2 = out_wide if weighted else 0
                        into = n_y[s] if weighted else n_y2[s]
                        act.activation(into[at2:at2 + out_wide, :], nb_hid2[at2:at2 + out_wide, :], ACT.Relu,
                                       bias=c.gcn_b[n + 1][at2:at2 + out_wide, :]).then_inc(S["n_y2"], 1)
                    g = live(i, 1)
                    if g is not None:
                        s = (u - 1) % 4
                        act.wait_ge(S["product"], g + 1)
                        wait_from(act, S["y_turned"], g - 3)
                        act.activation(y[s][out_at:out_at + out_wide, :], b_product[out_at:out_at + out_wide, :], ACT.Relu,
                                       bias=c.gcn_b[n][out_at:out_at + out_wide, :]).then_inc(S["y"], 1)
                        if lane:
                            act.wait_ge(S["n_hid"], g + 1)
                            wait_from(act, S["n_hid2"], g - 3)
                            wait_from(act, S["n_y1_turned"], g - 3)
                            wait_from(act, S["n_sum"], g - 3)
                            act.activation(n_y[s][0:out_wide, :], nb_hid[0:out_wide, :], ACT.Relu,
                                           bias=c.gcn_b[n][0:out_wide, :]).then_inc(S["n_y1"], 1)
                    g = live(i, 4)
                    if g is not None and lane:
                        s = u
                        act.wait_ge(S["n_sum_turned"], g + 1)
                        wait_from(act, S["normed"], g - 3)
                        act.copy(n_sum_rows[s][:, :], nb_sum[:, :]).then_inc(S["n_sum_rows"], 1)

                run_steps(act, step, 4, 8, norm_lag + 2)

            @block.vector
            def _(dve):
                def step(i, u):
                    g = live(i, 1)
                    if g is not None:
                        s = (u - 1) % 2
                        m = (u - 1) % 4
                        begin = isinstance(g, int) and g == 0
                        dve.wait_ge(S["mask_in"][m], landed(g, m, 4, 16))
                        wait_alone(dve, S["passed"], S["turned"], g + 1)
                        wait_from(dve, S["product"], g - 1)
                        wait_from(dve, S["agg"], g)
                        dve.tensor_tensor_scan(agg[s][0:wide, flow], mask[m][0:wide, flow], b_agg[0:wide, flow],
                                               0.0 if begin else agg[1 - s][0:wide, entry],
                                               ALU.mult, ALU.add).then_inc(S["agg"], 1)
                    g = live(i, 0)
                    if g is not None:
                        s = u % 2
                        cols = bass.ds(at(g) * TILES, TILES)
                        wait_from(dve, S["summed"], g - 1)
                        wait_alone(dve, S["passed"], S["own_in"][u], landed(g, u, 4, 16))
                        dve.tensor_tensor(by_tile(own_scaled[s], wide), by_tile(own_rows[u], wide),
                                          over_features(self_norm[:, cols], wide), ALU.mult).then_inc(S["own_scaled"], 1)
                        dve.wait_ge(S["gathered"][u], landed(g, u, 4, 16 * TILES))
                        dve.tensor_tensor(by_tile(src_scaled[s], wide), by_tile(src_rows[u], wide),
                                          over_features(norm[:, cols], wide), ALU.mult).then_inc(S["src_scaled"], 1)
                    g = live(i, 0)
                    if g is not None:
                        s = u % 2
                        dve.wait_ge(S["src_scaled"], g + 1)
                        dve.wait_ge(S["own_scaled"], g + 1)
                        wait_from(dve, S["turned"], g - 1)
                        dve.tensor_tensor(summed[s][:, :], src_scaled[s][:, :], own_scaled[s][:, :], ALU.add)\
                           .then_inc(S["summed"], 1)
                    g = live(i, 1)
                    if g is not None and n == 1:
                        s = (u - 1) % 4
                        begin = isinstance(g, int) and g == 0
                        dve.wait_ge(S["own_turned"], g + 1)
                        wait_from(dve, S["y_turned"], g - 3)
                        wait_from(dve, S["own_done"], g)
                        dve.tensor_tensor_scan(y[s][0:wide, flow], mask[s][0:wide, flow], b_own[0:wide, flow],
                                               0.0 if begin else y[(s - 1) % 4][0:wide, entry],
                                               ALU.mult, ALU.add).then_inc(S["own_done"], 1)
                    g = live(i, 3)
                    if g is not None and final:
                        s = (u - 3) % 4
                        dve.wait_ge(S["res_in"][s], landed(g, s, 4, 16))
                        dve.wait_ge(S["y_turned"], g + 1)
                        wait_from(dve, S["normed"], g - 3)
                        dve.tensor_tensor(res[s][:, :], b_rows[:, :], res_rows[s][:, :], ALU.add).then_inc(S["residual"], 1)
                        dve.wait_ge(S["residual"], g + 1)
                    if g is not None and lane:
                        s = (u - 3) % 4
                        dve.wait_ge(S["y_turned"], g + 1)
                        if not isinstance(g, int) or g >= 4:
                            wait_alone(dve, S["passed"], S["stored"][s], landed(g - 4, s, 4, 16))
                        dve.tensor_tensor(by_tile(rows[s], row_wide), by_tile(b_rows, row_wide),
                                          over_features(place_mask[:, bass.ds(at(g) * TILES, TILES)], row_wide),
                                          ALU.mult).then_inc(S["rows"], 1)
                        dve.wait_ge(S["n_y2"], g + 1)
                        wait_from(dve, S["n_sum_turned"], g - 1)
                        dve.tensor_tensor(n_sum[s % 2][:, :], (n_y[s] if weighted else n_y2[s])[:, :], n_xT[s][:, :],
                                          ALU.add).then_inc(S["n_sum"], 1)
                    g = live(i, norm_lag)
                    if g is not None:
                        s = (u - norm_lag) % 4
                        if lane:
                            dve.wait_ge(S["n_sum_rows"], g + 1)
                        wait_from(dve, S["root"], g - 1)
                        layernorm_stats(dve, S, S["stats"], S["moments"], g, (res if final else n_sum_rows)[s], ln[s % 2],
                                        spread[s % 2][:, :]).then_inc(S["spread"], 1)
                    g = live(i, norm_lag + 1)
                    if g is not None:
                        s = (u - norm_lag - 1) % 2
                        dve.wait_ge(S["root"], g + 1)
                        wait_from(dve, S["normed"], g - 1)
                        dve.reciprocal(plain[s][:, :], root[s][:, :]).then_inc(S["plain"], 1)
                        wait_alone(dve, S["passed"], S["plain"], g + 1)
                        mask_ = place_mask[:, bass.ds(at(g) * TILES, TILES)] if final else None
                        layernorm_factors(dve, S["scale"], S["shift"], g, plain[s][:, :], mask_, ln[s])

                run_steps(dve, step, 4, 8, norm_lag + 1)


def attention_pass(nc, a, c, e, r, bank, table, out_table):
    flow = slice(None, None, -1)
    same = r.same_next

    def at(g):
        return GROUPS - 1 - g

    with ExitStack() as ctx:
        S = named_semaphores(nc, ctx, "att", "staged turned src_done own_done q_ready k_ready q_done prod scores v_ready "
                             "highest carried before shrink_log weight_log shrink weight weighted den num "
                             "heads skipped own_back rden part logit z tanh gate skip_bias rst diff gated mixed "
                             "own_copied stats1 moments1 scale1 shift1 normed scaled_gamma affine negative prelu_done residual "
                             "stats2 moments2 scale2 shift2 x2_rows spread root filled",
                             "stored", "gathered own_in mask_in cut_in")

        def sb(name, shape, dt=F32, slots=2):
            return [ctx.enter_context(nc.sbuf_tensor(f"att_{name}{s}", shape, dt)) for s in range(slots)]

        src_rows, own_rows, x1_rows = (sb(m, [P, GROUP], slots=4) for m in ("src_rows", "own_rows", "x1_rows"))
        mask, cut = sb("mask", [P, GROUP], BF16, 4), sb("cut", [P, GROUP], BF16, 4)
        at_src = sb("at_src", [P, TILES], I32, 4)
        (srcT, ownT, q, prod, before, shrink_log, weight_log, shrink, weight, weighted, den, num,
         skip, rst, diff, gated, mixed, normed, gam, aff, neg, pre, res, x2_rows) = (
            sb(m, [P, GROUP]) for m in
            "srcT ownT q prod before shrink_log weight_log shrink weight weighted den num "
            "skip rst diff gated mixed normed gam aff neg pre res x2_rows".split())
        highest = sb("highest", [P, GROUP + 1])
        rden, part = sb("rden", [P, TILES, HEADS]), sb("part", [P, TILES, HEADS])
        logit, z, th, gate = (sb(m, [P, TILES]) for m in ("logit", "z", "th", "gate"))
        spread, root = sb("spread", [P, 2, TILES]), sb("root", [P, 2, TILES])
        power = ctx.enter_context(nc.sbuf_tensor("att_power", [P, 2, TILES], F32))

        def one(name, shape):
            return ctx.enter_context(nc.sbuf_tensor(f"att_{name}", shape, F32))

        ln1, ln2 = layernorm_buffers(one, "ln1"), layernorm_buffers(one, "ln2")
        b_own, b_src, b_qv, b_k, b_scores, b_heads, b_skip, b_num = bank
        b_x1 = b_k
        heads = b_heads[:, 0:TILES * 9].rearrange("p (j c) -> p j c", j=TILES)

        with nc.Block() as block:
            @block.sync
            def _(sp):
                def step(i, u):
                    g = live(i, 0)
                    if g is not None:
                        s = u
                        wait_alone(sp, S["passed"], S["turned"], g - 3)
                        sp.dma_start(tiles(own_rows[s][:, :]), group_rows(table, 0, at(g))).then_inc(S["own_in"][s], 16)
                        wait_alone(sp, S["passed"], S["own_done"], g - 3)
                        sp.dma_start(mask[s][:, :], same[bass.ds(at(g) * GROUP, GROUP)].rearrange("(o n) -> o n", o=1)
                                     .to_broadcast([P, GROUP])).then_inc(S["mask_in"][s], 16)
                        wait_alone(sp, S["passed"], S["before"], g - 3)
                        sp.dma_start(cut[s][:, :], r.cut_next[bass.ds(at(g) * GROUP, GROUP)].rearrange("(o n) -> o n", o=1)
                                     .to_broadcast([P, GROUP])).then_inc(S["cut_in"][s], 16)
                    g = live(i, 5)
                    if g is not None:
                        s = (u - 5) % 2
                        wait_alone(sp, S["passed"], S["x2_rows"], g + 1)
                        sp.dma_start(group_rows(out_table, 0, at(g)), tiles(x2_rows[s][:, :])).then_inc(S["stored"][s], 16)

                run_steps(sp, step, 4, 12, 5)
                for s in range(2):
                    sp.wait_ge(S["stored"][s], 16 * (GROUPS // 2))

            @block.gpsimd
            def _(pool):
                pool.memset(power[:, :, :], -0.5)
                for s in range(2):
                    pool.memset(spread[s][:, :, :], 1.0)
                pool.memset(highest[0][:, GROUP:GROUP + 1], FAR).then_inc(S["filled"], 1)
                pool.wait_ge(S["filled"], 1)

                def gather(g, s):
                    wait_alone(pool, S["passed"], S["turned"], g - 3)
                    pool.tensor_copy(at_src[s][:, :], e.src_at_end[:, bass.ds(at(g) * TILES, TILES)]).then_inc(S["staged"], 1)
                    wait_alone(pool, S["passed"], S["staged"], g + 1)
                    for j in range(TILES):
                        pool.indirect_dma_start(src_rows[s][:, j * D:(j + 1) * D], None, table[:, :],
                                                bass.IndirectOffsetOnAxis(ap=at_src[s][:, j:j + 1], axis=0))\
                            .then_inc(S["gathered"][s], 16)

                def step(i, u):
                    g = live(i, 0)
                    if g is not None:
                        gather(g, u)
                    if not isinstance(i, int) or i >= 2:
                        wait_alone(pool, S["passed"], S["spread"], i - 1)
                        pool.tensor_tensor(root[u % 2][:, :, :], spread[u % 2][:, :, :], power[:, :, :], ALU.pow)\
                            .then_inc(S["root"], 1)
                    g = live(i, 4)
                    if g is not None:
                        s = u % 2
                        affine(pool, S, c, g, normed[s], gam[s], aff[s])

                run_steps(pool, step, 4, 8, 5)

            @block.tensor
            def _(pe):
                def step(i, u):
                    g = live(i, 0)
                    if g is not None:
                        s = u
                        pe.wait_ge(S["gathered"][s], landed(g, s, 4, 16 * TILES))
                        pe.wait_ge(S["own_in"][s], landed(g, s, 4, 16))
                        wait_from(pe, S["src_done"], g)
                        wait_from(pe, S["own_done"], g)
                        transpose_tiles(pe, b_src, src_rows[s], c)
                        transpose_tiles(pe, b_own, own_rows[s], c).then_inc(S["turned"], 1)
                    g = live(i, 1)
                    if g is not None:
                        s = (u - 1) % 2
                        pe.wait_ge(S["num"], g + 1)
                        wait_from(pe, S["z"], g)
                        for j in range(TILES):
                            cols = slice(j * P, (j + 1) * P)
                            pe.matmul(heads[:, j, 0:4], den[s][:, cols], c.head_pick[:, :], start=True, stop=True)
                            pe.matmul(heads[:, j, 4:8], num[s][:, cols], c.gate_heads[:, :], start=True, stop=True)
                            last = pe.matmul(heads[:, j, 8:9], ownT[s][:, cols], c.gate_own[:, :], start=True, stop=True)
                        last.then_inc(S["heads"], 1)
                        wait_from(pe, S["skip_bias"], g)
                        wait_from(pe, S["rst"], g)
                        for j in range(TILES):
                            cols = slice(j * P, (j + 1) * P)
                            pe.matmul(b_skip[:, cols], ownT[s][:, cols], c.wskip[:, :], start=True, stop=True)
                        transpose_tiles(pe, b_num, num[s], c).then_inc(S["skipped"], 1)
                    g = live(i, 0)
                    if g is not None:
                        s = u % 2
                        pe.wait_ge(S["src_done"], g + 1)
                        wait_from(pe, S["weighted"], g)
                        wait_from(pe, S["own_copied"], g - 1)
                        pe.matmul(b_qv[:, :], c.wq[:, :], srcT[s][:, :], start=True, stop=True).then_inc(S["q_ready"], 1)
                        pe.wait_ge(S["own_done"], g + 1)
                        pe.matmul(b_k[:, :], c.wk[:, :], ownT[s][:, :], start=True, stop=True).then_inc(S["k_ready"], 1)
                        pe.wait_ge(S["q_done"], g + 1)
                        pe.matmul(b_qv[:, :], c.wv[:, :], srcT[s][:, :], start=True, stop=True).then_inc(S["v_ready"], 1)
                        pe.wait_ge(S["prod"], g + 1)
                        wait_from(pe, S["weight_log"], g)
                        pe.matmul(b_scores[:, :], c.head_sum[:, :], prod[s][:, :], start=True, stop=True).then_inc(S["scores"], 1)
                    g = live(i, 1)
                    if g is not None:
                        s = (u - 1) % 2
                        wait_from(pe, S["own_copied"], g)
                        transpose_tiles(pe, b_x1, ownT[s], c).then_inc(S["own_back"], 1)

                run_steps(pe, step, 4, 8, 1)

            @block.scalar
            def _(act):
                def step(i, u):
                    g = live(i, 0)
                    if g is not None:
                        s = u % 2
                        act.wait_ge(S["turned"], g + 1)
                        wait_from(act, S["v_ready"], g - 1)
                        act.copy(srcT[s][:, :], b_src[:, :]).then_inc(S["src_done"], 1)
                    g = live(i, 4)
                    if g is not None:
                        s = u % 2
                        act.wait_ge(S["shift2"], g + 1)
                        if not isinstance(g, int) or g >= 2:
                            act.wait_ge(S["stored"][s], landed(g - 2, s, 2, 16))
                        layernorm_apply(act, x2_rows[s], res[s], ln2[s]).then_inc(S["x2_rows"], 1)
                    g = live(i, 2)
                    if g is not None:
                        s = u % 2
                        act.wait_ge(S["shift1"], g + 1)
                        wait_from(act, S["scaled_gamma"], g - 1)
                        layernorm_apply(act, normed[s], mixed[s], ln1[s]).then_inc(S["normed"], 1)
                    g = live(i, 0)
                    if g is not None:
                        s = u % 2
                        act.wait_ge(S["q_ready"], g + 1)
                        wait_from(act, S["prod"], g - 1)
                        act.activation(q[s][:, :], b_qv[:, :], ACT.Identity, bias=c.bq[:, :]).then_inc(S["q_done"], 1)
                    g = live(i, 1)
                    if g is not None:
                        s = (u - 1) % 2
                        act.wait_ge(S["z"], g + 1)
                        wait_from(act, S["gate"], g - 1)
                        act.activation(th[s][:, :], z[s][:, :], ACT.Tanh, bias=c.gate_bias[:, :], scale=0.5)\
                           .then_inc(S["tanh"], 1)
                    g = live(i, 0)
                    if g is not None:
                        s = u % 2
                        act.wait_ge(S["shrink_log"], g + 1)
                        wait_from(act, S["num"], g - 1)
                        act.activation(shrink[s][:, :], shrink_log[s][:, :], ACT.Exp).then_inc(S["shrink"], 1)
                        act.wait_ge(S["weight_log"], g + 1)
                        act.activation(weight[s][:, :], weight_log[s][:, :], ACT.Exp).then_inc(S["weight"], 1)
                    g = live(i, 1)
                    if g is not None:
                        s = (u - 1) % 4
                        act.wait_ge(S["own_back"], g + 1)
                        wait_from(act, S["residual"], g - 3)
                        act.copy(x1_rows[s][:, :], b_x1[:, :]).then_inc(S["own_copied"], 1)

                run_steps(act, step, 4, 8, 4)

            @block.vector
            def _(dve):
                def step(i, u):
                    g = live(i, 0)
                    if g is not None:
                        s = u % 2
                        dve.wait_ge(S["mask_in"][u], landed(g, u, 4, 16))
                        dve.wait_ge(S["turned"], g + 1)
                        wait_from(dve, S["own_back"], g - 1)
                        wait_from(dve, S["own_done"], g)
                        begin = isinstance(g, int) and g == 0
                        dve.tensor_tensor_scan(ownT[s][:, flow], mask[u][:, flow], b_own[:, flow],
                                               0.0 if begin else ownT[1 - s][:, 0:1], ALU.mult, ALU.add)\
                           .then_inc(S["own_done"], 1)
                    if not isinstance(i, int) or i >= 1:
                        wait_alone(dve, S["passed"], S["root"], i)
                    for lag, scale_done, shift_done, read, n, ln in ((4, S["scale2"], S["shift2"], S["x2_rows"], 1, ln2),
                                                                     (2, S["scale1"], S["shift1"], S["normed"], 0, ln1)):
                        g = live(i, lag)
                        if g is not None:
                            s = u % 2
                            wait_alone(dve, S["passed"], read, g - 1)
                            mask_ = e.is_start[:, bass.ds(at(g) * TILES, TILES)] if n else None
                            layernorm_factors(dve, scale_done, shift_done, g, root[(u - 1) % 2][:, n, :], mask_, ln[s])
                    g = live(i, 1)
                    if g is not None:
                        s = (u - 1) % 2
                        dve.wait_ge(S["heads"], g + 1)
                        dve.reciprocal(rden[s][:, :, :], heads[:, :, 0:4]).then_inc(S["rden"], 1)
                        dve.wait_ge(S["rden"], g + 1)
                        dve.tensor_tensor(part[s][:, :, :], heads[:, :, 4:8], rden[s][:, :, :], ALU.mult).then_inc(S["part"], 1)
                        dve.wait_ge(S["part"], g + 1)
                        dve.tensor_reduce(logit[s][:, :], part[s][:, :, :], axis=AX.X, op=ALU.add).then_inc(S["logit"], 1)
                        dve.wait_ge(S["logit"], g + 1)
                        wait_from(dve, S["tanh"], g - 1)
                        dve.tensor_tensor(z[s][:, :], logit[s][:, :], heads[:, :, 8], ALU.add).then_inc(S["z"], 1)
                    g = live(i, 0)
                    if g is not None:
                        s = u % 2
                        dve.wait_ge(S["k_ready"], g + 1)
                        dve.wait_ge(S["q_done"], g + 1)
                        wait_from(dve, S["scores"], g - 1)
                        dve.scalar_tensor_tensor(prod[s][:, :], b_k[:, :], c.bk[:, :], q[s][:, :], ALU.add, ALU.mult)\
                           .then_inc(S["prod"], 1)
                    here = spread[u % 2]
                    last = None
                    g = live(i, 3)
                    if g is not None:
                        s = (u - 3) % 2
                        last = prelu_residual(dve, S, c, g, aff[s], neg[s], pre[s], x1_rows[(u - 3) % 4][:, :], res[s],
                                              S["x2_rows"], ln2[s], here[:, 1, :])
                    g = live(i, 0)
                    if g is not None:
                        s = u % 2
                        begin = isinstance(g, int) and g == 0
                        dve.wait_ge(S["cut_in"][u], landed(g, u, 4, 16))
                        dve.wait_ge(S["scores"], g + 1)
                        if begin:
                            dve.wait_ge(S["filled"], 1)
                        else:
                            dve.wait_ge(S["highest"], g)
                            dve.tensor_copy(highest[s][:, GROUP:GROUP + 1], highest[1 - s][:, 0:1])
                        dve.tensor_tensor_scan(highest[s][:, 0:GROUP][:, flow], cut[u][:, flow], b_scores[:, flow],
                                               FAR if begin else highest[1 - s][:, 0:1], ALU.add, ALU.max)\
                           .then_inc(S["highest"], 1)
                        dve.wait_ge(S["highest"], g + 1)
                        wait_from(dve, S["shrink"], g - 1)
                        dve.tensor_tensor(before[s][:, :], highest[s][:, 1:GROUP + 1], cut[u][:, :], ALU.add)\
                           .then_inc(S["before"], 1)
                        wait_from(dve, S["weight"], g - 1)
                        dve.tensor_tensor(weight_log[s][:, :], b_scores[:, :], highest[s][:, 0:GROUP], ALU.subtract)\
                           .then_inc(S["weight_log"], 1)
                        dve.wait_ge(S["before"], g + 1)
                        dve.tensor_tensor(shrink_log[s][:, :], before[s][:, :], highest[s][:, 0:GROUP], ALU.subtract)\
                           .then_inc(S["shrink_log"], 1)
                    g = live(i, 1)
                    if g is not None:
                        s = (u - 1) % 2
                        dve.wait_ge(S["skipped"], g + 1)
                        dve.tensor_tensor(tiles(skip[s][:, :]), tiles(b_skip[:, :]),
                                          c.bskip_row[:, :].unsqueeze(1).to_broadcast([P, TILES, D]), ALU.add)\
                           .then_inc(S["skip_bias"], 1)
                        dve.tensor_tensor(rst[s][:, :].rearrange("p (h f) -> p h f", f=HEAD),
                                          b_num[:, :].rearrange("p (h f) -> p h f", f=HEAD),
                                          rden[s][:, :, :].rearrange("p j h -> p (j h)").unsqueeze(2)
                                          .to_broadcast([P, TILES * HEADS, HEAD]), ALU.mult).then_inc(S["rst"], 1)
                        dve.wait_ge(S["rst"], g + 1)
                        dve.tensor_tensor(diff[s][:, :], skip[s][:, :], rst[s][:, :], ALU.subtract).then_inc(S["diff"], 1)
                        dve.wait_ge(S["tanh"], g + 1)
                        dve.tensor_scalar(gate[s][:, :], th[s][:, :], 0.5, 0.5, ALU.mult, ALU.add).then_inc(S["gate"], 1)
                        dve.wait_ge(S["gate"], g + 1)
                        dve.tensor_tensor(tiles(gated[s][:, :]), tiles(diff[s][:, :]), over_features(gate[s][:, :], D),
                                          ALU.mult).then_inc(S["gated"], 1)
                        dve.wait_ge(S["gated"], g + 1)
                        wait_from(dve, S["normed"], g - 1)
                        dve.tensor_tensor(mixed[s][:, :], gated[s][:, :], rst[s][:, :], ALU.add).then_inc(S["mixed"], 1)
                        dve.wait_ge(S["mixed"], g + 1)
                        last = layernorm_stats(dve, S, S["stats1"], S["moments1"], g, mixed[s], ln1[s], here[:, 0, :])
                    if last is None:
                        last = dve.memset(here[:, 0, :], 1.0)
                    last.then_inc(S["spread"], 1)
                    g = live(i, 0)
                    if g is not None:
                        s = u % 2
                        begin = isinstance(g, int) and g == 0
                        dve.wait_ge(S["weight"], g + 1)
                        dve.wait_ge(S["v_ready"], g + 1)
                        dve.scalar_tensor_tensor(weighted[s][:, :], b_qv[:, :], c.bv[:, :], weight[s][:, :],
                                                 ALU.add, ALU.mult).then_inc(S["weighted"], 1)
                        dve.wait_ge(S["shrink"], g + 1)
                        wait_from(dve, S["num"], g)
                        wait_from(dve, S["skipped"], g - 1)
                        dve.tensor_tensor_scan(den[s][:, flow], shrink[s][:, flow], weight[s][:, flow],
                                               0.0 if begin else den[1 - s][:, 0:1], ALU.mult, ALU.add)
                        dve.wait_ge(S["weighted"], g + 1)
                        dve.tensor_tensor_scan(num[s][:, flow], shrink[s][:, flow], weighted[s][:, flow],
                                               0.0 if begin else num[1 - s][:, 0:1], ALU.mult, ALU.add)\
                           .then_inc(S["num"], 1)

                run_steps(dve, step, 4, 8, 4)


def kernel(**inputs):
    import numpy as np
    import concourse.bacc as bacc
    from concourse.bass_utils import run_bass_kernel_spmd

    nc = bacc.Bacc("TRN2", target_bir_lowering=False, num_devices=1)
    arrays, aps = {}, {}

    def give(name, value):
        value = np.ascontiguousarray(value)
        arrays[name] = value
        aps[name] = nc.dram_tensor(name, value.shape, mybir.dt.from_np(value.dtype), kind="ExternalInput").ap()

    def padded(array, before, after, fill):
        array = np.asarray(array)
        return np.concatenate([np.full(before, fill[0], array.dtype), array, np.full(ROWS - N, fill[1], array.dtype),
                               np.full(after, fill[2], array.dtype)])

    def in_tiles(line):
        return line.reshape(COLS, P).T

    x = np.asarray(inputs["x"])
    give("x", np.concatenate([x, np.zeros((ROWS - N, D), x.dtype)]))
    dst = padded(inputs["dst"], 1, 1, (-1, N, -1))
    weight = padded(inputs["edge_weight"], 0, 0, (0, 0, 0))
    give("dst_line", dst)
    give("weight_line", weight)
    give("src_tiles", in_tiles(padded(inputs["src"], 0, 0, (0, 0, 0))))
    give("prev_tiles", in_tiles(dst[0:ROWS]))
    give("dst_tiles", in_tiles(dst[1:1 + ROWS]))
    give("next_tiles", in_tiles(dst[2:2 + ROWS]))
    give("weight_tiles", in_tiles(weight))
    for name, value in inputs.items():
        if name.startswith("L"):
            value = np.asarray(value)
            give(name, value.reshape(1) if value.ndim == 0 else value)
    out = nc.dram_tensor("out", (ROWS, D), F32, kind="ExternalOutput").ap()
    build(nc, aps, out)
    got = run_bass_kernel_spmd(nc, [arrays], core_ids=[0])
    return got.results[0]["out"][:N]
```

```python
from contextlib import ExitStack

import concourse.bass as bass
from concourse import mybir

F32 = mybir.dt.float32
I32 = mybir.dt.int32
BF16 = mybir.dt.bfloat16
ALU = mybir.AluOpType
ACT = mybir.ActivationFunctionType
AX = mybir.AxisListType

N = 50000
P = 128
D = 128
GROUP = 512
TILES = GROUP // P
GROUPS = 98
ROWS = GROUPS * GROUP
COLS = ROWS // P
NODE_BATCH = 7
CONV_TILES = COLS - (GROUPS - COLS // NODE_BATCH) * NODE_BATCH
H0 = 256
HALVES = H0 // P
LAYERS = 3
HEADS, HEAD = 4, 32
HID2 = 64
NODE0 = ROWS
NOWHERE = 4 * ROWS
FAR = -1.0e30
EPS = 1e-5


class Named:
    pass


def wait_from(eng, sem, count):
    if not isinstance(count, int) or count > 0:
        eng.wait_ge(sem, count)


def wait_alone(eng, passed, sem, count):
    wait_from(eng, sem, count)
    if not isinstance(count, int):
        eng.sem_inc(passed, 1)


def landed(g, s, slots, each):
    return (g - s) * (each // slots) + each


def groups_of_slot(s, slots=4):
    return (GROUPS - s + slots - 1) // slots


def run_steps(eng, step, slots, peeled, tail):
    for i in range(peeled):
        step(i, i % slots)
    with eng.Fori(peeled // slots, GROUPS // slots) as k:
        for s in range(slots):
            step(slots * k + s, s)
    for i in range(GROUPS - GROUPS % slots, GROUPS + tail):
        step(i, i % slots)


def live(i, lag):
    if isinstance(i, int) and not 0 <= i - lag < GROUPS:
        return None
    return i - lag


def group_rows(table, first_row, g):
    return table[bass.ds(first_row + g * GROUP, GROUP), :].rearrange("(j p) f -> p j f", p=P)


def tiles(ap):
    return ap.rearrange("p (j f) -> p j f", j=TILES)


def over_features(ap, width):
    return ap.unsqueeze(2).to_broadcast([P, TILES, width])


def build(nc, a, out):
    with ExitStack() as ctx:
        def sb(name, shape, dt=F32):
            return ctx.enter_context(nc.sbuf_tensor(name, shape, dt))

        def dram(name, shape, dt=F32):
            return nc.dram_tensor(name, shape, dt, kind="Internal").ap()

        c = Named()
        c.ident = sb("ident", [P, P])
        c.all_w_own = sb("w_own", [P, LAYERS, H0])
        c.all_w_src = sb("w_src", [P, LAYERS, H0])
        c.all_phi_w2 = sb("phi_w2", [P, LAYERS * HALVES, D])
        c.all_psi_w1 = sb("psi_w1", [P, LAYERS, H0])
        c.all_psi_w2 = sb("psi_w2", [P, LAYERS * HALVES, D])
        c.w_own, c.w_src, c.psi_w1 = ([w[:, l, :] for l in range(LAYERS)] for w in (c.all_w_own, c.all_w_src, c.all_psi_w1))
        c.phi_w2, c.psi_w2 = ([w[:, l * HALVES:(l + 1) * HALVES, :] for l in range(LAYERS)]
                              for w in (c.all_phi_w2, c.all_psi_w2))
        c.phi_b1 = sb("phi_b1", [P, LAYERS, HALVES])
        c.phi_b2 = sb("phi_b2", [P, LAYERS])
        c.psi_b1 = sb("psi_b1", [P, LAYERS, HALVES])
        c.psi_b1_mean = sb("psi_b1_mean", [P, LAYERS, HALVES])
        c.psi_b2 = sb("psi_b2", [P, LAYERS])
        c.hid_empty = sb("hid_empty", [P, LAYERS, HALVES])
        c.empty = sb("empty", [P, LAYERS])
        c.empty_relu = sb("empty_relu", [P, LAYERS])
        c.empty_row = sb("empty_row", [P, D])
        c.proj_w = sb("proj_w", [P, D])
        c.proj_b = sb("proj_b", [P, 1])
        c.h1_bias = sb("h1_bias", [P, 1])
        c.h2_bias = sb("h2_bias", [P, 1])
        c.wq, c.wk, c.wv, c.wskip = (sb(n, [P, D]) for n in ("wq", "wk", "wv", "wskip"))
        c.bq, c.bk, c.bv, c.bskip = (sb(n, [P, 1]) for n in ("bq", "bk", "bv", "bskip"))
        c.bskip_row = sb("bskip_row", [P, D])
        c.gate3 = sb("gate3", [P, 3])
        c.gate_skip = sb("gate_skip", [P, 1])
        c.gate_rst = sb("gate_rst", [P, 1])
        c.head_sum = sb("head_sum", [P, D])
        c.head_pick = sb("head_pick", [P, HEADS])
        c.gate_heads = sb("gate_heads", [P, HEADS])
        c.wskip_t = sb("wskip_t", [P, D])
        c.gate_own = sb("gate_own", [P, 1])
        c.gate_bias = sb("gate_bias", [P, 1])
        c.bgate = sb("bgate", [P, 1])
        c.gamma_row, c.beta_row = sb("gamma_row", [P, D]), sb("beta_row", [P, D])
        c.prelu = sb("prelu", [P, 1])
        c.minus_prelu = sb("minus_prelu", [P, 1])
        c.ones = sb("ones", [P, P])
        c.gcn_w = [sb(f"gcn_w{n}", s) for n, s in enumerate(([P, HID2], [HID2, HID2], [P, D], [P, D]))]
        c.gcn_b = [sb(f"gcn_b{n}", [P, 1]) for n in range(4)]

        e = Named()
        e.place = sb("e_place", [P, COLS, 4])
        e.place_row = sb("e_place_row", [P, COLS], I32)
        e.fetched = sb("e_fetched", [P, COLS, 4])
        e.src, e.dst, e.src_at_end, e.src_at_start, e.out_row = (
            sb(f"e_{n}", [P, COLS], I32) for n in ("src", "dst", "src_at_end", "src_at_start", "out_row"))
        e.norm2, e.norm3, e.self2, e.self3, e.is_end, e.is_start = (
            sb(f"e_{n}", [P, COLS]) for n in ("norm2", "norm3", "self2", "self3", "is_end", "is_start"))

        r = Named()
        r.same_prev, r.same_next, r.cut_next = (dram(n, [ROWS], BF16) for n in ("same_prev", "same_next", "cut_next"))
        r.inv_count, r.dinv2, r.dinv3 = (dram(n, [ROWS]) for n in ("inv_count", "dinv2", "dinv3"))
        t = Named()
        t.h1, t.h2, t.x1, t.x2, t.x3, t.z1 = (dram(f"t_{n}", [2 * ROWS, D]) for n in ("h1", "h2", "x1", "x2", "x3", "z1"))
        t.y1 = dram("t_y1", [2 * ROWS, HID2])
        t.place = dram("t_place", [ROWS, 4])
        bank = [ctx.enter_context(nc.psum_tensor(f"bank{n}", [P, GROUP], F32)) for n in range(8)]

        constants(nc, a, c, bank)
        segments(nc, a, c, e, r, t, bank)
        edge_masks(nc, a, e)
        node_space(nc, a, c, e, t, bank)
        conv_pass(nc, a, c, e, r, t, bank, 0, a["x"], a["x"], e.src, False, t.h1, e.is_end)
        edge_scalars(nc, a, c, e, r, bank)
        conv_pass(nc, a, c, e, r, t, bank, 1, t.h1, t.h1, e.src_at_end, True, t.h2, e.is_start)
        conv_pass(nc, a, c, e, r, t, bank, 2, t.h2, t.h2, e.src_at_start, False, t.x1, e.is_end)
        attention_pass(nc, c, e, r, bank, t.x1, t.x2)
        gcn_pass(nc, c, e, r, bank, 0, t.x2, e.src_at_start, False, t.y1, None, t.x3)
        gcn_pass(nc, c, e, r, bank, 1, t.y1, e.src_at_end, True, t.x3, t.x2, None)
        gcn_pass(nc, c, e, r, bank, 2, t.x3, e.src_at_start, False, t.z1, None, out)
        gcn_pass(nc, c, e, r, bank, 3, t.z1, e.src_at_end, True, out, t.x3, None)


def named_semaphores(nc, ctx, stage, names, slots="", four_slots=""):
    taken = []

    def take(name):
        taken.append(nc.alloc_semaphore(f"{stage}_{name}"))
        return taken[-1]

    def give_back():
        nc.clear_and_free_semaphores(taken)
        nc.all_engine_barrier()

    found = {n: take(n) for n in ["passed", *names.split()]}
    for count, some in ((2, slots), (4, four_slots)):
        for n in some.split():
            found[n] = [take(f"{n}{s}") for s in range(count)]
    ctx.callback(give_back)
    return found


def constants(nc, a, c, bank):
    with ExitStack() as ctx:
        S = named_semaphores(nc, ctx, "const", "loaded filled picked on_dve on_pe on_act")
        w_far = ctx.enter_context(nc.sbuf_tensor("w_far", [P, LAYERS, H0], F32))
        hid_wide = ctx.enter_context(nc.sbuf_tensor("hid_wide", [P, HALVES, P], F32))
        psi_b2_row = ctx.enter_context(nc.sbuf_tensor("psi_b2_row", [P, D], F32))
        loads = []

        def column(ap, dst):
            loads.append((dst, ap.rearrange("(p o) -> p o", o=1)))

        def on_all(ap, dst, width):
            loads.append((dst, ap.rearrange("(o n) -> o n", o=1).to_broadcast([P, width])))

        for first_row, w in ((0, w_far), (D, c.all_w_src)):
            loads.append((w[:, :, :], a["L0_gnn_phi_w1"][:, first_row:first_row + D, :].rearrange("l p n -> p l n")))
        loads.append((c.all_psi_w1[:, :, :], a["L0_gnn_psi_w1"].rearrange("l p n -> p l n")))
        for net, w2, b1, b2 in (("phi", c.all_phi_w2, c.phi_b1, c.phi_b2), ("psi", c.all_psi_w2, c.psi_b1, c.psi_b2)):
            loads.append((w2[:, :, :], a[f"L0_gnn_{net}_w2"].rearrange("l (k p) n -> p (l k) n", p=P)))
            for l in range(LAYERS):
                for h in range(HALVES):
                    column(a[f"L0_gnn_{net}_b1"][l, h * P:(h + 1) * P], b1[:, l, h:h + 1])
                column(a[f"L0_gnn_{net}_b2"][l], b2[:, l:l + 1])
        on_all(a["L0_gnn_psi_b2"][LAYERS - 1], psi_b2_row[:, :], D)
        loads.append((c.proj_w[:, :], a["L0_gnn_proj_w"]))
        column(a["L0_gnn_proj_b"], c.proj_b[:, :])
        for n, w, b in (("q", c.wq, c.bq), ("k", c.wk, c.bk), ("v", c.wv, c.bv), ("skip", c.wskip, c.bskip)):
            loads.append((w[:, :], a[f"L1_gnn_W{n}"]))
            column(a[f"L1_gnn_b{n}"], b[:, :])
        on_all(a["L1_gnn_bskip"], c.bskip_row[:, :], D)
        for n in range(3):
            loads.append((c.gate3[:, n:n + 1], a["L1_gnn_Wgate"][n * D:(n + 1) * D, :]))
        on_all(a["L1_gnn_bgate"], c.bgate[:, :], 1)
        on_all(a["L1_gnn_gamma"], c.gamma_row[:, :], D)
        on_all(a["L1_gnn_beta"], c.beta_row[:, :], D)
        on_all(a["L1_gnn_prelu_a"], c.prelu[:, :], 1)
        for n, (w, b) in enumerate((("L2_gnn_W1", "L2_gnn_b1"), ("L2_gnn_W2", "L2_gnn_b2"),
                                    ("L3_gnn_W1", "L3_gnn_b1"), ("L3_gnn_W2", "L3_gnn_b2"))):
            loads.append((c.gcn_w[n][:, :], a[w]))
            at = HID2 if n == 1 else 0
            width = HID2 if n < 2 else D
            column(a[b], c.gcn_b[n][at:at + width, :])

        with nc.Block() as block:
            @block.sync
            def _(sp):
                for dst, src in loads[::2]:
                    sp.dma_start(dst, src).then_inc(S["loaded"], 16)
                sp.wait_ge(S["loaded"], 16 * len(loads))

            @block.scalar
            def _(act):
                for dst, src in loads[1::2]:
                    act.dma_start(dst, src).then_inc(S["loaded"], 16)
                act.wait_ge(S["loaded"], 16 * len(loads))
                act.activation(c.hid_empty[:, :, :], c.psi_b1[:, :, :], ACT.Relu).then_inc(S["on_act"], 1)

            @block.gpsimd
            def _(pool):
                pool.memset(c.ident[:, :], 0.0)
                pool.memset(c.ones[:, :], 1.0)
                pool.memset(c.head_sum[:, :], 0.0)
                pool.memset(c.head_pick[:, :], 0.0)
                pool.memset(c.gate_heads[:, :], 0.0).then_inc(S["filled"], 1)
                pool.wait_ge(S["filled"], 1)
                pool.affine_select(out=c.ident[:, :], in_=c.ident[:, :], compare_op=ALU.not_equal, fill=1.0,
                                   base=0, pattern=[[-1, P]], channel_multiplier=1)
                pool.memset(c.gate_bias[:, :], 0.0).then_inc(S["picked"], 1)

            @block.vector
            def _(dve):
                dve.wait_ge(S["loaded"], 16 * len(loads))
                dve.wait_ge(S["picked"], 1)
                for h in range(HEADS):
                    at = slice(h * HEAD, (h + 1) * HEAD)
                    dve.memset(c.head_sum[at, at], float(HEAD) ** -0.5)
                    dve.memset(c.head_pick[h * HEAD:h * HEAD + 1, h:h + 1], 1.0)
                dve.tensor_tensor(c.all_w_own[:, :, :], w_far[:, :, :], c.all_w_src[:, :, :], ALU.subtract)
                dve.tensor_tensor(c.gate_skip[:, :], c.gate3[:, 0:1], c.gate3[:, 2:3], ALU.add)
                dve.tensor_tensor(c.gate_rst[:, :], c.gate3[:, 1:2], c.gate3[:, 2:3], ALU.subtract).then_inc(S["on_dve"], 1)
                dve.wait_ge(S["on_dve"], 1)
                for h in range(HEADS):
                    at = slice(h * HEAD, (h + 1) * HEAD)
                    dve.tensor_copy(c.gate_heads[at, h:h + 1], c.gate_rst[at, :])
                dve.wait_ge(S["on_pe"], 1)
                dve.tensor_copy(c.wskip_t[:, :], bank[0][:, 0:D]).then_inc(S["on_dve"], 1)
                dve.wait_ge(S["on_act"], 1)
                for h in range(HALVES):
                    last = dve.tensor_scalar(hid_wide[:, h, :], c.ones[:, :], c.hid_empty[:, LAYERS - 1, h:h + 1],
                                             None, ALU.mult)
                last.then_inc(S["on_dve"], 1)
                dve.wait_ge(S["on_pe"], 2)
                for l in range(LAYERS):
                    dve.tensor_tensor(c.psi_b1_mean[:, l, :], bank[1][:, 2 * l:2 * l + 2], c.psi_b1[:, l, :], ALU.add)
                dve.tensor_tensor(c.empty[:, :], bank[2][:, 0:LAYERS], c.psi_b2[:, :], ALU.add).then_inc(S["on_dve"], 1)
                dve.tensor_tensor(c.empty_row[:, :], bank[4][:, 0:D], psi_b2_row[:, :], ALU.add)
                dve.tensor_copy(c.gate_own[:, :], bank[3][:, 0:1])
                dve.tensor_tensor(c.bgate[:, :], c.bgate[:, :], bank[5][:, 0:1], ALU.add).then_inc(S["on_dve"], 1)
                dve.wait_ge(S["on_dve"], 5)
                dve.tensor_scalar(c.minus_prelu[:, :], c.prelu[:, :], -1.0, None, ALU.mult)
                dve.tensor_scalar(c.gate_bias[:, :], c.bgate[:, :], 0.5, None, ALU.mult)
                dve.tensor_scalar(c.empty_relu[:, :], c.empty[:, :], 0.0, None, ALU.max).then_inc(S["on_dve"], 1)
                dve.wait_ge(S["on_dve"], 6)
                dve.tensor_tensor(c.h1_bias[:, :], c.proj_b[:, :], c.empty_relu[:, 0:1], ALU.add).then_inc(S["on_dve"], 1)
                dve.wait_ge(S["on_dve"], 7)
                dve.tensor_tensor(c.h2_bias[:, :], c.h1_bias[:, :], c.empty_relu[:, 1:2], ALU.add)

            @block.tensor
            def _(pe):
                pe.wait_ge(S["loaded"], 16 * len(loads))
                pe.wait_ge(S["picked"], 1)
                pe.transpose(bank[0][:, 0:D], c.wskip[:, :], c.ident[:, :]).then_inc(S["on_pe"], 1)
                pe.wait_ge(S["on_act"], 1)
                pe.wait_ge(S["on_dve"], 3)
                for l in range(LAYERS):
                    for h in range(HALVES):
                        pe.matmul(bank[1][:, 2 * l + h:2 * l + h + 1], c.psi_w1[l][:, h * P:(h + 1) * P],
                                  c.phi_b2[:, l:l + 1], start=True, stop=True)
                    for h in range(HALVES):
                        pe.matmul(bank[2][:, l:l + 1], c.psi_w2[l][:, h, :], c.hid_empty[:, l, h:h + 1],
                                  start=(h == 0), stop=(h == HALVES - 1))
                for h in range(HALVES):
                    pe.matmul(bank[4][:, 0:D], hid_wide[:, h, :], c.psi_w2[LAYERS - 1][:, h, :],
                              start=(h == 0), stop=(h == HALVES - 1))
                pe.matmul(bank[3][:, 0:1], c.wskip_t[:, :], c.gate_skip[:, :], start=True, stop=True)
                pe.matmul(bank[5][:, 0:1], c.bskip[:, :].to_broadcast([P, P]), c.gate_skip[:, :],
                          start=True, stop=True).then_inc(S["on_pe"], 1)


def segments(nc, a, c, e, r, t, bank):
    with ExitStack() as ctx:
        S = named_semaphores(nc, ctx, "seg", "loaded filled chain columns lines carried carry_columns safe root "
                             "computed stored")

        def sb(name, shape, dt=F32):
            return ctx.enter_context(nc.sbuf_tensor(f"seg_{name}", shape, dt))

        raw = [sb(f"raw{n}", [P, COLS], I32) for n in range(3)]
        dst = [sb(f"dst{n}", [P, COLS]) for n in range(3)]
        weight, pos, one = sb("weight", [P, COLS]), sb("pos", [P, COLS]), sb("one", [P, COLS])
        pos_int = sb("pos_int", [P, COLS], I32)
        same = [sb("same_prev", [P, COLS]), sb("same_next", [P, COLS])]
        first, last = sb("first", [P, COLS]), sb("last", [P, COLS])
        row16 = [sb(f"row16_{n}", [P, COLS], BF16) for n in range(3)]
        data = [[sb(f"data{d}{q}", [P, COLS]) for q in range(3)] for d in range(2)]
        part = [[sb(f"part{d}{q}", [P, COLS]) for q in range(3)] for d in range(2)]
        whole = [[sb(f"whole{d}{q}", [P, COLS]) for q in range(3)] for d in range(2)]
        through = [sb(f"through{d}", [P, COLS]) for d in range(2)]
        columns = [sb(f"columns{d}", [P, 2, 3]) for d in range(2)]
        lines = [sb(f"lines{d}", [3, 2, P]) for d in range(2)]
        carry = [sb(f"carry{d}", [3, P + 1]) for d in range(2)]
        carry_in = [sb(f"carry_in{d}", [P, 3]) for d in range(2)]
        deg, above, inv = sb("deg", [P, 2, COLS]), sb("above", [P, 2, COLS]), sb("inv", [P, 2, COLS])
        safe, root, raw_inv = sb("safe", [P, 2, COLS]), sb("root", [P, 2, COLS]), sb("raw_inv", [P, 2, COLS])
        inv_count, elsewhere = sb("inv_count", [P, COLS]), sb("elsewhere", [P, COLS])
        node = sb("node", [P, COLS, 4])

        def linear(row):
            return row.rearrange("(p c) -> p c", p=P)

        with nc.Block() as block:
            @block.sync
            def _(sp):
                for n in range(3):
                    sp.dma_start(raw[n][:, :], linear(a["dst_line"][n:n + ROWS])).then_inc(S["loaded"], 16)
                sp.dma_start(weight[:, :], linear(a["weight_line"])).then_inc(S["loaded"], 16)
                sp.dma_start(e.src[:, :], a["src_tiles"]).then_inc(S["loaded"], 16)
                sp.dma_start(e.dst[:, :], a["dst_tiles"]).then_inc(S["loaded"], 16)
                sp.wait_ge(S["computed"], 1)
                sp.dma_start(t.place.rearrange("(p c) k -> p c k", p=P), node[:, :, :]).then_inc(S["stored"], 16)
                for row, tile in ((r.same_prev, row16[0]), (r.same_next, row16[1]), (r.cut_next, row16[2]),
                                  (r.inv_count, inv_count)):
                    sp.dma_start(linear(row), tile[:, :]).then_inc(S["stored"], 16)
                for n, row in enumerate((r.dinv2, r.dinv3)):
                    sp.dma_start(linear(row), inv[:, n, :]).then_inc(S["stored"], 16)
                sp.wait_ge(S["stored"], 16 * 7)
                sp.wait_ge(S["loaded"], 16 * 6)

            @block.gpsimd
            def _(pool):
                pool.iota(pos_int[:, :], pattern=[[1, COLS]], base=0, channel_multiplier=COLS)
                pool.memset(one[:, :], 1.0)
                for d in range(2):
                    pool.memset(carry[d][:, :], 0.0)
                pool.memset(node[:, :, 2:4], 1.0).then_inc(S["filled"], 1)

            @block.tensor
            def _(pe):
                for d in range(2):
                    pe.wait_ge(S["columns"], d + 1)
                    for n in range(2):
                        last_ = pe.transpose(bank[d][0:3, n * P:(n + 1) * P], columns[d][:, n, :], c.ident[:, :])
                    last_.then_inc(S["lines"], 1)
                    pe.wait_ge(S["carried"], d + 1)
                    pe.transpose(bank[2 + d][:, 0:3], carry[d][:, d:d + P], c.ident[0:3, 0:3])\
                      .then_inc(S["carry_columns"], 1)

            @block.scalar
            def _(act):
                act.wait_ge(S["safe"], 1)
                act.activation(root[:, :, :], safe[:, :, :], ACT.Sqrt).then_inc(S["root"], 1)

            @block.vector
            def _(dve):
                links = [0]

                def link(ins):
                    links[0] += 1
                    ins.then_inc(S["chain"], 1)
                    dve.wait_ge(S["chain"], links[0])

                dve.wait_ge(S["loaded"], 16 * 6)
                dve.wait_ge(S["filled"], 1)
                for n in range(3):
                    dve.tensor_copy(dst[n][:, :], raw[n][:, :])
                link(dve.tensor_copy(pos[:, :], pos_int[:, :]))
                dve.tensor_tensor(same[0][:, :], dst[1][:, :], dst[0][:, :], ALU.is_equal)
                dve.tensor_tensor(same[1][:, :], dst[1][:, :], dst[2][:, :], ALU.is_equal)
                dve.tensor_tensor(first[:, :], dst[1][:, :], dst[0][:, :], ALU.not_equal)
                link(dve.tensor_tensor(last[:, :], dst[1][:, :], dst[2][:, :], ALU.not_equal))
                dve.tensor_copy(row16[0][:, :], same[0][:, :])
                dve.tensor_copy(row16[1][:, :], same[1][:, :])
                dve.tensor_scalar(row16[2][:, :], last[:, :], FAR, None, ALU.mult)
                dve.tensor_scalar(elsewhere[:, :], last[:, :], -float(NOWHERE), float(NOWHERE), ALU.mult, ALU.add)
                link(dve.tensor_tensor(data[0][2][:, :], first[:, :], pos[:, :], ALU.mult))
                dve.tensor_tensor(e.place_row[:, :], elsewhere[:, :], dst[1][:, :], ALU.add)
                for d in range(2):
                    flow = slice(None, None, 1 - 2 * d)
                    edge = (COLS - 1) * (1 - d)
                    add = data[1] if d else [weight, one, data[0][2]]
                    if d:
                        for q, x in enumerate((whole[0][0], whole[0][1], pos)):
                            last_ = dve.tensor_tensor(data[1][q][:, :], last[:, :], x[:, :], ALU.mult)
                        link(last_)
                    for q in range(3):
                        dve.tensor_tensor_scan(part[d][q][:, flow], same[d][:, flow], add[q][:, flow], 0.0,
                                               ALU.mult, ALU.add)
                    link(dve.tensor_tensor_scan(through[d][:, flow], same[d][:, flow], one[:, flow], 1.0,
                                                ALU.mult, ALU.min))
                    for q in range(3):
                        dve.tensor_copy(columns[d][:, 0, q:q + 1], part[d][q][:, edge:edge + 1])
                        last_ = dve.tensor_copy(columns[d][:, 1, q:q + 1], through[d][:, edge:edge + 1])
                    last_.then_inc(S["columns"], 1)
                    dve.wait_ge(S["lines"], d + 1)
                    link(dve.tensor_copy(lines[d][:, :, :], bank[d][0:3, 0:2 * P].rearrange("q (n p) -> q n p", n=2)))
                    into = carry[d][:, 1 - d:1 - d + P][:, flow]
                    dve.tensor_tensor_scan(into, lines[d][:, 1, flow], lines[d][:, 0, flow], 0.0,
                                           ALU.mult, ALU.add).then_inc(S["carried"], 1)
                    dve.wait_ge(S["carry_columns"], d + 1)
                    link(dve.tensor_copy(carry_in[d][:, :], bank[2 + d][:, 0:3]))
                    for q in range(3):
                        last_ = dve.scalar_tensor_tensor(whole[d][q][:, :], through[d][:, :], carry_in[d][:, q:q + 1],
                                                         part[d][q][:, :], ALU.mult, ALU.add)
                    link(last_)
                total_weight, count, end = whole[1]
                start = whole[0][2]
                dve.tensor_scalar(deg[:, 0, :], total_weight[:, :], 1.0, None, ALU.add)
                link(dve.tensor_scalar(deg[:, 1, :], count[:, :], 1.0, None, ALU.add))
                dve.tensor_scalar(safe[:, :, :], deg[:, :, :], 1e-30, None, ALU.max).then_inc(S["safe"], 1)
                dve.tensor_scalar(above[:, :, :], deg[:, :, :], 0.0, None, ALU.is_gt)
                dve.wait_ge(S["root"], 1)
                link(dve.reciprocal(raw_inv[:, :, :], root[:, :, :]))
                link(dve.tensor_tensor(inv[:, :, :], raw_inv[:, :, :], above[:, :, :], ALU.mult))
                dve.reciprocal(inv_count[:, :], count[:, :])
                dve.tensor_copy(e.place[:, :, 0], end[:, :])
                dve.tensor_copy(e.place[:, :, 1], start[:, :])
                for n in range(2):
                    dve.tensor_copy(e.place[:, :, 2 + n], inv[:, n, :])
                for n in range(2):
                    last_ = dve.tensor_scalar(node[:, :, n], pos[:, :], float(NODE0), None, ALU.add)
                last_.then_inc(S["computed"], 1)


class LayerNorm:

    def __init__(self, sb, name):
        self.stats, self.moments = sb(f"{name}_stats", [P, TILES, 6]), sb(f"{name}_moments", [P, TILES, 2])
        self.scale, self.shift = sb(f"{name}_scale", [P, TILES]), sb(f"{name}_shift", [P, TILES])


def layernorm_buffers(sb, name):
    return [LayerNorm(sb, f"{name}{s}") for s in range(2)]


def layernorm_stats(dve, S, stats_done, moments_done, g, rows, ln, spread):
    for j in range(TILES):
        last = dve.bn_stats(ln.stats[:, j, :], rows[:, j * D:(j + 1) * D])
    last.then_inc(stats_done, 1)
    wait_alone(dve, S["passed"], stats_done, g + 1)
    for j in range(TILES):
        last = dve.bn_aggr(ln.moments[:, j, :], ln.stats[:, j, :])
    last.then_inc(moments_done, 1)
    dve.wait_ge(moments_done, g + 1)
    return dve.tensor_scalar(spread, ln.moments[:, :, 1], EPS, None, ALU.add)


def layernorm_factors(dve, scale_done, shift_done, g, root, mask, ln):
    if mask is None:
        dve.tensor_copy(ln.scale[:, :], root).then_inc(scale_done, 1)
    else:
        dve.tensor_tensor(ln.scale[:, :], root, mask, ALU.mult).then_inc(scale_done, 1)
    dve.wait_ge(scale_done, g + 1)
    dve.scalar_tensor_tensor(ln.shift[:, :], ln.moments[:, :, 0], -1.0, ln.scale[:, :], ALU.mult, ALU.mult)\
       .then_inc(shift_done, 1)


def layernorm_apply(act, out, rows, ln):
    for j in range(TILES):
        at = slice(j * D, (j + 1) * D)
        last = act.activation(out[:, at], rows[:, at], ACT.Identity, bias=ln.shift[:, j:j + 1], scale=ln.scale[:, j:j + 1])
    return last


def transpose_tiles(pe, out, rows, c):
    for j in range(TILES):
        at = slice(j * P, (j + 1) * P)
        last = pe.transpose(out[:, at], rows[:, at], c.ident[:, :])
    return last


def node_space(nc, a, c, e, t, bank):
    BATCH = NODE_BATCH
    SCATTERS = COLS // BATCH
    GATHERS = GROUPS - SCATTERS
    with ExitStack() as ctx:
        S = named_semaphores(nc, ctx, "node", "x_turned xT projected hT h_turned h_rows x1_turned x1T skipped tanh "
                             "centred stats0 moments0 scale0 shift0 x1_rows stats1 moments1 scale1 shift1 normed "
                             "skip_bias gate mixed scaled_gamma affine negative positive residual "
                             "stats2 moments2 scale2 shift2 x2_rows spread root filled staged unstaged",
                             "h1_out h2_out x1_out x2_out scattered gathered", "x_in")

        def sb(name, shape, dt=F32):
            return ctx.enter_context(nc.sbuf_tensor(f"node_{name}", shape, dt))

        x_rows = [sb(f"x_rows{s}", [P, GROUP]) for s in range(4)]
        x1_rows, xc, mixed, res = ([sb(f"{n}{s}", [P, GROUP]) for s in range(4)] for n in "x1_rows xc mixed res".split())
        (xT, h1T, h2T, h1_rows, h2_rows, x1T, skip, normed, gam, aff, neg, pos, x2_rows) = (
            [sb(f"{n}{s}", [P, GROUP]) for s in range(2)] for n in
            "xT h1T h2T h1_rows h2_rows x1T skip normed gam aff neg pos x2_rows".split())
        th, gate = ([sb(f"{n}{s}", [P, TILES]) for s in range(2)] for n in ("th", "gate"))
        ln = [layernorm_buffers(sb, f"ln{n}") for n in range(3)]
        spread, root = ([sb(f"{n}{s}", [P, 3, TILES]) for s in range(2)] for n in ("spread", "root"))
        power = sb("power", [P, 3, TILES])
        stage_row = [sb(f"stage_row{s}", [P, BATCH], I32) for s in range(2)]
        stage = [sb(f"stage{s}", [P, BATCH, 4]) for s in range(2)]
        fetch_row = [sb(f"fetch_row{s}", [P, BATCH], I32) for s in range(2)]
        fetch = [sb(f"fetch{s}", [P, BATCH, 4]) for s in range(2)]

        with nc.Block() as block:
            @block.sync
            def _(sp):
                def step(i, u):
                    g = live(i, 0)
                    if g is not None:
                        s = u
                        wait_alone(sp, S["passed"], S["x_turned"], g - 3)
                        wait_alone(sp, S["passed"], S["centred"], g - 3)
                        sp.dma_start(tiles(x_rows[s][:, :]), group_rows(a["x"], 0, g)).then_inc(S["x_in"][s], 16)
                    g = live(i, 4)
                    if g is not None:
                        s = u % 2
                        wait_alone(sp, S["passed"], S["h_rows"], g + 1)
                        sp.dma_start(group_rows(t.h1, NODE0, g), tiles(h1_rows[s][:, :])).then_inc(S["h1_out"][s], 16)
                        sp.dma_start(group_rows(t.h2, NODE0, g), tiles(h2_rows[s][:, :])).then_inc(S["h2_out"][s], 16)
                        wait_alone(sp, S["passed"], S["x1_rows"], g + 1)
                        sp.dma_start(group_rows(t.x1, NODE0, g), tiles(x1_rows[u][:, :]))\
                          .then_inc(S["x1_out"][s], 16)
                    g = live(i, 10)
                    if g is not None:
                        s = u % 2
                        wait_alone(sp, S["passed"], S["x2_rows"], g + 1)
                        sp.dma_start(group_rows(t.x2, NODE0, g), tiles(x2_rows[s][:, :])).then_inc(S["x2_out"][s], 16)

                run_steps(sp, step, 4, 12, 10)
                for s in range(2):
                    for out_ in (S["h1_out"], S["h2_out"], S["x1_out"], S["x2_out"]):
                        sp.wait_ge(out_[s], 16 * (GROUPS // 2))

            @block.gpsimd
            def _(pool):
                for s in range(2):
                    pool.memset(spread[s][:, :, :], 1.0)
                pool.memset(power[:, :, :], -0.5).then_inc(S["filled"], 1)
                pool.wait_ge(S["filled"], 1)

                def norms(i, s):
                    wait_alone(pool, S["passed"], S["spread"], i + 1)
                    pool.tensor_tensor(root[s][:, :, :], spread[s][:, :, :], power[:, :, :], ALU.pow).then_inc(S["root"], 1)

                def scatter(i, s):
                    at = bass.ds(i * BATCH, BATCH)
                    if not isinstance(i, int) or i >= 2:
                        wait_alone(pool, S["passed"], S["scattered"][s], (i - s) * (8 * BATCH))
                    pool.tensor_copy(stage_row[s][:, :], e.place_row[:, at])
                    pool.tensor_copy(stage[s][:, :, :], e.place[:, at, :]).then_inc(S["staged"], 1)
                    wait_alone(pool, S["passed"], S["staged"], i + 1)
                    for j in range(BATCH):
                        pool.indirect_dma_start(t.place[:, :], bass.IndirectOffsetOnAxis(ap=stage_row[s][:, j:j + 1], axis=0),
                                                stage[s][:, j, :], None, bounds_check=ROWS - 1, oob_is_err=False)\
                            .then_inc(S["scattered"][s], 16)
                    norms(i, s)

                def fetched(m, s):
                    wait_alone(pool, S["passed"], S["gathered"][s], (m - s) * (8 * BATCH) + 16 * BATCH)
                    pool.tensor_copy(e.fetched[:, bass.ds(m * BATCH, BATCH), :], fetch[s][:, :, :]).then_inc(S["unstaged"], 1)
                    wait_alone(pool, S["passed"], S["unstaged"], m + 1)

                def gather(m, s):
                    if not isinstance(m, int) or m >= 2:
                        fetched(m - 2, s)
                    pool.tensor_copy(fetch_row[s][:, :], e.src[:, bass.ds(m * BATCH, BATCH)]).then_inc(S["staged"], 1)
                    wait_alone(pool, S["passed"], S["staged"], SCATTERS + m + 1)
                    for j in range(BATCH):
                        pool.indirect_dma_start(fetch[s][:, j, :], None, t.place[:, :],
                                                bass.IndirectOffsetOnAxis(ap=fetch_row[s][:, j:j + 1], axis=0))\
                            .then_inc(S["gathered"][s], 16)
                    norms(SCATTERS + m, s)

                for i in range(2):
                    scatter(i, i)
                with pool.Fori(1, SCATTERS // 2) as k:
                    for s in range(2):
                        scatter(2 * k + s, s)
                for s in range(2):
                    pool.wait_ge(S["scattered"][s], 16 * BATCH * (SCATTERS // 2))
                for m in range(2):
                    gather(m, m)
                with pool.Fori(1, GATHERS // 2) as k:
                    for s in range(2):
                        gather(2 * k + s, s)
                for i in range(GROUPS, GROUPS + 6):
                    norms(i, i % 2)
                for m in (GATHERS - 2, GATHERS - 1):
                    fetched(m, m % 2)

            @block.tensor
            def _(pe):
                def step(i, u):
                    g = live(i, 3)
                    if g is not None:
                        pe.wait_ge(S["x1_rows"], g + 1)
                        wait_from(pe, S["x1T"], g)
                        transpose_tiles(pe, bank[4], x1_rows[(u - 3) % 4], c).then_inc(S["x1_turned"], 1)
                    g = live(i, 0)
                    if g is not None:
                        pe.wait_ge(S["x_in"][u], landed(g, u, 4, 16))
                        wait_from(pe, S["xT"], g)
                        transpose_tiles(pe, bank[0], x_rows[u], c).then_inc(S["x_turned"], 1)
                    g = live(i, 3)
                    if g is not None:
                        s = (u - 3) % 2
                        pe.wait_ge(S["x1T"], g + 1)
                        wait_from(pe, S["skip_bias"], g)
                        wait_from(pe, S["tanh"], g)
                        for j in range(TILES):
                            at = slice(j * P, (j + 1) * P)
                            pe.matmul(bank[5][:, at], x1T[s][:, at], c.wskip[:, :], start=True, stop=True)
                            last = pe.matmul(bank[6][:, j:j + 1], x1T[s][:, at], c.gate_own[:, :], start=True, stop=True)
                        last.then_inc(S["skipped"], 1)
                    g = live(i, 2)
                    if g is not None:
                        s = u % 2
                        pe.wait_ge(S["hT"], g + 1)
                        wait_from(pe, S["h_rows"], g)
                        transpose_tiles(pe, bank[2], h1T[s], c)
                        transpose_tiles(pe, bank[3], h2T[s], c).then_inc(S["h_turned"], 1)
                    g = live(i, 1)
                    if g is not None:
                        pe.wait_ge(S["xT"], g + 1)
                        wait_from(pe, S["hT"], g)
                        pe.matmul(bank[1][:, :], c.proj_w[:, :], xT[(u - 1) % 2][:, :], start=True, stop=True)\
                          .then_inc(S["projected"], 1)

                run_steps(pe, step, 4, 12, 3)

            @block.scalar
            def _(act):
                def step(i, u):
                    g = live(i, 6)
                    if g is not None:
                        negative_part(act, S, g, aff[u % 2], neg[u % 2])
                    g = live(i, 3)
                    if g is not None:
                        s = (u - 3) % 2
                        act.wait_ge(S["x1_turned"], g + 1)
                        wait_from(act, S["skipped"], g - 1)
                        act.copy(x1T[s][:, :], bank[4][:, :]).then_inc(S["x1T"], 1)
                    g = live(i, 0)
                    if g is not None:
                        s = u % 2
                        act.wait_ge(S["x_turned"], g + 1)
                        wait_from(act, S["projected"], g - 1)
                        act.copy(xT[s][:, :], bank[0][:, :]).then_inc(S["xT"], 1)
                    g = live(i, 8)
                    if g is not None:
                        s = u % 2
                        act.wait_ge(S["shift2"], g + 1)
                        if not isinstance(g, int) or g >= 2:
                            act.wait_ge(S["x2_out"][s], landed(g - 2, s, 2, 16))
                        layernorm_apply(act, x2_rows[s], res[u], ln[2][s]).then_inc(S["x2_rows"], 1)
                    g = live(i, 2)
                    if g is not None:
                        s, s4 = u % 2, (u - 2) % 4
                        act.wait_ge(S["shift0"], g + 1)
                        wait_from(act, S["x1_turned"], g - 3)
                        wait_from(act, S["residual"], g - 3)
                        if not isinstance(g, int) or g >= 4:
                            act.wait_ge(S["x1_out"][s], landed(g - 4, s, 2, 16))
                        layernorm_apply(act, x1_rows[s4], xc[s4], ln[0][s]).then_inc(S["x1_rows"], 1)
                    g = live(i, 3)
                    if g is not None:
                        s = (u - 3) % 2
                        act.wait_ge(S["skipped"], g + 1)
                        wait_from(act, S["gate"], g - 1)
                        act.activation(th[s][:, :], bank[6][:, 0:TILES], ACT.Tanh, bias=c.gate_bias[:, :], scale=0.5)\
                           .then_inc(S["tanh"], 1)
                    g = live(i, 5)
                    if g is not None:
                        s, s4 = (u - 5) % 2, (u - 5) % 4
                        act.wait_ge(S["shift1"], g + 1)
                        wait_from(act, S["scaled_gamma"], g - 1)
                        layernorm_apply(act, normed[s], mixed[s4], ln[1][s]).then_inc(S["normed"], 1)
                    g = live(i, 2)
                    if g is not None:
                        s = u % 2
                        act.wait_ge(S["h_turned"], g + 1)
                        if not isinstance(g, int) or g >= 2:
                            act.wait_ge(S["h1_out"][s], landed(g - 2, s, 2, 16))
                            act.wait_ge(S["h2_out"][s], landed(g - 2, s, 2, 16))
                        act.copy(h1_rows[s][:, :], bank[2][:, :])
                        act.copy(h2_rows[s][:, :], bank[3][:, :]).then_inc(S["h_rows"], 1)
                    g = live(i, 1)
                    if g is not None:
                        s = (u - 1) % 2
                        act.wait_ge(S["projected"], g + 1)
                        wait_from(act, S["h_turned"], g - 1)
                        act.activation(h1T[s][:, :], bank[1][:, :], ACT.Identity, bias=c.h1_bias[:, :])
                        act.activation(h2T[s][:, :], bank[1][:, :], ACT.Identity, bias=c.h2_bias[:, :]).then_inc(S["hT"], 1)

                run_steps(act, step, 4, 12, 8)

            @block.vector
            def _(dve):
                def step(i, u):
                    here = spread[u % 2]
                    if not isinstance(i, int) or i >= 2:
                        dve.wait_ge(S["root"], i - 1)
                    for lag, mark_scale, mark_shift, done, n in ((2, S["scale0"], S["shift0"], S["x1_rows"], 0),
                                                                 (8, S["scale2"], S["shift2"], S["x2_rows"], 2),
                                                                 (5, S["scale1"], S["shift1"], S["normed"], 1)):
                        g = live(i, lag)
                        if g is not None:
                            s = (u - lag) % 2
                            wait_from(dve, done, g - 1)
                            layernorm_factors(dve, mark_scale, mark_shift, g, root[u % 2][:, n, :], None, ln[n][s])
                    last = None
                    g = live(i, 6)
                    if g is not None:
                        s, s4 = u % 2, (u - 6) % 4
                        last = prelu_residual(dve, S, c, g, aff[s], neg[s], pos[s], x1_rows[s4][:, :], res[s4],
                                              S["x2_rows"], ln[2][s], here[:, 2, :], slots=4)
                    g = live(i, 0)
                    if g is not None:
                        s = u % 2
                        dve.wait_ge(S["x_in"][u], landed(g, u, 4, 16))
                        wait_from(dve, S["x1_rows"], g - 3)
                        dve.wait_ge(S["filled"], 1)
                        dve.tensor_tensor(tiles(xc[u][:, :]), tiles(x_rows[u][:, :]),
                                          c.empty_row[:, :].unsqueeze(1).to_broadcast([P, TILES, D]), ALU.add)\
                           .then_inc(S["centred"], 1)
                        dve.wait_ge(S["centred"], g + 1)
                        last = layernorm_stats(dve, S, S["stats0"], S["moments0"], g, xc[u], ln[0][s], here[:, 0, :])
                    g = live(i, 3)
                    if g is not None:
                        s, s4 = (u - 3) % 2, (u - 3) % 4
                        dve.wait_ge(S["skipped"], g + 1)
                        dve.tensor_tensor(tiles(skip[s][:, :]), tiles(bank[5][:, :]),
                                          c.bskip_row[:, :].unsqueeze(1).to_broadcast([P, TILES, D]), ALU.add)\
                           .then_inc(S["skip_bias"], 1)
                        dve.wait_ge(S["tanh"], g + 1)
                        dve.tensor_scalar(gate[s][:, :], th[s][:, :], 0.5, 0.5, ALU.mult, ALU.add).then_inc(S["gate"], 1)
                        dve.wait_ge(S["gate"], g + 1)
                        wait_from(dve, S["normed"], g - 3)
                        dve.tensor_tensor(tiles(mixed[s4][:, :]), tiles(skip[s][:, :]), over_features(gate[s][:, :], D),
                                          ALU.mult).then_inc(S["mixed"], 1)
                        dve.wait_ge(S["mixed"], g + 1)
                        last = layernorm_stats(dve, S, S["stats1"], S["moments1"], g, mixed[s4], ln[1][s], here[:, 1, :])
                    if last is None:
                        last = dve.memset(here[:, 0, :], 1.0)
                    last.then_inc(S["spread"], 1)
                    g = live(i, 5)
                    if g is not None:
                        s = (u - 5) % 2
                        affine(dve, S, c, g, normed[s], gam[s], aff[s])

                run_steps(dve, step, 4, 12, 8)


def affine(eng, S, c, g, normed, gam, aff):
    eng.wait_ge(S["normed"], g + 1)
    eng.tensor_tensor(tiles(gam[:, :]), tiles(normed[:, :]), c.gamma_row[:, :].unsqueeze(1).to_broadcast([P, TILES, D]),
                      ALU.mult).then_inc(S["scaled_gamma"], 1)
    eng.wait_ge(S["scaled_gamma"], g + 1)
    wait_from(eng, S["positive"], g - 1)
    wait_from(eng, S["negative"], g - 1)
    eng.tensor_tensor(tiles(aff[:, :]), tiles(gam[:, :]), c.beta_row[:, :].unsqueeze(1).to_broadcast([P, TILES, D]),
                      ALU.add).then_inc(S["affine"], 1)


def negative_part(act, S, g, aff, neg):
    act.wait_ge(S["affine"], g + 1)
    wait_from(act, S["residual"], g - 1)
    act.activation(neg[:, :], aff[:, :], ACT.Relu, scale=-1.0).then_inc(S["negative"], 1)


def prelu_residual(dve, S, c, g, aff, neg, pos, x1_rows, res, res_read, ln, spread, slots=2):
    dve.wait_ge(S["affine"], g + 1)
    dve.scalar_tensor_tensor(pos[:, :], aff[:, :], 0.0, x1_rows, ALU.max, ALU.add).then_inc(S["positive"], 1)
    dve.wait_ge(S["positive"], g + 1)
    dve.wait_ge(S["negative"], g + 1)
    wait_from(dve, res_read, g + 1 - slots)
    dve.scalar_tensor_tensor(res[:, :], neg[:, :], c.minus_prelu[:, :], pos[:, :], ALU.mult, ALU.add)\
       .then_inc(S["residual"], 1)
    dve.wait_ge(S["residual"], g + 1)
    return layernorm_stats(dve, S, S["stats2"], S["moments2"], g, res, ln, spread)


def edge_masks(nc, a, e):
    with ExitStack() as ctx:
        S = named_semaphores(nc, ctx, "mask", "loaded chain")
        near = [ctx.enter_context(nc.sbuf_tensor(f"mask_near{n}", [P, COLS], I32)) for n in range(2)]
        dst, elsewhere, *nearf = (ctx.enter_context(nc.sbuf_tensor(f"mask_{n}", [P, COLS], F32))
                                  for n in ("dst", "elsewhere", "nearf0", "nearf1"))

        with nc.Block() as block:
            @block.sync
            def _(sp):
                sp.dma_start(near[0][:, :], a["prev_tiles"]).then_inc(S["loaded"], 16)
                sp.dma_start(near[1][:, :], a["next_tiles"]).then_inc(S["loaded"], 16)
                sp.wait_ge(S["loaded"], 16 * 2)

            @block.vector
            def _(dve):
                dve.wait_ge(S["loaded"], 16 * 2)
                for n in range(2):
                    dve.tensor_copy(nearf[n][:, :], near[n][:, :])
                dve.tensor_copy(dst[:, :], e.dst[:, :]).then_inc(S["chain"], 1)
                dve.wait_ge(S["chain"], 1)
                dve.tensor_tensor(e.is_end[:, :], dst[:, :], nearf[1][:, :], ALU.not_equal)
                dve.tensor_tensor(e.is_start[:, :], dst[:, :], nearf[0][:, :], ALU.not_equal).then_inc(S["chain"], 1)
                dve.wait_ge(S["chain"], 2)
                dve.tensor_scalar(elsewhere[:, :], e.is_start[:, :], -float(NOWHERE), float(NOWHERE),
                                  ALU.mult, ALU.add).then_inc(S["chain"], 1)
                dve.wait_ge(S["chain"], 3)
                dve.tensor_tensor(e.out_row[:, :], elsewhere[:, :], dst[:, :], ALU.add)


def edge_scalars(nc, a, c, e, r, bank):
    QUARTER = COLS // 4
    with ExitStack() as ctx:
        S = named_semaphores(nc, ctx, "scal", "loaded turned chain")

        def sb(name, shape, dt=F32):
            return ctx.enter_context(nc.sbuf_tensor(f"scal_{name}", shape, dt))

        line = [sb(f"line{n}", [QUARTER, 4, P]) for n in range(2)]
        own = [sb(f"own{n}", [P, COLS]) for n in range(2)]
        weight, weighted_src = sb("weight", [P, COLS]), sb("weighted_src", [P, COLS])

        with nc.Block() as block:
            @block.sync
            def _(sp):
                for n, row in enumerate((r.dinv2, r.dinv3)):
                    sp.dma_start(line[n][:, :, :], row.rearrange("(b t p) -> t b p", b=4, p=P)).then_inc(S["loaded"], 16)
                sp.dma_start(weight[:, :], a["weight_tiles"]).then_inc(S["loaded"], 16)
                sp.wait_ge(S["loaded"], 16 * 3)

            @block.tensor
            def _(pe):
                pe.wait_ge(S["loaded"], 16 * 3)
                for n in range(2):
                    for b in range(4):
                        last = pe.transpose(bank[n][:, b * QUARTER:(b + 1) * QUARTER], line[n][:, b, :],
                                            c.ident[0:QUARTER, 0:QUARTER])
                last.then_inc(S["turned"], 1)

            @block.vector
            def _(dve):
                links = [0]

                def link(ins):
                    links[0] += 1
                    ins.then_inc(S["chain"], 1)
                    dve.wait_ge(S["chain"], links[0])

                dve.wait_ge(S["loaded"], 16 * 3)
                dve.tensor_copy(e.src_at_end[:, :], e.fetched[:, :, 0])
                dve.tensor_copy(e.src_at_start[:, :], e.fetched[:, :, 1])
                dve.wait_ge(S["turned"], 1)
                for n in range(2):
                    last = dve.tensor_copy(own[n][:, :], bank[n][:, 0:COLS])
                link(last)
                dve.tensor_tensor(weighted_src[:, :], weight[:, :], e.fetched[:, :, 2], ALU.mult)
                dve.tensor_tensor(e.self2[:, :], own[0][:, :], own[0][:, :], ALU.mult)
                dve.tensor_tensor(e.self3[:, :], own[1][:, :], own[1][:, :], ALU.mult)
                link(dve.tensor_tensor(e.norm3[:, :], own[1][:, :], e.fetched[:, :, 3], ALU.mult))
                dve.tensor_tensor(e.norm2[:, :], own[0][:, :], weighted_src[:, :], ALU.mult)


def conv_pass(nc, a, c, e, r, t, bank, l, src_table, own_table, src_rows_at, backward, out_table, place_mask):
    first_layer, last_layer = l == 0, l == LAYERS - 1
    flow = slice(None, None, -1) if backward else slice(None)
    entry = slice(GROUP - 1, GROUP) if not backward else slice(0, 1)
    same = r.same_next if backward else r.same_prev

    def at(g):
        return GROUPS - 1 - g if backward else g

    with ExitStack() as ctx:
        S = named_semaphores(nc, ctx, f"conv{l}", "staged own_staged turned src_done own_done phi_hid phi_act msg summed mean psi_hid "
                             "psi_act conv conv_act h h_turned rows residual stats moments spread root plain scale shift",
                             four_slots="gathered own_in mask_in inv_in x_in place_in stored")

        def sb(name, shape, dt=F32, slots=2):
            return [ctx.enter_context(nc.sbuf_tensor(f"conv{l}_{name}{s}", shape, dt)) for s in range(slots)]

        src_rows, own_rows, x_rows, res, rows, inv = (
            sb(n, [P, GROUP], slots=4) for n in "src_rows own_rows x_rows res rows inv".split())
        mask = sb("mask", [P, GROUP], BF16, 4)
        at_src, at_own = sb("at_src", [P, TILES], I32, 4), sb("at_own", [P, TILES], I32, 4)
        at_place, place = sb("at_place", [P, 1], I32, 4), sb("place", [P, 1, 4], F32, 4)
        place_col = COLS - CONV_TILES
        srcT, ownT, phi0, phi1, psi0, psi1, total, mean, convT, hT = (
            sb(n, [P, GROUP]) for n in "srcT ownT phi0 phi1 psi0 psi1 total mean convT hT".split())
        phi, psi = list(zip(phi0, phi1)), list(zip(psi0, psi1))
        spread, root, plain = (sb(n, [P, TILES]) for n in ("spread", "root", "plain"))
        ln = layernorm_buffers(lambda n, s: ctx.enter_context(nc.sbuf_tensor(f"conv{l}_{n}", s, F32)), "ln")
        b_own, b_src, b_phi, b_msg, b_psi, b_rows = bank[0], bank[1], bank[2:4], bank[4], bank[5:7], bank[7]
        b_conv, b_proj = b_psi
        norm_lag = 2

        with nc.Block() as block:
            @block.sync
            def _(sp):
                def step(i, u):
                    g = live(i, 0)
                    if g is not None:
                        s = u
                        if not first_layer:
                            wait_alone(sp, S["passed"], S["turned"], g - 3)
                            sp.dma_start(tiles(own_rows[s][:, :]), group_rows(own_table, 0, at(g))).then_inc(S["own_in"][s], 16)
                        wait_alone(sp, S["passed"], S["summed"], g - 3)
                        sp.dma_start(mask[s][:, :], same[bass.ds(at(g) * GROUP, GROUP)].rearrange("(o n) -> o n", o=1)
                                     .to_broadcast([P, GROUP])).then_inc(S["mask_in"][s], 16)
                        wait_alone(sp, S["passed"], S["mean"], g - 3)
                        sp.dma_start(inv[s][:, :], r.inv_count[bass.ds(at(g) * GROUP, GROUP)].rearrange("(o n) -> o n", o=1)
                                     .to_broadcast([P, GROUP])).then_inc(S["inv_in"][s], 16)
                    g = live(i, 6)
                    if g is not None:
                        s = (u - 6) % 4
                        wait_alone(sp, S["passed"], S["rows"], g + 1)
                        sp.dma_start(group_rows(out_table, 0, at(g)), tiles(rows[s][:, :])).then_inc(S["stored"][s], 16)

                run_steps(sp, step, 4, 12, 6)
                for s in range(4):
                    sp.wait_ge(S["stored"][s], 16 * groups_of_slot(s))

            @block.gpsimd
            def _(pool):
                def fetched(g, s):
                    wait_alone(pool, S["passed"], S["place_in"][s], landed(g, s, 4, 16))
                    pool.tensor_copy(e.fetched[:, bass.ds(place_col + g, 1), :], place[s][:, :, :])

                def gather(rows_, index, table, arrived, s):
                    for j in range(TILES):
                        pool.indirect_dma_start(rows_[:, j * D:(j + 1) * D], None, table[:, :],
                                                bass.IndirectOffsetOnAxis(ap=index[:, j:j + 1], axis=0))\
                            .then_inc(arrived[s], 16)

                def step(i, u):
                    g = live(i, 0)
                    if g is not None:
                        s = u
                        wait_alone(pool, S["passed"], S["turned"], g - 3)
                        if first_layer:
                            if not isinstance(g, int) or g >= 4:
                                fetched(g - 4, s)
                            pool.tensor_copy(at_place[s][:, :], e.src[:, bass.ds(place_col + g, 1)])
                            pool.tensor_copy(at_own[s][:, :], e.dst[:, bass.ds(at(g) * TILES, TILES)])
                        pool.tensor_copy(at_src[s][:, :], src_rows_at[:, bass.ds(at(g) * TILES, TILES)]).then_inc(S["staged"], 1)
                        wait_alone(pool, S["passed"], S["staged"], g + 1)
                        gather(src_rows[s], at_src[s], src_table, S["gathered"], s)
                        if first_layer:
                            gather(own_rows[s], at_own[s], own_table, S["own_in"], s)
                            pool.indirect_dma_start(place[s][:, 0, :], None, t.place[:, :],
                                                    bass.IndirectOffsetOnAxis(ap=at_place[s][:, 0:1], axis=0))\
                                .then_inc(S["place_in"][s], 16)
                    g = live(i, 2)
                    if g is not None and last_layer:
                        s = (u - 2) % 4
                        wait_alone(pool, S["passed"], S["residual"], g - 3)
                        pool.tensor_copy(at_own[s][:, :], e.dst[:, bass.ds(at(g) * TILES, TILES)]).then_inc(S["own_staged"], 1)
                        wait_alone(pool, S["passed"], S["own_staged"], g + 1)
                        gather(x_rows[s], at_own[s], a["x"], S["x_in"], s)

                run_steps(pool, step, 4, 8, 2 if last_layer else 0)
                if first_layer:
                    for g in range(GROUPS - 4, GROUPS):
                        fetched(g, g % 4)

            @block.tensor
            def _(pe):
                def step(i, u):
                    g = live(i, 0)
                    if g is not None:
                        pe.wait_ge(S["gathered"][u], landed(g, u, 4, 16 * TILES))
                        pe.wait_ge(S["own_in"][u], landed(g, u, 4, 16 * TILES if first_layer else 16))
                        wait_from(pe, S["own_done"], g)
                        wait_from(pe, S["src_done"], g)
                        transpose_tiles(pe, b_src, src_rows[u], c)
                        transpose_tiles(pe, b_own, own_rows[u], c).then_inc(S["turned"], 1)
                    g = live(i, 1)
                    if g is not None:
                        s = (u - 1) % 2
                        pe.wait_ge(S["mean"], g + 1)
                        for h in range(HALVES):
                            if h == 0:
                                wait_from(pe, S["conv_act"], g)
                            elif first_layer:
                                wait_from(pe, S["h"], g)
                            pe.matmul(b_psi[h][:, :], c.psi_w1[l][:, h * P:(h + 1) * P], mean[s][:, :],
                                      start=True, stop=True).then_inc(S["psi_hid"], 1)
                    g = live(i, 2)
                    if g is not None:
                        s = u % 2
                        pe.wait_ge(S["conv_act"] if last_layer else S["h"], g + 1)
                        wait_from(pe, S["residual"] if last_layer else S["rows"], g)
                        transpose_tiles(pe, b_rows, convT[s] if last_layer else hT[s], c).then_inc(S["h_turned"], 1)
                    g = live(i, 0)
                    if g is not None:
                        s = u % 2
                        pe.wait_ge(S["src_done"], g + 1)
                        pe.wait_ge(S["own_done"], g + 1)
                        for h in range(HALVES):
                            wait_from(pe, S["phi_act"], HALVES * g)
                            pe.matmul(b_phi[h][:, :], c.w_src[l][:, h * P:(h + 1) * P], srcT[s][:, :], start=True, stop=False)
                            pe.matmul(b_phi[h][:, :], c.w_own[l][:, h * P:(h + 1) * P], ownT[s][:, :],
                                      start=False, stop=True).then_inc(S["phi_hid"], 1)
                    g = live(i, 1)
                    if g is not None:
                        s = (u - 1) % 2
                        pe.wait_ge(S["psi_act"], HALVES * g + HALVES)
                        pe.matmul(b_conv[:, :], c.psi_w2[l][:, 0, :], psi[s][0][:, :], start=True, stop=False)
                    g = live(i, 0)
                    if g is not None:
                        s = u % 2
                        pe.wait_ge(S["phi_act"], HALVES * g + HALVES)
                        wait_from(pe, S["summed"], g)
                        for h in range(HALVES):
                            last = pe.matmul(b_msg[:, :], c.phi_w2[l][:, h, :], phi[s][h][:, :],
                                             start=(h == 0), stop=(h == HALVES - 1))
                        last.then_inc(S["msg"], 1)
                    g = live(i, 1)
                    if g is not None:
                        s = (u - 1) % 2
                        last = pe.matmul(b_conv[:, :], c.psi_w2[l][:, 1, :], psi[s][1][:, :], start=False, stop=True)
                        if first_layer:
                            last = pe.matmul(b_proj[:, :], c.proj_w[:, :], ownT[s][:, :], start=True, stop=True)
                        last.then_inc(S["conv"], 1)

                run_steps(pe, step, 4, 8, 2)

            @block.scalar
            def _(act):
                def step(i, u):
                    g = live(i, norm_lag + 1)
                    if g is not None and last_layer:
                        s = (u - norm_lag - 1) % 2
                        act.wait_ge(S["spread"], g + 1)
                        act.activation(root[s][:, :], spread[s][:, :], ACT.Sqrt).then_inc(S["root"], 1)
                    g = live(i, 0)
                    if g is not None:
                        s = u % 2
                        act.wait_ge(S["turned"], g + 1)
                        wait_from(act, S["phi_hid"], HALVES * (g - 1))
                        act.copy(srcT[s][:, :], b_src[:, :]).then_inc(S["src_done"], 1)
                        if first_layer:
                            wait_from(act, S["conv"], g - 1)
                            act.copy(ownT[s][:, :], b_own[:, :]).then_inc(S["own_done"], 1)
                    g = live(i, 1)
                    if g is not None:
                        s = (u - 1) % 2
                        wait_from(act, S["conv"], g - 1)
                        for h in range(HALVES):
                            act.wait_ge(S["psi_hid"], HALVES * g + h + 1)
                            act.activation(psi[s][h][:, :], b_psi[h][:, :], ACT.Relu,
                                           bias=c.psi_b1_mean[:, l, h:h + 1]).then_inc(S["psi_act"], 1)
                    g = live(i, 0)
                    if g is not None:
                        s = u % 2
                        wait_from(act, S["msg"], g - 1)
                        for h in range(HALVES):
                            act.wait_ge(S["phi_hid"], HALVES * g + h + 1)
                            act.activation(phi[s][h][:, :], b_phi[h][:, :], ACT.Relu,
                                           bias=c.phi_b1[:, l, h:h + 1]).then_inc(S["phi_act"], 1)
                    g = live(i, norm_lag + 2)
                    if g is not None and last_layer:
                        s = (u - norm_lag - 2) % 4
                        act.wait_ge(S["shift"], g + 1)
                        if not isinstance(g, int) or g >= 4:
                            act.wait_ge(S["stored"][s], landed(g - 4, s, 4, 16))
                        layernorm_apply(act, rows[s], res[s], ln[s % 2]).then_inc(S["rows"], 1)
                    g = live(i, 1)
                    if g is not None:
                        s = (u - 1) % 2
                        act.wait_ge(S["conv"], g + 1)
                        wait_from(act, S["h_turned"], g - 1)
                        act.activation(convT[s][:, :], b_conv[:, :], ACT.Identity if last_layer else ACT.Relu,
                                       bias=c.psi_b2[:, l:l + 1]).then_inc(S["conv_act"], 1)

                run_steps(act, step, 4, 12, norm_lag + 2)

            @block.vector
            def _(dve):
                def step(i, u):
                    g = live(i, 0)
                    if g is not None and not first_layer:
                        s = u % 2
                        dve.wait_ge(S["mask_in"][u], landed(g, u, 4, 16))
                        dve.wait_ge(S["turned"], g + 1)
                        wait_from(dve, S["phi_hid"], HALVES * (g - 1))
                        if not last_layer:
                            wait_from(dve, S["h"], g - 1)
                        wait_from(dve, S["own_done"], g)
                        carried = 0.0 if isinstance(g, int) and g == 0 else ownT[1 - s][:, entry]
                        dve.tensor_tensor_scan(ownT[s][:, flow], mask[u][:, flow], b_own[:, flow], carried,
                                               ALU.mult, ALU.add).then_inc(S["own_done"], 1)
                    g = live(i, norm_lag)
                    if g is not None and last_layer:
                        s = (u - norm_lag) % 4
                        dve.wait_ge(S["x_in"][s], landed(g, s, 4, 16 * TILES))
                        dve.wait_ge(S["h_turned"], g + 1)
                        wait_from(dve, S["rows"], g - 3)
                        dve.tensor_tensor(res[s][:, :], b_rows[:, :], x_rows[s][:, :], ALU.add).then_inc(S["residual"], 1)
                        dve.wait_ge(S["residual"], g + 1)
                        wait_from(dve, S["root"], g - 1)
                        layernorm_stats(dve, S, S["stats"], S["moments"], g, res[s], ln[s % 2], spread[s % 2][:, :]).then_inc(S["spread"], 1)
                    g = live(i, 0)
                    if g is not None:
                        s = u % 2
                        dve.wait_ge(S["mask_in"][u], landed(g, u, 4, 16))
                        dve.wait_ge(S["msg"], g + 1)
                        wait_from(dve, S["summed"], g)
                        carried = 0.0 if isinstance(g, int) and g == 0 else total[1 - s][:, entry]
                        dve.tensor_tensor_scan(total[s][:, flow], mask[u][:, flow], b_msg[:, flow], carried,
                                               ALU.mult, ALU.add).then_inc(S["summed"], 1)
                        dve.wait_ge(S["inv_in"][u], landed(g, u, 4, 16))
                        dve.wait_ge(S["summed"], g + 1)
                        wait_from(dve, S["psi_hid"], HALVES * (g - 1))
                        dve.tensor_tensor(mean[s][:, :], total[s][:, :], inv[u][:, :], ALU.mult).then_inc(S["mean"], 1)
                    g = live(i, 1)
                    if g is not None and not last_layer:
                        s = (u - 1) % 2
                        dve.wait_ge(S["conv_act"], g + 1)
                        wait_from(dve, S["h_turned"], g - 1)
                        if first_layer:
                            dve.scalar_tensor_tensor(hT[s][:, :], b_proj[:, :], c.proj_b[:, :], convT[s][:, :],
                                                     ALU.add, ALU.add).then_inc(S["h"], 1)
                        else:
                            dve.tensor_tensor(hT[s][:, :], convT[s][:, :], ownT[s][:, :], ALU.add).then_inc(S["h"], 1)
                    g = live(i, 2)
                    if g is not None and not last_layer:
                        s = (u - 2) % 4
                        dve.wait_ge(S["h_turned"], g + 1)
                        if not isinstance(g, int) or g >= 4:
                            wait_alone(dve, S["passed"], S["stored"][s], landed(g - 4, s, 4, 16))
                        dve.tensor_tensor(tiles(rows[s][:, :]), tiles(b_rows[:, :]),
                                          over_features(place_mask[:, bass.ds(at(g) * TILES, TILES)], D),
                                          ALU.mult).then_inc(S["rows"], 1)

                    g = live(i, norm_lag + 1)
                    if g is not None and last_layer:
                        s = (u - norm_lag - 1) % 2
                        dve.wait_ge(S["root"], g + 1)
                        wait_from(dve, S["rows"], g - 1)
                        dve.reciprocal(plain[s][:, :], root[s][:, :]).then_inc(S["plain"], 1)
                        dve.wait_ge(S["plain"], g + 1)
                        layernorm_factors(dve, S["scale"], S["shift"], g, plain[s][:, :],
                                          place_mask[:, bass.ds(at(g) * TILES, TILES)], ln[s])

                run_steps(dve, step, 4, 8, norm_lag + 1)


def gcn_pass(nc, c, e, r, bank, n, table, src_rows_at, backward, out_table, residual_table, node_table):
    final = residual_table is not None
    lane = not final
    weighted = n < 2
    wide = HID2 if n == 1 else D
    out_wide = HID2 if weighted else D
    norm, self_norm = (e.norm2, e.self2) if weighted else (e.norm3, e.self3)
    out_at = out_wide if n == 1 else 0
    to_output = n == 3
    flow = slice(None, None, -1) if backward else slice(None)
    entry = slice(GROUP - 1, GROUP) if not backward else slice(0, 1)
    same = r.same_next if backward else r.same_prev
    place_mask = e.is_start if backward else e.is_end
    row_wide = D if final else out_wide

    def at(g):
        return GROUPS - 1 - g if backward else g

    with ExitStack() as ctx:
        S = named_semaphores(nc, ctx, f"gcn{n}", "staged own_scaled src_scaled summed turned own_turned agg product y "
                             "own_done y_turned rows residual stats moments spread root plain scale shift normed out_staged "
                             "n_turned n_xT n_hid n_y1 n_hid2 n_y2 n_y1_turned n_y1_rows n_sum n_sum_turned n_sum_rows",
                             four_slots="gathered own_in mask_in res_in stored n_in n_y1_out n_out scattered")

        def sb(name, shape, dt=F32, slots=2):
            return [ctx.enter_context(nc.sbuf_tensor(f"gcn{n}_{name}{s}", shape, dt)) for s in range(slots)]

        src_rows, own_rows = (sb(m, [P, TILES * wide], slots=4) for m in ("src_rows", "own_rows"))
        src_scaled, own_scaled, summed = (sb(m, [P, TILES * wide]) for m in ("src_scaled", "own_scaled", "summed"))
        mask = sb("mask", [P, GROUP], BF16, 4)
        at_src = sb("at_src", [P, TILES], I32, 4)
        agg = sb("agg", [P, GROUP])
        y, rows = (sb(m, [P, GROUP], slots=4) for m in ("y", "rows"))
        if final:
            res_rows, res = (sb(m, [P, GROUP], slots=4) for m in ("res_rows", "res"))
            at_out = sb("at_out", [P, TILES], I32, 4)
        else:
            n_rows, n_xT, n_y, n_y2, n_y1_rows, n_sum_rows, n_new = (
                sb(m, [P, GROUP], slots=4) for m in "n_rows n_xT n_y n_y2 n_y1_rows n_sum_rows n_new".split())
            n_sum = sb("n_sum", [P, GROUP])
        spread, root, plain = (sb(m, [P, TILES]) for m in ("spread", "root", "plain"))
        ln = layernorm_buffers(lambda name, shape: ctx.enter_context(nc.sbuf_tensor(f"gcn{n}_{name}", shape, F32)), "ln")
        norm_lag = 3 if final else 5
        b_agg, b_product, b_rows, b_own = bank[0:4]
        nb_x, nb_hid, nb_hid2, nb_y1, nb_sum = bank[3:8]

        def by_tile(ap, width):
            return ap[:, 0:TILES * width].rearrange("p (j f) -> p j f", j=TILES)

        with nc.Block() as block:
            @block.sync
            def _(sp):
                def step(i, u):
                    g = live(i, 0)
                    if g is not None:
                        s = u
                        wait_alone(sp, S["passed"], S["own_scaled"], g - 3)
                        if n == 1:
                            wait_alone(sp, S["passed"], S["own_turned"], g - 3)
                        sp.dma_start(by_tile(own_rows[s], wide), group_rows(table, 0, at(g))).then_inc(S["own_in"][s], 16)
                        wait_alone(sp, S["passed"], S["own_done"] if n == 1 else S["agg"], g - 3)
                        sp.dma_start(mask[s][:, :], same[bass.ds(at(g) * GROUP, GROUP)].rearrange("(o n) -> o n", o=1)
                                     .to_broadcast([P, GROUP])).then_inc(S["mask_in"][s], 16)
                        if lane:
                            wait_alone(sp, S["passed"], S["n_turned"], g - 3)
                            sp.dma_start(tiles(n_rows[s][:, :]), group_rows(table, NODE0, g)).then_inc(S["n_in"][s], 16)
                    g = live(i, 1)
                    if g is not None and final:
                        s = (u - 1) % 4
                        wait_alone(sp, S["passed"], S["residual"], g - 3)
                        sp.dma_start(tiles(res_rows[s][:, :]), group_rows(residual_table, 0, at(g))).then_inc(S["res_in"][s], 16)
                    g = live(i, 6)
                    if g is not None:
                        s = (u - 6) % 4
                        if lane:
                            wait_alone(sp, S["passed"], S["rows"], g + 1)
                            sp.dma_start(group_rows(out_table, 0, at(g)), by_tile(rows[s], row_wide))\
                              .then_inc(S["stored"][s], 16)
                            wait_alone(sp, S["passed"], S["n_y1_rows"], g + 1)
                            sp.dma_start(group_rows(out_table, NODE0, g), by_tile(n_y1_rows[s], out_wide))\
                              .then_inc(S["n_y1_out"][s], 16)
                        elif not to_output:
                            wait_alone(sp, S["passed"], S["normed"], g + 1)
                            sp.dma_start(group_rows(out_table, 0, at(g)), tiles(rows[s][:, :])).then_inc(S["stored"][s], 16)
                    g = live(i, 9)
                    if g is not None and lane:
                        s = (u - 9) % 4
                        wait_alone(sp, S["passed"], S["normed"], g + 1)
                        base = 0 if node_table.shape[0] == ROWS else NODE0
                        sp.dma_start(group_rows(node_table, base, g), tiles(n_new[s][:, :])).then_inc(S["n_out"][s], 16)

                run_steps(sp, step, 4, 12, 9 if lane else 6)
                for s in range(4):
                    for out_ in ((S["stored"], S["n_y1_out"], S["n_out"]) if lane else () if to_output else (S["stored"],)):
                        sp.wait_ge(out_[s], 16 * groups_of_slot(s))

            @block.gpsimd
            def _(pool):
                def step(i, u):
                    g = live(i, 0)
                    if g is not None:
                        s = u
                        wait_alone(pool, S["passed"], S["src_scaled"], g - 3)
                        pool.tensor_copy(at_src[s][:, :], src_rows_at[:, bass.ds(at(g) * TILES, TILES)]).then_inc(S["staged"], 1)
                        wait_alone(pool, S["passed"], S["staged"], g + 1)
                        for j in range(TILES):
                            pool.indirect_dma_start(src_rows[s][:, j * wide:(j + 1) * wide], None, table[:, :],
                                                    bass.IndirectOffsetOnAxis(ap=at_src[s][:, j:j + 1], axis=0))\
                                .then_inc(S["gathered"][s], 16)
                    g = live(i, 7)
                    if g is not None and to_output:
                        s = (u - 7) % 4
                        wait_alone(pool, S["passed"], S["normed"], g + 1)
                        if not isinstance(g, int) or g >= 4:
                            wait_alone(pool, S["passed"], S["scattered"][s], landed(g - 4, s, 4, 16 * TILES))
                        pool.tensor_copy(at_out[s][:, :], e.out_row[:, bass.ds(at(g) * TILES, TILES)]).then_inc(S["out_staged"], 1)
                        wait_alone(pool, S["passed"], S["out_staged"], g + 1)
                        for j in range(TILES):
                            pool.indirect_dma_start(out_table[:, :], bass.IndirectOffsetOnAxis(ap=at_out[s][:, j:j + 1], axis=0),
                                                    rows[s][:, j * D:(j + 1) * D], None, bounds_check=ROWS - 1,
                                                    oob_is_err=False).then_inc(S["scattered"][s], 16)

                run_steps(pool, step, 4, 12, 7 if to_output else 0)
                if to_output:
                    for s in range(4):
                        pool.wait_ge(S["scattered"][s], 16 * TILES * groups_of_slot(s))

            @block.tensor
            def _(pe):
                def step(i, u):
                    g = live(i, 0)
                    if g is not None:
                        s = u % 2
                        wait_alone(pe, S["passed"], S["summed"], g + 1)
                        wait_alone(pe, S["passed"], S["agg"], g)
                        for j in range(TILES):
                            last = pe.transpose(b_agg[0:wide, j * P:(j + 1) * P],
                                                summed[s][:, j * wide:(j + 1) * wide], c.ident[:, :])
                        last.then_inc(S["turned"], 1)
                        if n == 1:
                            wait_alone(pe, S["passed"], S["own_done"], g)
                            for j in range(TILES):
                                last = pe.transpose(b_own[0:wide, j * P:(j + 1) * P],
                                                    own_rows[u][:, j * wide:(j + 1) * wide], c.ident[:, :])
                            last.then_inc(S["own_turned"], 1)
                        if lane:
                            wait_alone(pe, S["passed"], S["n_in"][u], landed(g, u, 4, 16))
                            wait_alone(pe, S["passed"], S["n_xT"], g)
                            transpose_tiles(pe, nb_x, n_rows[u], c).then_inc(S["n_turned"], 1)
                    g = live(i, 2)
                    if g is not None:
                        s = (u - 2) % 4
                        wait_alone(pe, S["passed"], S["y"], g + 1)
                        wait_alone(pe, S["passed"], S["residual"] if final else S["rows"], g)
                        for j in range(TILES):
                            last = pe.transpose(b_rows[:, j * row_wide:(j + 1) * row_wide],
                                                y[s][0:row_wide, j * P:(j + 1) * P], c.ident[0:row_wide, 0:row_wide])
                        last.then_inc(S["y_turned"], 1)
                        if lane:
                            wait_alone(pe, S["passed"], S["n_y1"], g + 1)
                            wait_alone(pe, S["passed"], S["n_y1_rows"], g)
                            for j in range(TILES):
                                last = pe.transpose(nb_y1[:, j * out_wide:(j + 1) * out_wide],
                                                    n_y[s][0:out_wide, j * P:(j + 1) * P], c.ident[0:out_wide, 0:out_wide])
                            last.then_inc(S["n_y1_turned"], 1)
                            wait_alone(pe, S["passed"], S["n_y2"], g)
                            at2 = out_wide if weighted else 0
                            pe.matmul(nb_hid2[at2:at2 + out_wide, :], c.gcn_w[n + 1][:, :], n_y[s][0:out_wide, :],
                                      start=True, stop=True).then_inc(S["n_hid2"], 1)
                    g = live(i, 1)
                    if g is not None:
                        s = (u - 1) % 2
                        wait_alone(pe, S["passed"], S["agg"], g + 1)
                        wait_alone(pe, S["passed"], S["y"], g)
                        pe.matmul(b_product[out_at:out_at + out_wide, :], c.gcn_w[n][:, :], agg[s][0:wide, :],
                                  start=True, stop=True).then_inc(S["product"], 1)
                        if lane:
                            wait_alone(pe, S["passed"], S["n_xT"], g + 1)
                            wait_alone(pe, S["passed"], S["n_y1"], g)
                            pe.matmul(nb_hid[0:out_wide, :], c.gcn_w[n][:, :], n_xT[(u - 1) % 4][:, :],
                                      start=True, stop=True).then_inc(S["n_hid"], 1)
                    g = live(i, 4)
                    if g is not None and lane:
                        s = u % 2
                        wait_alone(pe, S["passed"], S["n_sum"], g + 1)
                        wait_alone(pe, S["passed"], S["n_sum_rows"], g)
                        transpose_tiles(pe, nb_sum, n_sum[s], c).then_inc(S["n_sum_turned"], 1)

                run_steps(pe, step, 4, 12, 4)

            @block.scalar
            def _(act):
                def step(i, u):
                    g = live(i, norm_lag + 1)
                    if g is not None:
                        s = (u - norm_lag - 1) % 2
                        act.wait_ge(S["spread"], g + 1)
                        act.activation(root[s][:, :], spread[s][:, :], ACT.Sqrt).then_inc(S["root"], 1)
                    g = live(i, 0)
                    if g is not None and lane:
                        s = u
                        act.wait_ge(S["n_turned"], g + 1)
                        wait_from(act, S["n_hid"], g - 3)
                        wait_from(act, S["n_sum"], g - 3)
                        act.copy(n_xT[s][:, :], nb_x[:, :]).then_inc(S["n_xT"], 1)
                    g = live(i, 3)
                    if g is not None and lane:
                        s = (u - 3) % 4
                        act.wait_ge(S["n_y1_turned"], g + 1)
                        if not isinstance(g, int) or g >= 4:
                            act.wait_ge(S["n_y1_out"][s], landed(g - 4, s, 4, 16))
                        act.copy(n_y1_rows[s][:, 0:TILES * out_wide], nb_y1[:, 0:TILES * out_wide]).then_inc(S["n_y1_rows"], 1)
                    g = live(i, norm_lag + 2)
                    if g is not None:
                        s = (u - norm_lag - 2) % 4
                        act.wait_ge(S["shift"], g + 1)
                        into, from_ = (rows[s], res[s]) if final else (n_new[s], n_sum_rows[s])
                        sent, each = ((S["scattered"], 16 * TILES) if to_output else
                                      (S["stored"] if final else S["n_out"], 16))
                        if not isinstance(g, int) or g >= 4:
                            act.wait_ge(sent[s], landed(g - 4, s, 4, each))
                        layernorm_apply(act, into, from_, ln[s % 2]).then_inc(S["normed"], 1)
                    g = live(i, 2)
                    if g is not None and lane:
                        s = (u - 2) % 4
                        act.wait_ge(S["n_hid2"], g + 1)
                        wait_from(act, S["n_sum"], g - 3)
                        at2 = out_wide if weighted else 0
                        into = n_y[s] if weighted else n_y2[s]
                        act.activation(into[at2:at2 + out_wide, :], nb_hid2[at2:at2 + out_wide, :], ACT.Relu,
                                       bias=c.gcn_b[n + 1][at2:at2 + out_wide, :]).then_inc(S["n_y2"], 1)
                    g = live(i, 1)
                    if g is not None:
                        s = (u - 1) % 4
                        act.wait_ge(S["product"], g + 1)
                        wait_from(act, S["y_turned"], g - 3)
                        act.activation(y[s][out_at:out_at + out_wide, :], b_product[out_at:out_at + out_wide, :], ACT.Relu,
                                       bias=c.gcn_b[n][out_at:out_at + out_wide, :]).then_inc(S["y"], 1)
                        if lane:
                            act.wait_ge(S["n_hid"], g + 1)
                            wait_from(act, S["n_hid2"], g - 3)
                            wait_from(act, S["n_y1_turned"], g - 3)
                            wait_from(act, S["n_sum"], g - 3)
                            act.activation(n_y[s][0:out_wide, :], nb_hid[0:out_wide, :], ACT.Relu,
                                           bias=c.gcn_b[n][0:out_wide, :]).then_inc(S["n_y1"], 1)
                    g = live(i, 4)
                    if g is not None and lane:
                        s = u
                        act.wait_ge(S["n_sum_turned"], g + 1)
                        wait_from(act, S["normed"], g - 3)
                        act.copy(n_sum_rows[s][:, :], nb_sum[:, :]).then_inc(S["n_sum_rows"], 1)

                run_steps(act, step, 4, 12, norm_lag + 2)

            @block.vector
            def _(dve):
                def step(i, u):
                    g = live(i, 1)
                    if g is not None:
                        s = (u - 1) % 2
                        m = (u - 1) % 4
                        begin = isinstance(g, int) and g == 0
                        dve.wait_ge(S["mask_in"][m], landed(g, m, 4, 16))
                        wait_alone(dve, S["passed"], S["turned"], g + 1)
                        wait_from(dve, S["product"], g - 1)
                        wait_from(dve, S["agg"], g)
                        dve.tensor_tensor_scan(agg[s][0:wide, flow], mask[m][0:wide, flow], b_agg[0:wide, flow],
                                               0.0 if begin else agg[1 - s][0:wide, entry],
                                               ALU.mult, ALU.add).then_inc(S["agg"], 1)
                    g = live(i, 0)
                    if g is not None:
                        s = u % 2
                        cols = bass.ds(at(g) * TILES, TILES)
                        wait_from(dve, S["summed"], g - 1)
                        wait_alone(dve, S["passed"], S["own_in"][u], landed(g, u, 4, 16))
                        dve.tensor_tensor(by_tile(own_scaled[s], wide), by_tile(own_rows[u], wide),
                                          over_features(self_norm[:, cols], wide), ALU.mult).then_inc(S["own_scaled"], 1)
                        dve.wait_ge(S["gathered"][u], landed(g, u, 4, 16 * TILES))
                        dve.tensor_tensor(by_tile(src_scaled[s], wide), by_tile(src_rows[u], wide),
                                          over_features(norm[:, cols], wide), ALU.mult).then_inc(S["src_scaled"], 1)
                    g = live(i, 0)
                    if g is not None:
                        s = u % 2
                        dve.wait_ge(S["src_scaled"], g + 1)
                        dve.wait_ge(S["own_scaled"], g + 1)
                        wait_from(dve, S["turned"], g - 1)
                        dve.tensor_tensor(summed[s][:, :], src_scaled[s][:, :], own_scaled[s][:, :], ALU.add)\
                           .then_inc(S["summed"], 1)
                    g = live(i, 1)
                    if g is not None and n == 1:
                        s = (u - 1) % 4
                        begin = isinstance(g, int) and g == 0
                        dve.wait_ge(S["own_turned"], g + 1)
                        wait_from(dve, S["y_turned"], g - 3)
                        wait_from(dve, S["own_done"], g)
                        dve.tensor_tensor_scan(y[s][0:wide, flow], mask[s][0:wide, flow], b_own[0:wide, flow],
                                               0.0 if begin else y[(s - 1) % 4][0:wide, entry],
                                               ALU.mult, ALU.add).then_inc(S["own_done"], 1)
                    g = live(i, 3)
                    if g is not None and final:
                        s = (u - 3) % 4
                        dve.wait_ge(S["res_in"][s], landed(g, s, 4, 16))
                        dve.wait_ge(S["y_turned"], g + 1)
                        wait_from(dve, S["normed"], g - 3)
                        dve.tensor_tensor(res[s][:, :], b_rows[:, :], res_rows[s][:, :], ALU.add).then_inc(S["residual"], 1)
                        dve.wait_ge(S["residual"], g + 1)
                    if g is not None and lane:
                        s = (u - 3) % 4
                        dve.wait_ge(S["y_turned"], g + 1)
                        if not isinstance(g, int) or g >= 4:
                            wait_alone(dve, S["passed"], S["stored"][s], landed(g - 4, s, 4, 16))
                        dve.tensor_tensor(by_tile(rows[s], row_wide), by_tile(b_rows, row_wide),
                                          over_features(place_mask[:, bass.ds(at(g) * TILES, TILES)], row_wide),
                                          ALU.mult).then_inc(S["rows"], 1)
                        dve.wait_ge(S["n_y2"], g + 1)
                        wait_from(dve, S["n_sum_turned"], g - 1)
                        dve.tensor_tensor(n_sum[s % 2][:, :], (n_y[s] if weighted else n_y2[s])[:, :], n_xT[s][:, :],
                                          ALU.add).then_inc(S["n_sum"], 1)
                    g = live(i, norm_lag)
                    if g is not None:
                        s = (u - norm_lag) % 4
                        if lane:
                            dve.wait_ge(S["n_sum_rows"], g + 1)
                        wait_from(dve, S["root"], g - 1)
                        layernorm_stats(dve, S, S["stats"], S["moments"], g, (res if final else n_sum_rows)[s], ln[s % 2],
                                        spread[s % 2][:, :]).then_inc(S["spread"], 1)
                    g = live(i, norm_lag + 1)
                    if g is not None:
                        s = (u - norm_lag - 1) % 2
                        dve.wait_ge(S["root"], g + 1)
                        wait_from(dve, S["normed"], g - 1)
                        dve.reciprocal(plain[s][:, :], root[s][:, :]).then_inc(S["plain"], 1)
                        wait_alone(dve, S["passed"], S["plain"], g + 1)
                        mask_ = place_mask[:, bass.ds(at(g) * TILES, TILES)] if final else None
                        layernorm_factors(dve, S["scale"], S["shift"], g, plain[s][:, :], mask_, ln[s])

                run_steps(dve, step, 4, 12, norm_lag + 1)


def attention_pass(nc, c, e, r, bank, table, out_table):
    flow = slice(None, None, -1)
    same = r.same_next

    def at(g):
        return GROUPS - 1 - g

    with ExitStack() as ctx:
        S = named_semaphores(nc, ctx, "att", "staged turned src_done own_done q_ready k_ready q_done prod scores v_ready "
                             "v_done highest before shrink_log weight_log shrink weight weighted num "
                             "heads num_turned skipped own_back rden part logit z tanh gate rst diff mixed "
                             "own_copied stats1 moments1 scale1 shift1 normed scaled_gamma affine negative positive residual "
                             "stats2 moments2 scale2 shift2 x2_rows spread root filled",
                             "stored", "gathered own_in mask_in cut_in")

        def sb(name, shape, dt=F32, slots=2):
            return [ctx.enter_context(nc.sbuf_tensor(f"att_{name}{s}", shape, dt)) for s in range(slots)]

        src_rows, own_rows, x1_rows, ownT = (sb(m, [P, GROUP], slots=4) for m in ("src_rows", "own_rows", "x1_rows", "ownT"))
        mask, cut = sb("mask", [P, GROUP], BF16, 4), sb("cut", [P, GROUP], BF16, 4)
        at_src = sb("at_src", [P, TILES], I32, 4)
        (srcT, q, v, prod, before, shrink_log, weight_log, shrink, weight, weighted, den, num,
         rst, diff, mixed, normed, gam, aff, neg, pos, res, x2_rows) = (
            sb(m, [P, GROUP]) for m in
            "srcT q v prod before shrink_log weight_log shrink weight weighted den num "
            "rst diff mixed normed gam aff neg pos res x2_rows".split())
        highest = sb("highest", [P, GROUP + 1])
        rden, part = sb("rden", [P, TILES, HEADS]), sb("part", [P, TILES, HEADS])
        logit, z, th, gate = (sb(m, [P, TILES]) for m in ("logit", "z", "th", "gate"))
        spread, root = sb("spread", [P, 2, TILES]), sb("root", [P, 2, TILES])
        power = ctx.enter_context(nc.sbuf_tensor("att_power", [P, 2, TILES], F32))

        def one(name, shape):
            return ctx.enter_context(nc.sbuf_tensor(f"att_{name}", shape, F32))

        ln1, ln2 = layernorm_buffers(one, "ln1"), layernorm_buffers(one, "ln2")
        b_own, b_src, b_qv, b_k, b_scores, b_heads, b_skip, b_num = bank
        b_x1 = b_k
        heads = b_heads[:, 0:TILES * 9].rearrange("p (j c) -> p j c", j=TILES)

        with nc.Block() as block:
            @block.sync
            def _(sp):
                def step(i, u):
                    g = live(i, 0)
                    if g is not None:
                        s = u
                        wait_alone(sp, S["passed"], S["turned"], g - 3)
                        sp.dma_start(tiles(own_rows[s][:, :]), group_rows(table, 0, at(g))).then_inc(S["own_in"][s], 16)
                        wait_alone(sp, S["passed"], S["own_done"], g - 3)
                        sp.dma_start(mask[s][:, :], same[bass.ds(at(g) * GROUP, GROUP)].rearrange("(o n) -> o n", o=1)
                                     .to_broadcast([P, GROUP])).then_inc(S["mask_in"][s], 16)
                        wait_alone(sp, S["passed"], S["before"], g - 3)
                        sp.dma_start(cut[s][:, :], r.cut_next[bass.ds(at(g) * GROUP, GROUP)].rearrange("(o n) -> o n", o=1)
                                     .to_broadcast([P, GROUP])).then_inc(S["cut_in"][s], 16)
                    g = live(i, 10)
                    if g is not None:
                        s = u % 2
                        wait_alone(sp, S["passed"], S["x2_rows"], g + 1)
                        sp.dma_start(group_rows(out_table, 0, at(g)), tiles(x2_rows[s][:, :])).then_inc(S["stored"][s], 16)

                run_steps(sp, step, 4, 12, 10)
                for s in range(2):
                    sp.wait_ge(S["stored"][s], 16 * (GROUPS // 2))

            @block.gpsimd
            def _(pool):
                pool.memset(power[:, :, :], -0.5)
                for s in range(2):
                    pool.memset(spread[s][:, :, :], 1.0)
                pool.memset(highest[0][:, GROUP:GROUP + 1], FAR).then_inc(S["filled"], 1)
                pool.wait_ge(S["filled"], 1)

                def gather(g, s):
                    wait_alone(pool, S["passed"], S["turned"], g - 3)
                    pool.tensor_copy(at_src[s][:, :], e.src_at_end[:, bass.ds(at(g) * TILES, TILES)]).then_inc(S["staged"], 1)
                    wait_alone(pool, S["passed"], S["staged"], g + 1)
                    for j in range(TILES):
                        pool.indirect_dma_start(src_rows[s][:, j * D:(j + 1) * D], None, table[:, :],
                                                bass.IndirectOffsetOnAxis(ap=at_src[s][:, j:j + 1], axis=0))\
                            .then_inc(S["gathered"][s], 16)

                def step(i, u):
                    if not isinstance(i, int) or i >= 3:
                        wait_alone(pool, S["passed"], S["spread"], i - 2)
                        pool.tensor_tensor(root[(u - 3) % 2][:, :, :], spread[(u - 3) % 2][:, :, :], power[:, :, :], ALU.pow)\
                            .then_inc(S["root"], 1)
                    g = live(i, 0)
                    if g is not None:
                        gather(g, u)
                    g = live(i, 7)
                    if g is not None:
                        s = (u - 7) % 2
                        affine(pool, S, c, g, normed[s], gam[s], aff[s])

                run_steps(pool, step, 4, 12, 10)

            @block.tensor
            def _(pe):
                def step(i, u):
                    g = live(i, 0)
                    if g is not None:
                        s = u
                        pe.wait_ge(S["gathered"][s], landed(g, s, 4, 16 * TILES))
                        pe.wait_ge(S["own_in"][s], landed(g, s, 4, 16))
                        wait_from(pe, S["src_done"], g)
                        wait_from(pe, S["own_done"], g)
                        transpose_tiles(pe, b_own, own_rows[s], c)
                        transpose_tiles(pe, b_src, src_rows[s], c).then_inc(S["turned"], 1)
                    g = live(i, 3)
                    if g is not None:
                        s = (u - 3) % 2
                        own = ownT[(u - 3) % 4]
                        pe.wait_ge(S["num"], g + 1)
                        wait_from(pe, S["z"], g)
                        for j in range(TILES):
                            cols = slice(j * P, (j + 1) * P)
                            pe.matmul(heads[:, j, 0:4], den[s][:, cols], c.head_pick[:, :], start=True, stop=True)
                            pe.matmul(heads[:, j, 4:8], num[s][:, cols], c.gate_heads[:, :], start=True, stop=True)
                            last = pe.matmul(heads[:, j, 8:9], own[:, cols], c.gate_own[:, :], start=True, stop=True)
                        last.then_inc(S["heads"], 1)
                        wait_from(pe, S["rst"], g)
                        transpose_tiles(pe, b_num, num[s], c).then_inc(S["num_turned"], 1)
                        wait_from(pe, S["diff"], g)
                        for j in range(TILES):
                            cols = slice(j * P, (j + 1) * P)
                            pe.matmul(b_skip[:, cols], own[:, cols], c.wskip[:, :], start=True, stop=False)
                            last = pe.matmul(b_skip[:, cols], c.ones[0:1, :], c.bskip_row[0:1, :], start=False, stop=True)
                        last.then_inc(S["skipped"], 1)
                    g = live(i, 1)
                    if g is not None:
                        s = (u - 1) % 2
                        pe.wait_ge(S["q_done"], g + 1)
                        pe.matmul(b_qv[:, :], c.wv[:, :], srcT[s][:, :], start=True, stop=True).then_inc(S["v_ready"], 1)
                        pe.wait_ge(S["prod"], g + 1)
                        wait_from(pe, S["weight_log"], g)
                        pe.matmul(b_scores[:, :], c.head_sum[:, :], prod[s][:, :], start=True, stop=True).then_inc(S["scores"], 1)
                    g = live(i, 3)
                    if g is not None:
                        wait_from(pe, S["own_copied"], g)
                        transpose_tiles(pe, b_x1, ownT[(u - 3) % 4], c).then_inc(S["own_back"], 1)
                    g = live(i, 0)
                    if g is not None:
                        s = u % 2
                        pe.wait_ge(S["src_done"], g + 1)
                        wait_from(pe, S["v_done"], g)
                        pe.matmul(b_qv[:, :], c.wq[:, :], srcT[s][:, :], start=True, stop=True).then_inc(S["q_ready"], 1)
                        pe.wait_ge(S["own_done"], g + 1)
                        wait_from(pe, S["prod"], g)
                        wait_from(pe, S["own_copied"], g - 2)
                        pe.matmul(b_k[:, :], c.wk[:, :], ownT[u][:, :], start=True, stop=True).then_inc(S["k_ready"], 1)

                run_steps(pe, step, 4, 12, 3)

            @block.scalar
            def _(act):
                def step(i, u):
                    g = live(i, 7)
                    if g is not None:
                        s = (u - 7) % 2
                        negative_part(act, S, g, aff[s], neg[s])
                    g = live(i, 1)
                    if g is not None:
                        s = (u - 1) % 2
                        act.wait_ge(S["q_ready"], g + 1)
                        wait_from(act, S["prod"], g - 1)
                        act.activation(q[s][:, :], b_qv[:, :], ACT.Identity, bias=c.bq[:, :]).then_inc(S["q_done"], 1)
                    g = live(i, 2)
                    if g is not None:
                        s = u % 2
                        act.wait_ge(S["weight_log"], g + 1)
                        wait_from(act, S["num"], g - 1)
                        act.activation(weight[s][:, :], weight_log[s][:, :], ACT.Exp).then_inc(S["weight"], 1)
                        act.wait_ge(S["shrink_log"], g + 1)
                        act.activation(shrink[s][:, :], shrink_log[s][:, :], ACT.Exp).then_inc(S["shrink"], 1)
                    g = live(i, 4)
                    if g is not None:
                        s = u % 2
                        act.wait_ge(S["z"], g + 1)
                        wait_from(act, S["gate"], g - 1)
                        act.activation(th[s][:, :], z[s][:, :], ACT.Tanh, bias=c.gate_bias[:, :], scale=0.5)\
                           .then_inc(S["tanh"], 1)
                    g = live(i, 1)
                    if g is not None:
                        s = (u - 1) % 2
                        act.wait_ge(S["v_ready"], g + 1)
                        wait_from(act, S["weighted"], g - 1)
                        act.activation(v[s][:, :], b_qv[:, :], ACT.Identity, bias=c.bv[:, :]).then_inc(S["v_done"], 1)
                    g = live(i, 0)
                    if g is not None:
                        s = u % 2
                        act.wait_ge(S["turned"], g + 1)
                        wait_from(act, S["v_ready"], g - 1)
                        act.copy(srcT[s][:, :], b_src[:, :]).then_inc(S["src_done"], 1)
                    g = live(i, 3)
                    if g is not None:
                        s = (u - 3) % 4
                        act.wait_ge(S["own_back"], g + 1)
                        wait_from(act, S["residual"], g - 3)
                        act.copy(x1_rows[s][:, :], b_x1[:, :]).then_inc(S["own_copied"], 1)
                    g = live(i, 5)
                    if g is not None:
                        s = (u - 5) % 2
                        act.wait_ge(S["shift1"], g + 1)
                        wait_from(act, S["scaled_gamma"], g - 1)
                        layernorm_apply(act, normed[s], mixed[s], ln1[s]).then_inc(S["normed"], 1)
                    g = live(i, 8)
                    if g is not None:
                        s = u % 2
                        act.wait_ge(S["shift2"], g + 1)
                        if not isinstance(g, int) or g >= 2:
                            act.wait_ge(S["stored"][s], landed(g - 2, s, 2, 16))
                        layernorm_apply(act, x2_rows[s], res[s], ln2[s]).then_inc(S["x2_rows"], 1)

                run_steps(act, step, 4, 12, 8)

            @block.vector
            def _(dve):
                def step(i, u):
                    here = spread[u % 2]
                    last = None
                    g = live(i, 1)
                    if g is not None:
                        s = (u - 1) % 2
                        dve.wait_ge(S["k_ready"], g + 1)
                        dve.wait_ge(S["q_done"], g + 1)
                        wait_from(dve, S["scores"], g - 1)
                        dve.scalar_tensor_tensor(prod[s][:, :], b_k[:, :], c.bk[:, :], q[s][:, :], ALU.add, ALU.mult)\
                           .then_inc(S["prod"], 1)
                    g = live(i, 7)
                    if g is not None:
                        s = (u - 7) % 2
                        last = prelu_residual(dve, S, c, g, aff[s], neg[s], pos[s], x1_rows[(u - 7) % 4][:, :], res[s],
                                              S["x2_rows"], ln2[s], here[:, 1, :])
                    g = live(i, 2)
                    if g is not None:
                        s = u % 2
                        begin = isinstance(g, int) and g == 0
                        dve.wait_ge(S["weight"], g + 1)
                        dve.wait_ge(S["v_done"], g + 1)
                        wait_from(dve, S["num"], g)
                        dve.tensor_tensor(weighted[s][:, :], v[s][:, :], weight[s][:, :], ALU.mult).then_inc(S["weighted"], 1)
                        dve.wait_ge(S["shrink"], g + 1)
                        wait_from(dve, S["num_turned"], g - 1)
                        dve.tensor_tensor_scan(den[s][:, flow], shrink[s][:, flow], weight[s][:, flow],
                                               0.0 if begin else den[1 - s][:, 0:1], ALU.mult, ALU.add)
                        dve.wait_ge(S["weighted"], g + 1)
                        dve.tensor_tensor_scan(num[s][:, flow], shrink[s][:, flow], weighted[s][:, flow],
                                               0.0 if begin else num[1 - s][:, 0:1], ALU.mult, ALU.add)\
                           .then_inc(S["num"], 1)
                    g = live(i, 0)
                    if g is not None:
                        s = u
                        begin = isinstance(g, int) and g == 0
                        dve.wait_ge(S["mask_in"][s], landed(g, s, 4, 16))
                        dve.wait_ge(S["turned"], g + 1)
                        wait_from(dve, S["own_back"], g - 3)
                        wait_from(dve, S["own_done"], g)
                        dve.tensor_tensor_scan(ownT[s][:, flow], mask[s][:, flow], b_own[:, flow],
                                               0.0 if begin else ownT[(s - 1) % 4][:, 0:1], ALU.mult, ALU.add)\
                           .then_inc(S["own_done"], 1)
                    if not isinstance(i, int) or i >= 1:
                        wait_alone(dve, S["passed"], S["root"], i)
                    for lag, scale_done, shift_done, read, n, ln in ((8, S["scale2"], S["shift2"], S["x2_rows"], 1, ln2),
                                                                     (5, S["scale1"], S["shift1"], S["normed"], 0, ln1)):
                        g = live(i, lag)
                        if g is not None:
                            s = (u - lag) % 2
                            wait_alone(dve, S["passed"], read, g - 1)
                            mask_ = e.is_start[:, bass.ds(at(g) * TILES, TILES)] if n else None
                            layernorm_factors(dve, scale_done, shift_done, g, root[(u - 1) % 2][:, n, :], mask_, ln[s])
                    g = live(i, 3)
                    if g is not None:
                        s = (u - 3) % 2
                        dve.wait_ge(S["heads"], g + 1)
                        dve.reciprocal(rden[s][:, :, :], heads[:, :, 0:4]).then_inc(S["rden"], 1)
                        dve.wait_ge(S["rden"], g + 1)
                        dve.tensor_tensor(part[s][:, :, :], heads[:, :, 4:8], rden[s][:, :, :], ALU.mult).then_inc(S["part"], 1)
                        dve.wait_ge(S["num_turned"], g + 1)
                        dve.tensor_tensor(rst[s][:, :].rearrange("p (h f) -> p h f", f=HEAD),
                                          b_num[:, :].rearrange("p (h f) -> p h f", f=HEAD),
                                          rden[s][:, :, :].rearrange("p j h -> p (j h)").unsqueeze(2)
                                          .to_broadcast([P, TILES * HEADS, HEAD]), ALU.mult).then_inc(S["rst"], 1)
                        dve.wait_ge(S["part"], g + 1)
                        dve.tensor_reduce(logit[s][:, :], part[s][:, :, :], axis=AX.X, op=ALU.add).then_inc(S["logit"], 1)
                    g = live(i, 1)
                    if g is not None:
                        s = (u - 1) % 2
                        m = (u - 1) % 4
                        begin = isinstance(g, int) and g == 0
                        dve.wait_ge(S["cut_in"][m], landed(g, m, 4, 16))
                        dve.wait_ge(S["scores"], g + 1)
                        if begin:
                            dve.wait_ge(S["filled"], 1)
                        else:
                            dve.wait_ge(S["highest"], g)
                            dve.tensor_copy(highest[s][:, GROUP:GROUP + 1], highest[1 - s][:, 0:1])
                        dve.tensor_tensor_scan(highest[s][:, 0:GROUP][:, flow], cut[m][:, flow], b_scores[:, flow],
                                               FAR if begin else highest[1 - s][:, 0:1], ALU.add, ALU.max)\
                           .then_inc(S["highest"], 1)
                    g = live(i, 3)
                    if g is not None:
                        s = (u - 3) % 2
                        dve.wait_ge(S["logit"], g + 1)
                        wait_from(dve, S["tanh"], g - 1)
                        dve.tensor_tensor(z[s][:, :], logit[s][:, :], heads[:, :, 8], ALU.add).then_inc(S["z"], 1)
                    g = live(i, 1)
                    if g is not None:
                        s = (u - 1) % 2
                        m = (u - 1) % 4
                        dve.wait_ge(S["highest"], g + 1)
                        wait_from(dve, S["shrink"], g - 1)
                        dve.tensor_tensor(before[s][:, :], highest[s][:, 1:GROUP + 1], cut[m][:, :], ALU.add)\
                           .then_inc(S["before"], 1)
                        wait_from(dve, S["weight"], g - 1)
                        dve.tensor_tensor(weight_log[s][:, :], b_scores[:, :], highest[s][:, 0:GROUP], ALU.subtract)\
                           .then_inc(S["weight_log"], 1)
                        dve.wait_ge(S["before"], g + 1)
                        dve.tensor_tensor(shrink_log[s][:, :], before[s][:, :], highest[s][:, 0:GROUP], ALU.subtract)\
                           .then_inc(S["shrink_log"], 1)
                    g = live(i, 3)
                    if g is not None:
                        s = (u - 3) % 2
                        dve.wait_ge(S["skipped"], g + 1)
                        dve.wait_ge(S["rst"], g + 1)
                        dve.tensor_tensor(diff[s][:, :], b_skip[:, :], rst[s][:, :], ALU.subtract).then_inc(S["diff"], 1)
                    g = live(i, 4)
                    if g is not None:
                        s = u % 2
                        dve.wait_ge(S["tanh"], g + 1)
                        dve.tensor_scalar(gate[s][:, :], th[s][:, :], 0.5, 0.5, ALU.mult, ALU.add).then_inc(S["gate"], 1)
                        dve.wait_ge(S["gate"], g + 1)
                        dve.wait_ge(S["diff"], g + 1)
                        wait_from(dve, S["normed"], g - 1)
                        for j in range(TILES):
                            cols = slice(j * P, (j + 1) * P)
                            mix = dve.scalar_tensor_tensor(mixed[s][:, cols], diff[s][:, cols], gate[s][:, j:j + 1],
                                                           rst[s][:, cols], ALU.mult, ALU.add)
                        mix.then_inc(S["mixed"], 1)
                        dve.wait_ge(S["mixed"], g + 1)
                        last = layernorm_stats(dve, S, S["stats1"], S["moments1"], g, mixed[s], ln1[s], here[:, 0, :])
                    if last is None:
                        last = dve.memset(here[:, 0, :], 1.0)
                    last.then_inc(S["spread"], 1)

                run_steps(dve, step, 4, 12, 8)


def kernel(**inputs):
    import numpy as np
    import concourse.bacc as bacc
    from concourse.bass_utils import run_bass_kernel_spmd

    nc = bacc.Bacc("TRN2", target_bir_lowering=False, num_devices=1)
    arrays, aps = {}, {}

    def give(name, value):
        value = np.ascontiguousarray(value)
        arrays[name] = value
        aps[name] = nc.dram_tensor(name, value.shape, mybir.dt.from_np(value.dtype), kind="ExternalInput").ap()

    def padded(array, before, after, fill):
        array = np.asarray(array)
        return np.concatenate([np.full(before, fill[0], array.dtype), array, np.full(ROWS - N, fill[1], array.dtype),
                               np.full(after, fill[2], array.dtype)])

    def in_tiles(line):
        return line.reshape(COLS, P).T

    x = np.asarray(inputs["x"])
    give("x", np.concatenate([x, np.zeros((ROWS - N, D), x.dtype)]))
    dst = padded(inputs["dst"], 1, 1, (-1, N, -1))
    weight = padded(inputs["edge_weight"], 0, 0, (0, 0, 0))
    give("dst_line", dst)
    give("weight_line", weight)
    give("src_tiles", in_tiles(padded(inputs["src"], 0, 0, (0, 0, 0))))
    give("prev_tiles", in_tiles(dst[0:ROWS]))
    give("dst_tiles", in_tiles(dst[1:1 + ROWS]))
    give("next_tiles", in_tiles(dst[2:2 + ROWS]))
    give("weight_tiles", in_tiles(weight))
    for name, value in inputs.items():
        if name.startswith("L"):
            value = np.asarray(value)
            give(name, value.reshape(1) if value.ndim == 0 else value)
    out = nc.dram_tensor("out", (ROWS, D), F32, kind="ExternalOutput").ap()
    build(nc, aps, out)
    got = run_bass_kernel_spmd(nc, [arrays], core_ids=[0])
    return got.results[0]["out"][:N]
```
